# Optimizing a Trainium2 kernel written in Bass

```python
import numpy as np
import jax
import jax.numpy as jnp

def _softmax(x, axis=-1):
    return jax.nn.softmax(x, axis=axis)

def _gelu(x):
    return jax.nn.gelu(x, approximate=True)

def _silu(x):
    return jax.nn.silu(x)

def _sigmoid(x):
    return jax.nn.sigmoid(x)

def _layernorm(x, axis=-1, eps=1e-05):
    m = jnp.mean(x, axis=axis, keepdims=True)
    v = jnp.var(x, axis=axis, keepdims=True)
    return (x - m) / jnp.sqrt(v + eps)

def _scatter_add(tgt, idx, src, axis=0):
    return tgt.at[idx].add(src)

def _segment_sum(src, seg, n):
    return jax.ops.segment_sum(src, seg, n)
kernel_name = 'mk_perceiver_d1_seqx_r4_420608'

def setup_inputs(seed: int=0):
    np.random.seed(seed)
    _w = jnp.asarray

    def _rec_inputs():
        import jax
        import jax.numpy as jnp
        _rk = jax.random.key(seed)
        x = -0.0002928 + 1 * jax.random.normal(jax.random.fold_in(_rk, 1), (1, 256, 256), jnp.float32)
        _lenS = 256 - jax.random.randint(jax.random.fold_in(_rk, 7), (1,), 0, max(1, 256 // 4) + 1, jnp.int32)
        _lenS2 = 4096 - jax.random.randint(jax.random.fold_in(_rk, 8), (1,), 0, max(1, 4096 // 4) + 1, jnp.int32)
        _ctx_768P = jax.random.normal(jax.random.fold_in(_rk, 11), (1, 16, 192), jnp.float32)
        _ctx_768c = jax.random.dirichlet(jax.random.fold_in(_rk, 511), 0.3 * jnp.ones((16,), jnp.float32), (1, 4096))
        _ctx_768t = jnp.einsum('bsk,bkd->bsd', _ctx_768c, _ctx_768P)
        _ctx_768t = _ctx_768t * jax.lax.rsqrt(jnp.mean(jnp.square(_ctx_768t)) + 1e-12) * 0.953939
        ctx_768 = -0.00423632 + 0.9977 * (_ctx_768t + 0.3 * jax.random.normal(jax.random.fold_in(_rk, 611), (1, 4096, 192), jnp.float32))
        return (x, ctx_768)
    x, ctx_768 = _rec_inputs()

    def _L0_xattn_setup():
        import jax, jax.numpy as jnp
        import numpy as np
        B, N, QD = (2, 512, 256)
        CTX_LEN, TCD = (77, 192)
        NUM_PROMPT, PD = (64, 256)
        HEADS, DIM_HEAD = (8, 64)
        INNER = HEADS * DIM_HEAD
        SCALE = DIM_HEAD ** (-0.5)
        key = jax.random.key(seed)
        ks = jax.random.split(key, 10)
        s = lambda *sh: 1.0 / np.sqrt(sh[0])
        return {'x': jax.random.normal(ks[0], (B, N, QD), jnp.float32), 'context': jax.random.normal(ks[1], (B, CTX_LEN, TCD), jnp.float32), 'prompt': jax.random.normal(ks[2], (1, NUM_PROMPT, PD), jnp.float32), 'w_prompt': jax.random.normal(ks[3], (PD, TCD), jnp.float32) * s(PD), 'w_img': jax.random.normal(ks[4], (QD, TCD), jnp.float32) * s(QD), 'w_q': jax.random.normal(ks[5], (QD, INNER), jnp.float32) * s(QD), 'w_k': jax.random.normal(ks[6], (TCD, INNER), jnp.float32) * s(TCD), 'w_v': jax.random.normal(ks[7], (TCD, INNER), jnp.float32) * s(TCD), 'w_out': jax.random.normal(ks[8], (INNER, QD), jnp.float32) * s(INNER), 'b_out': jax.random.normal(ks[9], (QD,), jnp.float32) * 0.01}
    _L0_xattn_all = _L0_xattn_setup()
    _L0_xattn_in = {k: v for k, v in _L0_xattn_all.items() if k in ('prompt', 'w_prompt', 'w_img', 'w_q', 'w_k', 'w_v', 'w_out', 'b_out')}
    del _L0_xattn_all

    def _L0_attn_setup():
        import jax, jax.numpy as jnp
        import numpy as np
        import math
        B, T, C = (2, 512, 256)
        H, L = (16, 64)
        DH = C // H
        DHE = DH // 2
        THETA = 10000.0

        def _rope_cache(t, dim):
            inv_freq = 1.0 / THETA ** (jnp.arange(0, dim, 2, dtype=jnp.float32) / dim)
            freqs = jnp.arange(t, dtype=jnp.float32)[:, None] * inv_freq[None, :]
            emb = jnp.concatenate((freqs, freqs), axis=-1)
            return (jnp.cos(emb), jnp.sin(emb))

        def _apply_rope(x, cos, sin):
            x1 = x[..., 0::2]
            x2 = x[..., 1::2]
            rot = jnp.stack((-x2, x1), axis=-1).reshape(x.shape)
            return x * cos[None, None] + rot * sin[None, None]
        key = jax.random.key(seed)
        ks = jax.random.split(key, 10)
        s = 0.02
        return {'x': jax.random.normal(ks[0], (B, T, C), jnp.float32), 'Wq_down': jax.random.normal(ks[1], (C, H * L), jnp.float32) * s, 'Wk_down': jax.random.normal(ks[2], (C, H * L), jnp.float32) * s, 'Wv_down': jax.random.normal(ks[3], (C, H * L), jnp.float32) * s, 'Wq_up_c': jax.random.normal(ks[4], (L, DHE), jnp.float32) * s, 'Wq_up_e': jax.random.normal(ks[5], (L, DHE), jnp.float32) * s, 'Wk_up_c': jax.random.normal(ks[6], (L, DHE), jnp.float32) * s, 'Wk_up_e': jax.random.normal(ks[7], (L, DHE), jnp.float32) * s, 'Wv_up': jax.random.normal(ks[8], (L, DH), jnp.float32) * s, 'Wc': jax.random.normal(ks[9], (C, C), jnp.float32) * s}
    _L0_attn_all = _L0_attn_setup()
    _L0_attn_in = {k: v for k, v in _L0_attn_all.items() if k in ('Wq_down', 'Wk_down', 'Wv_down', 'Wq_up_c', 'Wq_up_e', 'Wk_up_c', 'Wk_up_e', 'Wv_up', 'Wc')}
    del _L0_attn_all

    def _L0_ffn_setup():
        import jax, jax.numpy as jnp
        import numpy as np
        TOP_K = 2

        def _swiglu_mlp(x, wgu, wd, inter):
            gu = x @ wgu
            a = jax.nn.silu(gu[:, :inter]) * gu[:, inter:]
            return a @ wd
        key = jax.random.key(seed)
        ks = jax.random.split(key, 6)
        H, I, E = (256, 704, 8)
        B, S = (2, 256)
        w = 0.02
        return {'x': jax.random.normal(ks[0], (B, S, H), jnp.float32), 'gate_w': jax.random.normal(ks[1], (H, E), jnp.float32) * w, 'base_wgu': jax.random.normal(ks[2], (H, 2 * I), jnp.float32) * w, 'base_wd': jax.random.normal(ks[3], (I, H), jnp.float32) * w, 'exp_wgu': jax.random.normal(ks[4], (E, H, 2 * I), jnp.float32) * w, 'exp_wd': jax.random.normal(ks[5], (E, I, H), jnp.float32) * w}
    _L0_ffn_all = _L0_ffn_setup()
    _L0_ffn_in = {k: v for k, v in _L0_ffn_all.items() if k in ('gate_w', 'base_wgu', 'base_wd', 'exp_wgu', 'exp_wd')}
    del _L0_ffn_all
    return {'x': x, 'ctx_768': ctx_768, 'L0_xattn_prompt': _L0_xattn_in['prompt'], 'L0_xattn_w_prompt': _L0_xattn_in['w_prompt'], 'L0_xattn_w_img': _L0_xattn_in['w_img'], 'L0_xattn_w_q': _L0_xattn_in['w_q'], 'L0_xattn_w_k': _L0_xattn_in['w_k'], 'L0_xattn_w_v': _L0_xattn_in['w_v'], 'L0_xattn_w_out': _L0_xattn_in['w_out'], 'L0_xattn_b_out': _L0_xattn_in['b_out'], 'L0_attn_Wq_down': _L0_attn_in['Wq_down'], 'L0_attn_Wk_down': _L0_attn_in['Wk_down'], 'L0_attn_Wv_down': _L0_attn_in['Wv_down'], 'L0_attn_Wq_up_c': _L0_attn_in['Wq_up_c'], 'L0_attn_Wq_up_e': _L0_attn_in['Wq_up_e'], 'L0_attn_Wk_up_c': _L0_attn_in['Wk_up_c'], 'L0_attn_Wk_up_e': _L0_attn_in['Wk_up_e'], 'L0_attn_Wv_up': _L0_attn_in['Wv_up'], 'L0_attn_Wc': _L0_attn_in['Wc'], 'L0_ffn_gate_w': _L0_ffn_in['gate_w'], 'L0_ffn_base_wgu': _L0_ffn_in['base_wgu'], 'L0_ffn_base_wd': _L0_ffn_in['base_wd'], 'L0_ffn_exp_wgu': _L0_ffn_in['exp_wgu'], 'L0_ffn_exp_wd': _L0_ffn_in['exp_wd']}

def reference(x, ctx_768, L0_xattn_prompt, L0_xattn_w_prompt, L0_xattn_w_img, L0_xattn_w_q, L0_xattn_w_k, L0_xattn_w_v, L0_xattn_w_out, L0_xattn_b_out, L0_attn_Wq_down, L0_attn_Wk_down, L0_attn_Wv_down, L0_attn_Wq_up_c, L0_attn_Wq_up_e, L0_attn_Wk_up_c, L0_attn_Wk_up_e, L0_attn_Wv_up, L0_attn_Wc, L0_ffn_gate_w, L0_ffn_base_wgu, L0_ffn_base_wd, L0_ffn_exp_wgu, L0_ffn_exp_wd):
    import jax
    import jax.numpy as jnp

    def _L0_xattn_ref(x, context, prompt, w_prompt, w_img, w_q, w_k, w_v, w_out, b_out):
        import jax, jax.numpy as jnp
        import numpy as np
        B, N, QD = (2, 512, 256)
        CTX_LEN, TCD = (77, 192)
        NUM_PROMPT, PD = (64, 256)
        HEADS, DIM_HEAD = (8, 64)
        INNER = HEADS * DIM_HEAD
        SCALE = DIM_HEAD ** (-0.5)
        b, n, _ = x.shape
        q = x @ w_q
        prompt_ctx = jnp.broadcast_to(prompt @ w_prompt, (b, NUM_PROMPT, TCD))
        img_ctx = x @ w_img
        ctx = jnp.concatenate([context, prompt_ctx, img_ctx], axis=1)
        k = ctx @ w_k
        v = ctx @ w_v
        split = lambda t: t.reshape(b, t.shape[1], HEADS, DIM_HEAD).transpose(0, 2, 1, 3)
        qh, kh, vh = (split(q), split(k), split(v))
        sim = jnp.einsum('bhid,bhjd->bhij', qh, kh) * SCALE
        attn = jax.nn.softmax(sim, axis=-1)
        out = jnp.einsum('bhij,bhjd->bhid', attn, vh)
        out = out.transpose(0, 2, 1, 3).reshape(b, n, INNER)
        return out @ w_out + b_out

    def _L0_attn_ref(x, Wq_down, Wk_down, Wv_down, Wq_up_c, Wq_up_e, Wk_up_c, Wk_up_e, Wv_up, Wc):
        import jax, jax.numpy as jnp
        import numpy as np
        import math
        B, T, C = (2, 512, 256)
        H, L = (16, 64)
        DH = C // H
        DHE = DH // 2
        THETA = 10000.0

        def _rope_cache(t, dim):
            inv_freq = 1.0 / THETA ** (jnp.arange(0, dim, 2, dtype=jnp.float32) / dim)
            freqs = jnp.arange(t, dtype=jnp.float32)[:, None] * inv_freq[None, :]
            emb = jnp.concatenate((freqs, freqs), axis=-1)
            return (jnp.cos(emb), jnp.sin(emb))

        def _apply_rope(x, cos, sin):
            x1 = x[..., 0::2]
            x2 = x[..., 1::2]
            rot = jnp.stack((-x2, x1), axis=-1).reshape(x.shape)
            return x * cos[None, None] + rot * sin[None, None]
        b, t, c = x.shape
        q_lat = (x @ Wq_down).reshape(b, t, H, L)
        k_lat = (x @ Wk_down).reshape(b, t, H, L)
        v_lat = (x @ Wv_down).reshape(b, t, H, L)
        q_c = jnp.einsum('bthl,ld->bhtd', q_lat, Wq_up_c)
        q_e = jnp.einsum('bthl,ld->bhtd', q_lat, Wq_up_e)
        k_c = jnp.einsum('bthl,ld->bhtd', k_lat, Wk_up_c)
        k_e = jnp.einsum('bthl,ld->bhtd', k_lat, Wk_up_e)
        v = jnp.einsum('bthl,ld->bhtd', v_lat, Wv_up)
        cos, sin = _rope_cache(t, DHE)
        q = jnp.concatenate([q_c, _apply_rope(q_e, cos, sin)], axis=-1)
        k = jnp.concatenate([k_c, _apply_rope(k_e, cos, sin)], axis=-1)
        scale = 1.0 / math.sqrt(DH)
        scores = jnp.einsum('bhqd,bhkd->bhqk', q, k) * scale
        causal = jnp.tril(jnp.ones((t, t), dtype=bool))
        scores = jnp.where(causal[None, None], scores, -jnp.inf)
        att = jax.nn.softmax(scores, axis=-1)
        y = jnp.einsum('bhqk,bhkd->bhqd', att, v)
        y = y.transpose(0, 2, 1, 3).reshape(b, t, c)
        return y @ Wc

    def _L0_ffn_ref(x, gate_w, base_wgu, base_wd, exp_wgu, exp_wd):
        import jax, jax.numpy as jnp
        import numpy as np
        TOP_K = 2

        def _swiglu_mlp(x, wgu, wd, inter):
            gu = x @ wgu
            a = jax.nn.silu(gu[:, :inter]) * gu[:, inter:]
            return a @ wd
        orig_shape = x.shape
        H = orig_shape[-1]
        I = base_wd.shape[0]
        E = gate_w.shape[1]
        xt = x.reshape(-1, H)
        T = xt.shape[0]
        base_y = _swiglu_mlp(xt, base_wgu, base_wd, I)
        logits = xt @ gate_w
        probs = jax.nn.softmax(logits.astype(jnp.float32), axis=-1)
        topw, topi = jax.lax.top_k(probs, TOP_K)
        topw = topw / jnp.sum(topw, axis=-1, keepdims=True)
        topw = topw.astype(x.dtype)
        cw = jnp.zeros((T, E), x.dtype).at[jnp.arange(T)[:, None], topi].add(topw)
        out = base_y
        for e in range(E):
            ye = _swiglu_mlp(xt, exp_wgu[e], exp_wd[e], I)
            out = out + cw[:, e:e + 1] * ye
        return out.reshape(orig_shape)
    x = x + _L0_xattn_ref(_layernorm(x, axis=-1), ctx_768, L0_xattn_prompt, L0_xattn_w_prompt, L0_xattn_w_img, L0_xattn_w_q, L0_xattn_w_k, L0_xattn_w_v, L0_xattn_w_out, L0_xattn_b_out)
    x = x + _L0_attn_ref(_layernorm(x, axis=-1), L0_attn_Wq_down, L0_attn_Wk_down, L0_attn_Wv_down, L0_attn_Wq_up_c, L0_attn_Wq_up_e, L0_attn_Wk_up_c, L0_attn_Wk_up_e, L0_attn_Wv_up, L0_attn_Wc)
    x = x + _L0_ffn_ref(_layernorm(x, axis=-1), L0_ffn_gate_w, L0_ffn_base_wgu, L0_ffn_base_wd, L0_ffn_exp_wgu, L0_ffn_exp_wd)
    return x

_drawn_inputs = setup_inputs


def setup_inputs(seed=0):
    import zlib

    import numpy as np

    out = dict(_drawn_inputs(seed))
    spreads = {}
    factors = {'L0_xattn_prompt': 8.0,
     'L0_xattn_w_prompt': 8.0,
     'L0_xattn_w_img': 5.908,
     'L0_xattn_b_out': 149.676,
     'L0_attn_Wq_down': 8.0,
     'L0_attn_Wk_down': 8.0,
     'L0_attn_Wv_down': 8.0,
     'L0_attn_Wq_up_c': 8.0,
     'L0_attn_Wq_up_e': 8.0,
     'L0_attn_Wk_up_c': 8.0,
     'L0_attn_Wk_up_e': 8.0,
     'L0_attn_Wv_up': 8.0,
     'L0_attn_Wc': 8.0,
     'L0_ffn_gate_w': 19.116,
     'L0_ffn_exp_wgu': 15.059,
     'L0_ffn_exp_wd': 15.14,
     'L0_ffn_base_wgu': 8.0,
     'L0_ffn_base_wd': 8.0}
    for name, (base, spread) in spreads.items():
        noise = np.random.default_rng([zlib.crc32(name.encode()), seed]).standard_normal(out[name].shape)
        drawn = base * np.exp(spread * noise) if base else spread * noise
        out[name] = jnp.asarray(drawn.astype(out[name].dtype))
    for name, factor in factors.items():
        out[name] = (out[name] * factor).astype(out[name].dtype)
    return out
```

```python
import math
from contextlib import ExitStack

import numpy as np

import concourse.bass as bass
from concourse import mybir

F32 = mybir.dt.float32
F32R = mybir.dt.float32r
ALU = mybir.AluOpType
ACT = mybir.ActivationFunctionType
AX_X = mybir.AxisListType.X

P = 128
T, C = 256, 256
TT, CC = T // P, C // P
D_CTX = 192
REST = D_CTX - P
N_CTX, N_PROMPT = 4096, 64
KEYS = N_CTX + N_PROMPT + T
JT = (KEYS + P - 1) // P
CHUNK = 512
NCH = (KEYS + CHUNK - 1) // CHUNK
XH, XD = 8, 64
PAIRS = XH // 2
AH, AL, AD = 16, 64, 16
AG = AH // 4
WPAD = C + 16
E, I = 8, 704
IFULL, ITAIL = I // P, I % P
ICH = IFULL + 1
EPS = 1e-5
NEG = -1e30


def keys_of(c):
    return min(CHUNK, KEYS - c * CHUNK)


def tiles_of(c):
    return range(4 * c, min(4 * c + 4, JT))


def rows_of(jt):
    return min(P, KEYS - jt * P)


def rope_tables():
    half = AD // 2
    inv = (1.0 / np.power(np.float32(10000.0), np.arange(0, half, 2, dtype=np.float32) / np.float32(half))).astype(np.float32)
    freqs = (np.arange(T, dtype=np.float32)[:, None] * inv[None, :]).astype(np.float32)
    emb = np.concatenate((freqs, freqs), axis=-1)
    cos, sin = np.cos(emb).astype(np.float32), np.sin(emb).astype(np.float32)
    tab = np.zeros((P, 2, T), np.float32)
    for r in range(4):
        tab[32 * r:32 * r + half, 0] = 1.0
        tab[32 * r + half:32 * r + AD, 0] = cos.T
        tab[32 * r + half:32 * r + AD, 1] = sin.T * np.tile(np.float32([-1, 1]), half // 2)[:, None]
    return tab


def perceiver(nc, x, ctxT, promptT, w_prompt, w_img, w_q, w_k, w_v, w_out, b_out, wdT, ups, w_c,
              gate_w, base_wgu, base_wd, exp_wgu, exp_wd, rope, out):
    with ExitStack() as stack:
        sem_of = {}

        def sem(name):
            sem_of[name] = stack.enter_context(nc.semaphore(name))
            return sem_of[name]

        top = [0]

        def at(name, shape, dt, offset=None):
            size = int(np.prod(shape[1:])) * 4
            if offset is None:
                offset = base + top[0]
                top[0] += (size + 31) // 32 * 32
            return nc.alloc_sbuf_tensor_at(name, shape, dt, offset=offset)

        def psum(name):
            return stack.enter_context(nc.psum_tensor(name, [P, 512], F32))

        base = (nc.sbuf_base + 31) // 32 * 32
        ks_at = base + top[0]
        ks = at("ks", [P, 2, KEYS], F32R)
        v_at = base + top[0]
        v = at("v", [P, JT, 4 * XD], F32)
        c_at = base + top[0]
        c1h = at("c1h", [P, KEYS], F32R)
        c1l = at("c1l", [P, KEYS], F32R)
        cr = at("cr", [P, KEYS], F32R)
        qs_at = base + top[0]
        qh = at("qh", [P, XH, T], F32R)
        ql = at("ql", [P, XH, T], F32R)
        wk1h, wk1l, wkrh, wkrl = (at(n, [P, 512], F32R) for n in ("wk1h", "wk1l", "wkrh", "wkrl"))
        wv1h, wv1l, wvrh, wvrl = (at(n, [P, 512], F32R) for n in ("wv1h", "wv1l", "wvrh", "wvrl"))
        wout = at("wout", [P, PAIRS, C], F32)
        weff = {n: at("weff_" + n, [P, CC, AH * 32], F32) for n in ("q", "qr", "k", "kr")}
        weff["v"] = at("weff_v", [P, CC, C], F32)
        ident = at("ident", [P, P], F32)
        mask = at("mask", [P, 2 * P], F32)
        ones = at("ones", [P, P], F32)
        gsel = at("gsel", [P, XD], F32)
        RING = 5
        ering_at = base + top[0]
        ering = at("ering", [P, RING, 512], F32)
        mb_at = base + top[0]
        mb = at("mb", [P, 2, 512], F32)
        xn = at("xn", [P, TT, C], F32, mb_at)
        diag = at("diag", [P, 512], F32)
        den = at("den", [P, 512], F32)
        pvs = at("pvs", [P, T], F32)
        rden = at("rden", [P, T], F32)
        ot_at = base + top[0]
        ot = at("ot", [P, PAIRS, T], F32)
        xs = at("xs", [P, TT, C], F32)
        xnT = at("xnT", [P, CC, T], F32)
        bb = at("bb", [P, C], F32)
        mx = at("mx", [P, 4, NCH], F32)
        m4 = at("m4", [P, 2, 4], F32)
        st = at("st", [P, TT, 6], F32)
        ag = at("ag", [P, TT, 2], F32)
        sd = at("sd", [P, TT], F32)
        rs = at("rs", [P, TT], F32)
        epst = at("epst", [P, 1], F32)
        iota8 = at("iota8", [P, E], F32)
        gatew = at("gatew", [P, CC, E], F32)
        bdq = at("bdq", [P, 2, 2, AD], F32)
        bdk = at("bdk", [P, 2, 2, AD], F32)
        bdv = at("bdv", [P, 2, AD], F32)
        assert base + top[0] <= nc.sbuf_usable_end, (base + top[0], nc.sbuf_usable_end)

        wdt_s = at("wdt_s", [P, 3, 8, C], F32, ks_at)
        wqd = at("wqd", [P, CC, XH, 2, XD], F32, ks_at + 3 * 8 * C * 4)
        raw = at("raw", [P, 8, 2, CHUNK], F32, v_at)
        wraw = at("wraw", [P, 4, 512], F32, ering_at)
        wimg = at("wimg", [P, CC, D_CTX], F32, ks_at + 3 * 8 * C * 4 + CC * XH * 2 * XD * 4)
        assert 3 * 8 * C * 4 + CC * XH * 2 * XD * 4 + CC * D_CTX * 4 <= 2 * KEYS * 4
        wprm = at("wprm", [P, CC, D_CTX], F32, ot_at)
        prm = at("prm", [P, CC, N_PROMPT], F32, ot_at + CC * D_CTX * 4)

        s2 = at("s2", [P, 3, 2048], F32, c_at)
        pt = at("pt", [P, AH, 3 * P], F32, c_at + 3 * 2048 * 4)
        q2 = at("q2", [P, AG, T], F32, qs_at)
        k2 = at("k2", [P, AG, T], F32, qs_at + 4096)
        r2 = at("r2", [P, 4, 2, T], F32, qs_at + 8192)
        v2 = at("v2", [P, TT, WPAD], F32, qs_at + 16384)
        wc = at("wc", [P, AG, C], F32, qs_at + 18560)
        y2 = at("y2", [P, AG, T], F32, qs_at + 22656)
        tab = at("tab", [P, 2, T], F32, qs_at + 28672)
        mx2 = at("mx2", [P, 32], F32, qs_at + 26752)
        nb2 = at("nb2", [P, 32], F32, qs_at + 26880)
        dn2 = at("dn2", [P, 32], F32, qs_at + 27008)
        rd2 = at("rd2", [P, 32], F32, qs_at + 27136)
        SLOT = (CC * 2 * I + ICH * C) * 4
        slot_at = [ks_at + i * SLOT for i in range(4)] + [c_at + i * SLOT for i in range(3)]
        NSLOT = len(slot_at)
        assert 4 * SLOT <= c_at - ks_at and 3 * SLOT <= qs_at - c_at
        wgu = [at(f"wgu{i}", [P, CC, 2 * I], F32, a) for i, a in enumerate(slot_at)]
        wd = [at(f"wd{i}", [P, ICH, C], F32, a + CC * 2 * I * 4) for i, a in enumerate(slot_at)]
        hid = [at(f"hid{i}", [P, ICH, T], F32, qs_at + i * ICH * T * 4) for i in range(2)]
        sg = at("sg", [P, 2, T], F32, qs_at + 2 * ICH * T * 4)
        acc = at("acc", [P, TT, C], F32, qs_at + 2 * ICH * T * 4 + 2048)
        cw_at = qs_at + 27264
        lg = at("lg", [P, TT, 8], F32, cw_at)
        t8 = at("t8", [P, TT, 8], F32, cw_at + 64)
        ng = at("ng", [P, TT], F32, cw_at + 128)
        ex = at("ex", [P, TT, 8], F32, cw_at + 160)
        e8 = at("e8", [P, TT, 8], F32, cw_at + 224)
        i8 = at("i8", [P, TT, 8], mybir.dt.uint32, cw_at + 288)
        fi = at("fi", [P, TT, 8], F32, cw_at + 352)
        sl = at("sl", [P, TT, 8], F32, cw_at + 416)
        w2 = at("w2", [P, TT], F32, cw_at + 480)
        rw = at("rw", [P, TT], F32, cw_at + 512)
        cw = at("cw", [P, TT, 8], F32, cw_at + 544)

        bank = [psum(f"bank{i}") for i in range(8)]
        ST, PJ, PR, PV, DEN = bank[0:3], bank[3], bank[4:6], bank[6], bank[7]

        x_in, wdt_in, up_in, qw_in, cw_in, kvw_in, misc_in = (sem(n) for n in (
            "x_in", "wdt_in", "up_in", "qw_in", "cw_in", "kvw_in", "misc_in"))
        raw_in = [sem(f"raw_in{i}") for i in range(4)]
        ffn_in = [sem(f"ffn_in{i}") for i in range(NSLOT)]
        wc_in, wc_zero = sem("wc_in"), sem("wc_zero")
        out_done, tab_in, gsel_ready = sem("out_done"), sem("tab_in"), sem("gsel_ready")
        const_ready, bd_zero, bd_ready = sem("const_ready"), sem("bd_zero"), sem("bd_ready")
        fold_done, fold_out = sem("fold_done"), sem("fold_out")
        ln_ready, sd_ready, xn_ready, xt_done, xt_ready = (
            sem("ln_ready"), sem("sd_ready"), sem("xn_ready"), sem("xt_done"), sem("xt_ready"))
        dchain = sem("dchain")
        qp_done, qh_ready, ql_ready = sem("qp_done"), sem("qh_ready"), sem("ql_ready")
        xc_done = sem("xc_done")
        whi, wlo = sem("whi"), sem("wlo")
        chi, clo = sem("chi"), sem("clo")
        vp_done, vp_out = sem("vp_done"), sem("vp_out")
        kp_done, khi, klo = sem("kp_done"), sem("khi"), sem("klo")
        pr_done, pr_max = sem("pr_done"), sem("pr_max")
        dg_ready, mb_done, mb_ready = sem("dg_ready"), sem("mb_done"), sem("mb_ready")
        st_done, mid_ready, e_ready, pv_done = sem("st_done"), sem("mid_ready"), sem("e_ready"), sem("pv_done")
        den_out, pv_out, db_done, ot_ready = sem("den_out"), sem("pv_out"), sem("db_done"), sem("ot_ready")
        xo_done, xb_ready = sem("xo_done"), sem("xb_ready")
        qk_done, qk_ready, v2_done, v2_ready = sem("qk_done"), sem("qk_ready"), sem("v2_done"), sem("v2_ready")
        s2_done, s2_ready, p2_ready, pn_ready = sem("s2_done"), sem("s2_ready"), sem("p2_ready"), sem("pn_ready")
        tp_done, tpa, tpd = sem("tp_done"), sem("tpa"), sem("tpd")
        y2_done, y2_ready, o2_done = sem("y2_done"), sem("y2_ready"), sem("o2_done")
        lg_done, ex_ready, ng_ready, cw_ready = sem("lg_done"), sem("ex_ready"), sem("ng_ready"), sem("cw_ready")
        gu_done, sg_ready, hid_ready, yd_done, acc_ready = (
            sem("gu_done"), sem("sg_ready"), sem("hid_ready"), sem("yd_done"), sem("acc_ready"))

        block = stack.enter_context(nc.Block())

        VG = [(jt, min(jt + 2, JT)) for jt in range(0, JT, 2)]

        def vg_of(c):
            return range(2 * c, min(2 * c + 2, len(VG)))

        def kp_index(p, c):
            return p * NCH + c

        def expert(e):
            return (base_wgu, base_wd) if e == 0 else (exp_wgu[e - 1], exp_wd[e - 1])

        def GU(n):
            return bank[n % 6]

        def pt_dst(i):
            return pt[:, :, :].rearrange("p h k -> p (h k)")[:, 512 * i:512 * i + 512]

        @block.sync
        def _(sp):
            sp.dma_start(xs[:, :, :], x.rearrange("(t p) c -> p t c", p=P)).then_inc(x_in, 16)
            for rep in range(2):
                for ct in range(CC):
                    sp.dma_start(wqd[:, ct, :, rep, :],
                                 w_q[ct * P:(ct + 1) * P, :].rearrange("p (h d) -> p h d", d=XD)).then_inc(qw_in, 16)
            sp.dma_start(wraw[:, 0, :], w_k[0:P, :]).then_inc(kvw_in, 16)
            sp.dma_start(wraw[:, 2, :], w_v[0:P, :]).then_inc(kvw_in, 16)
            for n in range(4):
                for part in range(2):
                    rows = P if part == 0 else REST
                    sp.dma_start(raw[0:rows, 2 * n:2 * n + 2, part, :],
                                 ctxT[part * P:part * P + rows, 2 * n * CHUNK:(2 * n + 2) * CHUNK].rearrange(
                                     "p (c k) -> p c k", c=2)).then_inc(raw_in[n], 16)
            sp.dma_start(wout[:, :, :], w_out.rearrange("(a p) c -> p a c", p=P)).then_inc(misc_in, 16)
            sp.dma_start(bb[:, :], b_out.rearrange("(a c) -> a c", a=1).broadcast_to([P, C])).then_inc(misc_in, 16)
            sp.dma_start(gatew[:, :, :], gate_w.rearrange("(a p) e -> p a e", p=P)).then_inc(misc_in, 16)
            for e in range(E + 1):
                s = e % NSLOT
                if e == 0:
                    sp.wait_ge(pv_done, PAIRS * JT)
                    sp.dma_start(tab[:, :, :], rope).then_inc(tab_in, 16)
                if e == 4:
                    sp.wait_ge(y2_done, 2)
                if e >= NSLOT:
                    sp.wait_ge(yd_done, e - NSLOT + 1)
                gu, dn = expert(e)
                sp.dma_start(wgu[s][:, :, :], gu.rearrange("(a p) n -> p a n", p=P)).then_inc(ffn_in[s], 16)
                sp.dma_start(wd[s][:, 0:IFULL, :], dn[0:IFULL * P, :].rearrange("(a p) c -> p a c", p=P)).then_inc(ffn_in[s], 16)
                sp.dma_start(wd[s][0:ITAIL, IFULL, :], dn[IFULL * P:I, :]).then_inc(ffn_in[s], 16)
            sp.wait_ge(acc_ready, (E + 1) * TT)
            sp.dma_start(out.rearrange("(t p) c -> p t c", p=P), acc[:, :, :]).then_inc(out_done, 16)
            sp.wait_ge(out_done, 16)

        @block.gpsimd
        def _(pool):
            for bd in (bdq, bdk, bdv):
                pool.memset(bd[:], 0.0).then_inc(bd_zero, 1)
            pool.wait_ge(bd_zero, 3)
            for n, bd in ((0, bdq), (1, bdk)):
                for h in range(2):
                    rows = slice(AL * h, AL * h + AL)
                    pool.dma_start(bd[rows, 0, h, 0:8], ups[2 * n]).then_inc(up_in, 16)
                    pool.dma_start(bd[rows, 0, h, 8:16], ups[2 * n + 1]).then_inc(up_in, 16)
                    pairs = bd[rows, 1, h, 8:16].rearrange("p (m two) -> p m two", two=2)
                    src = ups[2 * n + 1].rearrange("p (m two) -> p m two", two=2)
                    for k in range(2):
                        with nc.allow_non_contiguous_dma(reason="four columns"):
                            pool.dma_start(pairs[:, :, k], src[:, :, 1 - k]).then_inc(up_in, 16)
            for h in range(2):
                pool.dma_start(bdv[AL * h:AL * h + AL, h, :], ups[4]).then_inc(up_in, 16)
            pool.memset(ident[:], 0.0).then_inc(const_ready, 1)
            pool.memset(mask[:], 0.0).then_inc(const_ready, 1)
            pool.memset(ones[:], 1.0).then_inc(const_ready, 1)
            pool.memset(epst[:], EPS).then_inc(const_ready, 1)
            for n in ("q", "qr", "k", "kr", "v"):
                pool.memset(weff[n][:], 0.0).then_inc(const_ready, 1)
            for e in range(E):
                pool.memset(iota8[:, e:e + 1], float(e)).then_inc(const_ready, 1)
            pool.wait_ge(const_ready, 9 + E)
            pool.affine_select(out=ident[:, :], in_=ident[:, :], compare_op=ALU.not_equal, fill=1.0, base=0,
                               pattern=[[-1, P]], channel_multiplier=1).then_inc(const_ready, 1)
            pool.affine_select(out=mask[:, P:2 * P], in_=mask[:, P:2 * P], compare_op=ALU.is_ge, fill=NEG, base=0,
                               pattern=[[-1, P]], channel_multiplier=1).then_inc(const_ready, 1)
            pool.wait_ge(pv_done, PAIRS * JT)
            pool.memset(v2[:, :, C:WPAD], 0.0).then_inc(wc_zero, 1)
            pool.memset(wc[:, :, :], 0.0).then_inc(wc_zero, 1)
            pool.wait_ge(wc_zero, 2)
            for r in range(4):
                pool.dma_start(wc[32 * r:32 * r + AD, :, :],
                               w_c.rearrange("(g r d) c -> r d g c", g=AG, r=4)[r]).then_inc(wc_in, 16)

        CONST = 11 + E

        @block.scalar
        def _(act):
            for n in range(3):
                act.dma_start(wdt_s[:, n, :, :], wdT[n].rearrange("(k p) c -> p k c", p=P)).then_inc(wdt_in, 16)
            for half in range(2):
                act.dma_start(wraw[64 * half:64 * half + REST, 1, :], w_k[P:D_CTX, :]).then_inc(kvw_in, 16)
                act.dma_start(wraw[64 * half:64 * half + REST, 3, :], w_v[P:D_CTX, :]).then_inc(kvw_in, 16)
            act.dma_start(wimg[:, :, :], w_img.rearrange("(a p) n -> p a n", p=P)).then_inc(cw_in, 16)
            act.dma_start(wprm[:, :, :], w_prompt.rearrange("(a p) n -> p a n", p=P)).then_inc(cw_in, 16)
            act.dma_start(prm[:, :, :], promptT.rearrange("(a p) n -> p a n", p=P)).then_inc(cw_in, 16)

            def ln_root(n):
                act.wait_ge(ln_ready, n + 1)
                act.activation(sd[:, :], ag[:, :, 1], ACT.Sqrt, bias=epst[:, 0:1]).then_inc(sd_ready, 1)

            def xt_copy(n, ps):
                act.wait_ge(xt_done, n + 1)
                act.activation(xnT[:, :, :], ps[:, :].rearrange("p (a t) -> p a t", a=CC), ACT.Copy).then_inc(xt_ready, 1)

            act.wait_ge(const_ready, CONST)
            ln_root(0)
            for i, (n, ct, ps) in enumerate((("q", 0, ST[0]), ("q", 1, ST[1]), ("k", 0, ST[2]), ("k", 1, PJ))):
                act.wait_ge(fold_done, i + 1)
                src = ps[:, :].rearrange("p (k two h d) -> p two k h d", k=8, two=2, h=2)
                for j, nm in enumerate((n, n + "r")):
                    act.activation(weff[nm][:, ct, :].rearrange("p (k h d) -> p k h d", k=8, h=2)[:, :, :, 0:AD],
                                   src[:, j, :, :, :], ACT.Copy).then_inc(fold_out, 1)
            act.wait_ge(fold_done, 5)
            act.activation(weff["v"][:, :, 0:C], PR[0][:, :].rearrange("p (a m) -> p a m", a=CC), ACT.Copy).then_inc(fold_out, 1)
            xt_copy(0, PR[1])
            act.wait_ge(kvw_in, 96)
            for i, w in enumerate((wk1h, wkrh, wv1h, wvrh)):
                act.activation(w[:, :], wraw[:, i, :], ACT.Copy).then_inc(whi, 1)
            for i in range(4):
                act.wait_ge(qp_done, i + 1)
                act.activation(qh[:, 2 * i:2 * i + 2, :], bank[i][:, :].rearrange("p (h t) -> p h t", h=2),
                               ACT.Copy).then_inc(qh_ready, 1)
            for c in range(NCH):
                cols = slice(c * CHUNK, c * CHUNK + keys_of(c))
                if c < 8:
                    act.wait_ge(raw_in[c // 2], 32)
                    s1, s2_ = raw[:, c, 0, :], raw[0:REST, c, 1, :]
                else:
                    act.wait_ge(xc_done, 1)
                    s1, s2_ = PV[:, 0:keys_of(c)], DEN[0:REST, 0:keys_of(c)]
                act.activation(c1h[:, cols], s1, ACT.Copy).then_inc(chi, 1)
                act.activation(cr[0:REST, cols], s2_, ACT.Copy).then_inc(chi, 1)

            def values_out(half, c):
                for g in vg_of(c):
                    a, b = VG[g]
                    i = half * len(VG) + g
                    act.wait_ge(vp_done, i + 1)
                    if half == 0:
                        act.wait_ge(clo, 2 * min(c + 1, 8))
                        ps = ST[g % 3]
                    else:
                        ps = PJ
                    r = rows_of(b - 1)
                    act.activation(v[0:r, a:b, :], ps[0:r, 0:256 * (b - a)].rearrange("p (j d) -> p j d", d=4 * XD),
                                   ACT.Copy).then_inc(vp_out, 1)

            def keys_hi(p, c):
                w = keys_of(c)
                cols = slice(c * CHUNK, c * CHUNK + w)
                act.wait_ge(kp_done, kp_index(p, c) + 1)
                act.activation(ks[0:64, 0, cols], PJ[0:64, 0:w], ACT.Copy).then_inc(khi, 1)
                act.activation(ks[64:128, 1, cols], PJ[64:128, 0:w], ACT.Copy).then_inc(khi, 1)

            def mb_copy(p):
                act.wait_ge(mb_done, p + 1)
                if p >= 2:
                    act.wait_ge(mid_ready, JT * (p - 1))
                act.activation(mb[:, p % 2, :], PR[0][:, :], ACT.Copy).then_inc(mb_ready, 1)

            for c in range(NCH):
                values_out(0, c)
                keys_hi(0, c)
            mb_copy(0)

            def exp_tile(n):
                r = rows_of(n % JT)
                act.wait_ge(mid_ready, n + 1)
                e = ering[0:r, n % RING, :]
                act.activation(e, e, ACT.Exp, scale=XD ** -0.5).then_inc(e_ready, 1)

            for p in range(PAIRS):
                for c in range(NCH):
                    for jt in tiles_of(c):
                        exp_tile(p * JT + jt)
                    if p == 1 and c >= 1:
                        values_out(1, c - 1)
                    if p + 1 < PAIRS:
                        keys_hi(p + 1, c)
                if p == 1:
                    values_out(1, NCH - 1)
                act.wait_ge(pv_done, JT * (p + 1))
                if p:
                    act.wait_ge(ot_ready, p)
                act.activation(pvs[:, :], PV[:, 0:T], ACT.Copy).then_inc(pv_out, 1)
                if p + 1 < PAIRS:
                    mb_copy(p + 1)

            ln_root(1)
            xt_copy(1, PR[1])
            act.wait_ge(v2_done, 1)
            act.activation(v2[:, :, 0:C], bank[0][:, :].rearrange("p (t c) -> p t c", t=TT), ACT.Copy).then_inc(v2_ready, 1)
            for rd in range(3):
                nh, w = (16, P) if rd == 0 else (8, 2 * P)
                o = (0, 16, 24)[rd]
                act.wait_ge(s2_ready, rd + 1)
                for i in range(nh):
                    e = s2[:, rd, i * w:(i + 1) * w]
                    act.activation(e, e, ACT.Exp, bias=nb2[:, o + i:o + i + 1], scale=AD ** -0.5,
                                   accum_out=dn2[:, o + i:o + i + 1]).then_inc(p2_ready, 1)
            for i in range(0, 12, 2):
                act.wait_ge(tp_done, i + 1)
                act.activation(pt_dst(i), bank[i % 8][:, :], ACT.Copy).then_inc(tpa, 1)
            act.wait_ge(y2_done, 1)
            act.activation(y2[:, 0:2, :], bank[4][:, :].rearrange("p (g t) -> p g t", g=2), ACT.Copy).then_inc(y2_ready, 1)

            ln_root(2)
            xt_copy(2, PR[1])
            act.wait_ge(ng_ready, 1)
            for tt in range(TT):
                act.activation(ex[:, tt, :], lg[:, tt, :], ACT.Exp, bias=ng[:, tt:tt + 1]).then_inc(ex_ready, 1)
            for e in range(E + 1):
                for i in range(ICH):
                    n = e * ICH + i
                    r = P if i < IFULL else ITAIL
                    act.wait_ge(gu_done, n + 1)
                    if n >= 2:
                        act.wait_ge(hid_ready, n - 1)
                    act.activation(sg[0:r, n % 2, :], GU(n)[0:r, 0:T], ACT.Silu).then_inc(sg_ready, 1)

        @block.vector
        def _(dve):
            chain = [0]

            def link(ins):
                chain[0] += 1
                ins.then_inc(dchain, 1)
                dve.wait_ge(dchain, chain[0])

            def layernorm(n, src):
                for tt in range(TT):
                    link(dve.bn_stats(st[:, tt, :], src[:, tt, :]))
                for tt in range(TT - 1):
                    link(dve.bn_aggr(ag[:, tt, :], st[:, tt, :]))
                dve.bn_aggr(ag[:, TT - 1, :], st[:, TT - 1, :]).then_inc(ln_ready, 1)
                dve.wait_ge(sd_ready, n + 1)
                link(dve.reciprocal(rs[:, :], sd[:, :]))
                for tt in range(TT):
                    dve.tensor_scalar(xn[:, tt, :], src[:, tt, :], ag[:, tt, 0:1], rs[:, tt:tt + 1],
                                      ALU.subtract, ALU.mult).then_inc(xn_ready, 1)

            link(dve.memset(gsel[:, :], 0.0))
            for r in range(4):
                dve.memset(gsel[32 * r:32 * r + 1, :], 1.0).then_inc(gsel_ready, 1)
            dve.wait_ge(x_in, 16)
            layernorm(0, xs)
            dve.wait_ge(kvw_in, 96)
            for i, (w, h) in enumerate(((wk1l, wk1h), (wkrl, wkrh), (wv1l, wv1h), (wvrl, wvrh))):
                dve.wait_ge(whi, i + 1)
                dve.tensor_tensor(w[:, :], wraw[:, i, :], h[:, :].bitcast(F32), ALU.subtract).then_inc(wlo, 1)
            for i in range(4):
                dve.wait_ge(qh_ready, i + 1)
                dve.tensor_tensor(ql[:, 2 * i:2 * i + 2, :], bank[i][:, :].rearrange("p (h t) -> p h t", h=2),
                                  qh[:, 2 * i:2 * i + 2, :].bitcast(F32), ALU.subtract).then_inc(ql_ready, 1)
            for c in range(NCH):
                w = keys_of(c)
                cols = slice(c * CHUNK, c * CHUNK + w)
                s1, s2_ = (raw[:, c, 0, :], raw[0:REST, c, 1, :]) if c < 8 else (PV[:, 0:w], DEN[0:REST, 0:w])
                dve.wait_ge(chi, 2 * c + 1)
                dve.tensor_tensor(c1l[:, cols], s1, c1h[:, cols].bitcast(F32), ALU.subtract).then_inc(clo, 1)
                dve.wait_ge(chi, 2 * c + 2)
                dve.tensor_tensor(cr[REST:P, cols], s2_, cr[0:REST, cols].bitcast(F32), ALU.subtract).then_inc(clo, 1)

            def keys_lo(p, c):
                w = keys_of(c)
                cols = slice(c * CHUNK, c * CHUNK + w)
                dve.wait_ge(kp_done, kp_index(p, c) + 1)
                dve.wait_ge(khi, 2 * kp_index(p, c) + 1)
                dve.tensor_tensor(ks[64:128, 0, cols], PJ[0:64, 0:w], ks[0:64, 0, cols].bitcast(F32),
                                  ALU.subtract).then_inc(klo, 1)
                dve.wait_ge(khi, 2 * kp_index(p, c) + 2)
                dve.tensor_tensor(ks[0:64, 1, cols], PJ[64:128, 0:w], ks[64:128, 1, cols].bitcast(F32),
                                  ALU.subtract).then_inc(klo, 1)

            def chunk_max(p, c):
                w = keys_of(c)
                for k in range(4):
                    i = 4 * kp_index(p, c) + k
                    dve.wait_ge(pr_done, i + 1)
                    dve.tensor_reduce(mx[:, k, c:c + 1], PR[k % 2][:, 0:w], AX_X, ALU.max).then_inc(pr_max, 1)

            def pair_max(p):
                dve.wait_ge(pr_max, 4 * kp_index(p, NCH - 1) + 4)
                link(dve.tensor_reduce(m4[:, p % 2, :], mx[:, :, :], AX_X, ALU.max))
                if p:
                    dve.wait_ge(mb_done, p)
                for k in range(4):
                    dve.tensor_scalar(diag[:, k * P:(k + 1) * P], ident[:, :], m4[:, p % 2, k:k + 1], None,
                                      ALU.mult).then_inc(dg_ready, 1)

            dve.wait_ge(const_ready, CONST)
            for c in range(NCH):
                keys_lo(0, c)
                if c >= 1:
                    chunk_max(0, c - 1)
            chunk_max(0, NCH - 1)
            pair_max(0)
            dve.wait_ge(misc_in, 48)
            dve.wait_ge(xn_ready, TT)
            for tt in range(TT):
                link(dve.tensor_tensor(xs[:, tt, :], xs[:, tt, :], bb[:, :], ALU.add))

            def sub_tile(n):
                p, jt = divmod(n, JT)
                r = rows_of(jt)
                dve.wait_ge(st_done, n + 1)
                if jt == 0:
                    dve.wait_ge(mb_ready, p + 1)
                if n >= RING:
                    dve.wait_ge(pv_done, n - RING + 1)
                dve.tensor_tensor(ering[0:r, n % RING, :], ST[n % 3][0:r, :], mb[0:r, p % 2, :],
                                  ALU.subtract).then_inc(mid_ready, 1)

            for p in range(PAIRS):
                for c in range(NCH):
                    for jt in tiles_of(c):
                        sub_tile(p * JT + jt)
                    if p + 1 < PAIRS:
                        if c >= 1:
                            chunk_max(p + 1, c - 1)
                        keys_lo(p + 1, c)
                dve.wait_ge(pv_done, JT * (p + 1))
                dve.tensor_copy(den[:, :], DEN[:, :]).then_inc(den_out, 1)
                if p + 1 < PAIRS:
                    chunk_max(p + 1, NCH - 1)
                    pair_max(p + 1)
                dve.wait_ge(db_done, p + 1)
                link(dve.reciprocal(rden[:, :], PR[1][:, 0:T]))
                dve.wait_ge(pv_out, p + 1)
                dve.tensor_tensor(ot[:, p, :], pvs[:, :], rden[:, :], ALU.mult).then_inc(ot_ready, 1)

            dve.wait_ge(xo_done, 1)
            link(dve.tensor_tensor(xs[:, :, :], ST[0][:, :].rearrange("p (t c) -> p t c", t=TT), xs[:, :, :], ALU.add))
            layernorm(1, xs)
            dve.wait_ge(tab_in, 16)
            for n, (dst, lo) in enumerate(((q2, 0), (k2, 4))):
                for g in range(AG):
                    dve.wait_ge(qk_done, 4 * n + g + 1)
                    link(dve.tensor_tensor(r2[:, g, :, :], bank[lo + g][:, :].rearrange("p (a t) -> p a t", a=2),
                                           tab[:, :, :], ALU.mult))
                    dve.tensor_tensor(dst[:, g, :], r2[:, g, 0, :], r2[:, g, 1, :], ALU.add).then_inc(qk_ready, 1)
            for rd in range(3):
                nh, w = (16, P) if rd == 0 else (8, 2 * P)
                o, b0 = ((0, 0), (16, 4), (24, 0))[rd]
                mk = mask[:, P:2 * P] if rd == 0 else mask[:, :]
                for r in range(4):
                    dve.wait_ge(s2_done, 4 * rd + r + 1)
                    n = 512 // w
                    link(dve.tensor_tensor(s2[:, rd, 512 * r:512 * r + 512].rearrange("p (a k) -> p a k", k=w),
                                           bank[b0 + r][:, :].rearrange("p (a k) -> p a k", k=w),
                                           mk.rearrange("p (a k) -> p a k", a=1).broadcast_to([P, n, w]), ALU.add))
                link(dve.tensor_reduce(mx2[:, o:o + nh], s2[:, rd, :].rearrange("p (h k) -> p h k", k=w), AX_X, ALU.max))
                dve.tensor_scalar(nb2[:, o:o + nh], mx2[:, o:o + nh], -AD ** -0.5, None, ALU.mult).then_inc(s2_ready, 1)
            for rd in range(3):
                nh, w = (16, P) if rd == 0 else (8, 2 * P)
                o = (0, 16, 24)[rd]
                dve.wait_ge(p2_ready, (16, 24, 32)[rd])
                link(dve.reciprocal(rd2[:, o:o + nh], dn2[:, o:o + nh]))
                pr = s2[:, rd, :].rearrange("p (h k) -> p h k", k=w)
                rb = rd2[:, o:o + nh].rearrange("p (h a) -> p h a", a=1).broadcast_to([P, nh, w])
                dve.tensor_tensor(pr, pr, rb, ALU.mult).then_inc(pn_ready, 1)
            for i in range(1, 12, 2):
                dve.wait_ge(tp_done, i + 1)
                dve.tensor_copy(pt_dst(i), bank[i % 8][:, :]).then_inc(tpd, 1)
            dve.wait_ge(y2_done, 2)
            dve.tensor_copy(y2[:, 2:4, :], bank[5][:, :].rearrange("p (g t) -> p g t", g=2)).then_inc(y2_ready, 1)

            dve.wait_ge(o2_done, 1)
            link(dve.tensor_tensor(xs[:, :, :], bank[6][:, :].rearrange("p (t c) -> p t c", t=TT), xs[:, :, :], ALU.add))
            layernorm(2, xs)
            dve.wait_ge(lg_done, 1)
            link(dve.tensor_copy(lg[:, :, :], PR[0][:, 0:TT * E].rearrange("p (t e) -> p t e", t=TT)))
            for tt in range(TT):
                link(dve.max(t8[:, tt, :], lg[:, tt, :]))
            dve.tensor_scalar(ng[:, :], t8[:, :, 0], -1.0, None, ALU.mult).then_inc(ng_ready, 1)
            dve.wait_ge(ex_ready, TT)
            for tt in range(TT):
                link(dve.max(e8[:, tt, :], ex[:, tt, :]))
            for tt in range(TT):
                link(dve.max_index(i8[:, tt, :], e8[:, tt, :], ex[:, tt, :]))
            link(dve.tensor_copy(fi[:, :, :], i8[:, :, :]))
            for tt in range(TT):
                link(dve.tensor_scalar(sl[:, tt, :], iota8[:, :], fi[:, tt, 0:1], None, ALU.is_equal))
                link(dve.scalar_tensor_tensor(out=sl[:, tt, :], in0=iota8[:, :], scalar=fi[:, tt, 1:2],
                                              in1=sl[:, tt, :], op0=ALU.is_equal, op1=ALU.add))
            link(dve.tensor_tensor(w2[:, :], e8[:, :, 0], e8[:, :, 1], ALU.add))
            link(dve.reciprocal(rw[:, :], w2[:, :]))
            for tt in range(TT):
                link(dve.scalar_tensor_tensor(out=cw[:, tt, :], in0=ex[:, tt, :], scalar=rw[:, tt:tt + 1],
                                              in1=sl[:, tt, :], op0=ALU.mult, op1=ALU.mult))

            def hidden(e):
                for i in range(ICH):
                    n = e * ICH + i
                    r = P if i < IFULL else ITAIL
                    dve.wait_ge(sg_ready, n + 1)
                    if i == 0 and e >= 2:
                        dve.wait_ge(yd_done, e - 1)
                    dve.tensor_tensor(hid[e % 2][0:r, i, :], GU(n)[0:r, T:2 * T], sg[0:r, n % 2, :],
                                      ALU.mult).then_inc(hid_ready, 1)

            hidden(0)
            for e in range(E + 1):
                if e < E:
                    hidden(e + 1)
                dve.wait_ge(yd_done, e + 1)
                if e:
                    dve.wait_ge(acc_ready, TT * e)
                for tt in range(TT):
                    y = bank[6 + e % 2][:, tt * C:(tt + 1) * C]
                    if e == 0:
                        dve.tensor_tensor(acc[:, tt, :], y, xs[:, tt, :], ALU.add).then_inc(acc_ready, 1)
                    else:
                        dve.scalar_tensor_tensor(out=acc[:, tt, :], in0=y, scalar=cw[:, tt, e - 1:e],
                                                 in1=acc[:, tt, :], op0=ALU.mult, op1=ALU.add).then_inc(acc_ready, 1)

        @block.tensor
        def _(pe):
            mm = pe.matmul

            def transposed(n, ps):
                pe.wait_ge(xn_ready, TT * (n + 1))
                for ct in range(CC):
                    for tt in range(TT):
                        ins = pe.transpose(ps[:, ct * T + tt * P:ct * T + (tt + 1) * P],
                                           xn[:, tt, ct * P:(ct + 1) * P], ident[:, :])
                ins.then_inc(xt_done, 1)

            pe.wait_ge(const_ready, CONST)
            pe.wait_ge(up_in, 16 * 18)
            pe.wait_ge(wdt_in, 48)
            pe.wait_ge(bd_zero, 3)
            for w, bd, banks in ((0, bdq, ST[0:2]), (1, bdk, (ST[2], PJ))):
                for ct in range(CC):
                    for k in range(8):
                        ins = mm(banks[ct][:, 64 * k:64 * k + 64], wdt_s[:, w, k, ct * P:(ct + 1) * P],
                                 bd[:, :, :, :].rearrange("p a h d -> p (a h d)"), start=True, stop=True)
                    ins.then_inc(fold_done, 1)
            for ct in range(CC):
                for k in range(8):
                    ins = mm(PR[0][:, ct * C + 32 * k:ct * C + 32 * k + 32], wdt_s[:, 2, k, ct * P:(ct + 1) * P],
                             bdv[:, :, :].rearrange("p h d -> p (h d)"), start=True, stop=True)
            ins.then_inc(fold_done, 1)
            transposed(0, PR[1])
            pe.wait_ge(qw_in, 64)
            pe.wait_ge(xt_ready, 1)
            for h in range(XH):
                if h % 2 == 0:
                    pe.wait_ge(fold_out, 2 * (h // 2 + 1))
                for ct in range(CC):
                    ins = mm(bank[h // 2][:, (h % 2) * T:(h % 2 + 1) * T], wqd[:, ct, h, :, :].rearrange("p a d -> p (a d)"),
                             xnT[:, ct, :], start=(ct == 0), stop=(ct == CC - 1))
                if h % 2:
                    ins.then_inc(qp_done, 1)
            pe.wait_ge(cw_in, 48)
            for ps, lo, n in ((PV, 0, P), (DEN, P, REST)):
                for o, w, rhs, width in ((0, wprm, prm, N_PROMPT), (N_PROMPT, wimg, xnT, T)):
                    for ct in range(CC):
                        ins = mm(ps[0:n, o:o + width], w[:, ct, lo:lo + n], rhs[:, ct, :],
                                 start=(ct == 0), stop=(ct == CC - 1))
            ins.then_inc(xc_done, 1)

            def values(half, c):
                for g in vg_of(c):
                    i = half * len(VG) + g
                    a, b = VG[g]
                    if half == 0:
                        ps = ST[g % 3]
                        if g < 3:
                            pe.wait_ge(ql_ready, 3)
                        else:
                            pe.wait_ge(vp_out, g - 2)
                    else:
                        ps = PJ
                        if g > 2 * c:
                            pe.wait_ge(vp_out, i)
                        else:
                            kp_free()
                    cols = slice(half * 4 * XD, (half + 1) * 4 * XD)
                    for jt in range(a, b):
                        r = rows_of(jt)
                        keys = slice(jt * P, jt * P + r)
                        o = ps[0:r, (jt - a) * 256:(jt - a) * 256 + 256]
                        terms = ((c1h, wv1h), (c1h, wv1l), (c1l, wv1h), (cr, wvrh), (cr, wvrl))
                        for t, (s, w) in enumerate(terms):
                            ins = mm(o, s[:, keys], w[:, cols], start=(t == 0), stop=(t == len(terms) - 1))
                    ins.then_inc(vp_done, 1)

            kp_last = [None]

            def kp_free():
                if kp_last[0] is not None:
                    pe.wait_ge(klo, 2 * kp_last[0] + 2)
                    pe.wait_ge(khi, 2 * kp_last[0] + 2)

            def keys(p, c):
                w = keys_of(c)
                chunk = slice(c * CHUNK, c * CHUNK + w)
                cols = slice(p * P, (p + 1) * P)
                if kp_index(p, c) == 0:
                    pe.wait_ge(ql_ready, 4)
                else:
                    kp_free()
                terms = ((wk1h, c1h), (wk1h, c1l), (wk1l, c1h), (wkrh, cr), (wkrl, cr))
                for t, (s, m) in enumerate(terms):
                    ins = mm(PJ[:, 0:w], s[:, cols], m[:, chunk], start=(t == 0), stop=(t == len(terms) - 1))
                ins.then_inc(kp_done, 1)
                kp_last[0] = kp_index(p, c)

            def look(p, c):
                w = keys_of(c)
                pe.wait_ge(khi, 2 * kp_index(p, c) + 2)
                pe.wait_ge(klo, 2 * kp_index(p, c) + 2)
                for k in range(4):
                    i = 4 * kp_index(p, c) + k
                    if i >= 2:
                        pe.wait_ge(pr_max, i - 1)
                    if c == 0 and k == 0 and p:
                        pe.wait_ge(mb_ready, p)
                    if c == 0 and k == 1 and p >= 2:
                        pe.wait_ge(ot_ready, p - 1)
                    h, qt = divmod(k, 2)
                    mm(PR[k % 2][:, 0:w], qh[:, 2 * p + h, qt * P:(qt + 1) * P],
                       ks[:, h, c * CHUNK:c * CHUNK + w], start=True, stop=True).then_inc(pr_done, 1)

            def spread_max(p):
                pe.wait_ge(dg_ready, 4 * (p + 1))
                pe.wait_ge(pr_max, 4 * kp_index(p, NCH - 1) + 4)
                mm(PR[0][:, :], ones[:, :], diag[:, :], start=True, stop=True).then_inc(mb_done, 1)

            pe.wait_ge(qh_ready, 4)
            pe.wait_ge(fold_out, 9)
            pe.wait_ge(wlo, 4)
            for c in range(NCH):
                pe.wait_ge(clo, 2 * c + 2)
                values(0, c)
                keys(0, c)
                if c >= 1:
                    look(0, c - 1)
            look(0, NCH - 1)
            spread_max(0)
            pe.wait_ge(vp_out, len(VG))

            def scores(n):
                p, jt = divmod(n, JT)
                r = rows_of(jt)
                if n >= 3:
                    pe.wait_ge(mid_ready, n - 2)
                kcols = slice(jt * P, jt * P + r)
                for h in range(2):
                    o = ST[n % 3][0:r, h * T:(h + 1) * T]
                    mm(o, ks[:, h, kcols], qh[:, 2 * p + h, :], start=True, stop=False)
                    ins = mm(o, ks[:, h, kcols], ql[:, 2 * p + h, :], start=False, stop=True)
                ins.then_inc(st_done, 1)

            def attend(n):
                p, jt = divmod(n, JT)
                r = rows_of(jt)
                pe.wait_ge(e_ready, n + 1)
                if jt == 0 and p:
                    pe.wait_ge(pv_out, p)
                    pe.wait_ge(den_out, p)
                if jt == 0 and p == 2:
                    pe.wait_ge(vp_out, 2 * len(VG))
                e = ering[0:r, n % RING, :]
                for h in range(2):
                    d0 = (p % 2) * P + h * XD
                    mm(PV[64 * h:64 * h + 64, 0:T], v[0:r, jt, d0:d0 + XD], e[:, h * T:(h + 1) * T],
                       start=(jt == 0), stop=(jt == JT - 1))
                g = jt % 4
                mm(DEN[32 * g:32 * g + 32, :], ones[0:r, 0:32], e, start=(jt < 4), stop=(jt + 4 >= JT)).then_inc(pv_done, 1)

            LAG = 2
            for p in range(PAIRS):
                for c in range(NCH):
                    for jt in tiles_of(c):
                        n = p * JT + jt
                        scores(n)
                        if jt >= LAG:
                            attend(n - LAG)
                    if c >= 1:
                        if p + 1 < PAIRS:
                            look(p + 1, c - 1)
                        if p == 1:
                            values(1, c - 1)
                            if p + 1 < PAIRS:
                                pe.wait_ge(vp_out, len(VG) + 2 * c)
                    if p + 1 < PAIRS:
                        keys(p + 1, c)
                for n in range(p * JT + JT - LAG, (p + 1) * JT):
                    attend(n)
                if p == 1:
                    values(1, NCH - 1)
                if p + 1 < PAIRS:
                    look(p + 1, NCH - 1)
                pe.wait_ge(gsel_ready, 4)
                pe.wait_ge(den_out, p + 1)
                if p + 1 < PAIRS:
                    pe.wait_ge(pr_max, 4 * kp_index(p + 1, NCH - 1) + 4)
                for h in range(2):
                    ins = mm(PR[1][64 * h:64 * h + 64, 0:T], gsel[:, :], den[:, h * T:(h + 1) * T], start=True, stop=True)
                ins.then_inc(db_done, 1)
                if p + 1 < PAIRS:
                    spread_max(p + 1)

            pe.wait_ge(mid_ready, PAIRS * JT)
            for tt in range(TT):
                for p in range(PAIRS):
                    if tt == 0:
                        pe.wait_ge(ot_ready, p + 1)
                    ins = mm(ST[0][:, tt * C:(tt + 1) * C], ot[:, p, tt * P:(tt + 1) * P], wout[:, p, :],
                             start=(p == 0), stop=(p == PAIRS - 1))
            ins.then_inc(xo_done, 1)

            transposed(1, PR[1])
            pe.wait_ge(xt_ready, 2)

            for n, (w, wr) in enumerate((("q", "qr"), ("k", "kr"))):
                for g in range(AG):
                    ps = bank[4 * n + g]
                    for j, nm in enumerate((w, wr)):
                        for ct in range(CC):
                            ins = mm(ps[:, j * T:(j + 1) * T], weff[nm][:, ct, g * P:(g + 1) * P], xnT[:, ct, :],
                                     start=(ct == 0), stop=(ct == CC - 1))
                    ins.then_inc(qk_done, 1)
            pe.wait_ge(qk_ready, 1)
            for tt in range(TT):
                for ct in range(CC):
                    ins = mm(bank[0][:, tt * C:(tt + 1) * C], xnT[:, ct, tt * P:(tt + 1) * P], weff["v"][:, ct, 0:C],
                             start=(ct == 0), stop=(ct == CC - 1))
            ins.then_inc(v2_done, 1)
            pe.wait_ge(qk_ready, 8)
            pe.wait_ge(v2_ready, 1)
            for rd in range(3):
                qt = 0 if rd == 0 else 1
                gs = ((0, 1, 2, 3), (0, 1), (2, 3))[rd]
                b0, w = ((0, P), (4, 2 * P), (0, 2 * P))[rd]
                for r in range(4):
                    if rd == 2:
                        pe.wait_ge(s2_ready, 1)
                    for i, g in enumerate(gs):
                        rows = slice(32 * r, 32 * r + AD)
                        ins = mm(bank[b0 + r][:, i * w:(i + 1) * w], q2[rows, g, qt * P:(qt + 1) * P], k2[rows, g, 0:w],
                                 start=True, stop=True)
                    ins.then_inc(s2_done, 1)
            for i, (rd, off, pos) in enumerate(BLOCKS):
                if i % 4 == 0:
                    b = i // 4
                    pe.wait_ge(pn_ready, rd + 1)
                    if b >= 8:
                        pe.wait_ge(tpa if b % 2 == 0 else tpd, (b - 8) // 2 + 1)
                    elif b < 4:
                        pe.wait_ge(s2_ready, 3)
                else:
                    pe.wait_ge(pn_ready, rd + 1)
                ins = pe.transpose(bank[(i // 4) % 8][:, (i % 4) * P:(i % 4 + 1) * P], s2[:, rd, off:off + P], ident[:, :])
                if i % 4 == 3:
                    ins.then_inc(tp_done, 1)
            pe.wait_ge(tpa, 6)
            pe.wait_ge(tpd, 6)
            pe.wait_ge(wc_zero, 2)
            ptf = pt[:, :, :].rearrange("p h k -> p (h k)")
            for half in range(2):
                for g in (2 * half, 2 * half + 1):
                    for r in range(4):
                        h = 4 * g + r
                        vc = slice(AD * h, AD * h + 32)
                        o = bank[4 + half][32 * r:32 * r + 32, :]
                        c0 = (g % 2) * T
                        b = {k: BLOCK_AT[(h, k)] for k in range(3)}
                        mm(o[:, c0:c0 + P], v2[:, 0, vc], ptf[:, b[0]:b[0] + P], start=True, stop=True)
                        mm(o[:, c0 + P:c0 + T], v2[:, 0, vc], ptf[:, b[1]:b[1] + P], start=True, stop=False)
                        ins = mm(o[:, c0 + P:c0 + T], v2[:, 1, vc], ptf[:, b[2]:b[2] + P], start=False, stop=True)
                ins.then_inc(y2_done, 1)
            pe.wait_ge(y2_ready, 2)
            pe.wait_ge(wc_in, 64)
            for tt in range(TT):
                for g in range(AG):
                    ins = mm(bank[6][:, tt * C:(tt + 1) * C], y2[:, g, tt * P:(tt + 1) * P], wc[:, g, :],
                             start=(g == 0), stop=(g == AG - 1))
            ins.then_inc(o2_done, 1)

            transposed(2, PR[1])
            pe.wait_ge(xt_ready, 3)
            for tt in range(TT):
                for ct in range(CC):
                    ins = mm(PR[0][:, tt * E:(tt + 1) * E], xnT[:, ct, tt * P:(tt + 1) * P], gatew[:, ct, :],
                             start=(ct == 0), stop=(ct == CC - 1))
            ins.then_inc(lg_done, 1)
            pe.wait_ge(ng_ready, 1)

            def gate_up(e):
                s = e % NSLOT
                pe.wait_ge(ffn_in[s], 48 * (e // NSLOT + 1))
                for i in range(ICH):
                    n = e * ICH + i
                    r = P if i < IFULL else ITAIL
                    if n >= 6:
                        pe.wait_ge(hid_ready, n - 5)
                    for j in range(2):
                        for ct in range(CC):
                            ins = mm(GU(n)[0:r, j * T:(j + 1) * T], wgu[s][:, ct, j * I + i * P:j * I + i * P + r],
                                     xnT[:, ct, :], start=(ct == 0), stop=(ct == CC - 1))
                    ins.then_inc(gu_done, 1)

            def down(e):
                s = e % NSLOT
                if e >= 2:
                    pe.wait_ge(acc_ready, TT * (e - 1))
                pe.wait_ge(hid_ready, (e + 1) * ICH)
                for tt in range(TT):
                    for i in range(ICH):
                        r = P if i < IFULL else ITAIL
                        ins = mm(bank[6 + e % 2][:, tt * C:(tt + 1) * C], hid[e % 2][0:r, i, tt * P:(tt + 1) * P],
                                 wd[s][0:r, i, :], start=(i == 0), stop=(i == ICH - 1))
                ins.then_inc(yd_done, 1)

            gate_up(0)
            for e in range(E + 1):
                if e < E:
                    gate_up(e + 1)
                down(e)


BLOCKS, BLOCK_AT = [], {}
for _rd, _gs, _w in ((0, (0, 1, 2, 3), P), (1, (0, 1), 2 * P), (2, (2, 3), 2 * P)):
    for _r in range(4):
        for _i, _g in enumerate(_gs):
            for _kt in range(_w // P):
                BLOCK_AT[(4 * _g + _r, 0 if _rd == 0 else 1 + _kt)] = P * len(BLOCKS)
                BLOCKS.append((_rd, 512 * _r + _i * _w + _kt * P, len(BLOCKS)))


def kernel(**inputs):
    import concourse.bacc as bacc
    from concourse.bass_utils import run_bass_kernel_spmd

    g = {k: np.asarray(a) for k, a in inputs.items()}
    arrays = {
        "x": g["x"][0],
        "ctxT": g["ctx_768"][0].T,
        "promptT": g["L0_xattn_prompt"][0].T,
        "w_prompt": g["L0_xattn_w_prompt"], "w_img": g["L0_xattn_w_img"], "w_q": g["L0_xattn_w_q"],
        "w_k": g["L0_xattn_w_k"], "w_v": g["L0_xattn_w_v"], "w_out": g["L0_xattn_w_out"], "b_out": g["L0_xattn_b_out"],
        "wdT0": g["L0_attn_Wq_down"].T, "wdT1": g["L0_attn_Wk_down"].T, "wdT2": g["L0_attn_Wv_down"].T,
        "up0": g["L0_attn_Wq_up_c"], "up1": g["L0_attn_Wq_up_e"], "up2": g["L0_attn_Wk_up_c"],
        "up3": g["L0_attn_Wk_up_e"], "up4": g["L0_attn_Wv_up"], "w_c": g["L0_attn_Wc"],
        "gate_w": g["L0_ffn_gate_w"], "base_wgu": g["L0_ffn_base_wgu"], "base_wd": g["L0_ffn_base_wd"],
        "exp_wgu": g["L0_ffn_exp_wgu"], "exp_wd": g["L0_ffn_exp_wd"],
        "rope": rope_tables(),
    }
    arrays = {k: np.ascontiguousarray(a) for k, a in arrays.items()}
    nc = bacc.Bacc("TRN2", target_bir_lowering=False, num_devices=1)
    ap = {k: nc.dram_tensor(k, a.shape, F32, kind="ExternalInput").ap() for k, a in arrays.items()}
    out = nc.dram_tensor("out", (T, C), F32, kind="ExternalOutput").ap()
    perceiver(nc, ap["x"], ap["ctxT"], ap["promptT"], ap["w_prompt"], ap["w_img"], ap["w_q"], ap["w_k"], ap["w_v"],
              ap["w_out"], ap["b_out"], [ap[f"wdT{i}"] for i in range(3)], [ap[f"up{i}"] for i in range(5)],
              ap["w_c"], ap["gate_w"], ap["base_wgu"], ap["base_wd"], ap["exp_wgu"], ap["exp_wd"], ap["rope"], out)
    r = run_bass_kernel_spmd(nc, [arrays], core_ids=[0])
    return r.results[0]["out"].reshape(1, T, C)
```

```python
import math
from contextlib import ExitStack

import numpy as np

import concourse.bass as bass
from concourse import mybir

F32 = mybir.dt.float32
F32R = mybir.dt.float32r
ALU = mybir.AluOpType
ACT = mybir.ActivationFunctionType
AX_X = mybir.AxisListType.X

P = 128
T, C = 256, 256
TT, CC = T // P, C // P
D_CTX = 192
REST = D_CTX - P
N_CTX, N_PROMPT = 4096, 64
KEYS = N_CTX + N_PROMPT + T
JT = (KEYS + P - 1) // P
CHUNK = 512
NCH = (KEYS + CHUNK - 1) // CHUNK
XH, XD = 8, 64
PAIRS = XH // 2
AH, AL, AD = 16, 64, 16
AG = AH // 4
WPAD = C + 16
E, I = 8, 704
IFULL, ITAIL = I // P, I % P
ICH = IFULL + 1
EPS = 1e-5
NEG = -1e30


def keys_of(c):
    return min(CHUNK, KEYS - c * CHUNK)


def tiles_of(c):
    return range(4 * c, min(4 * c + 4, JT))


def rows_of(jt):
    return min(P, KEYS - jt * P)


def place(p, c):
    return p * NCH + (c if p == 0 else (c + 1) % NCH)


KEYS_AT = {0: NCH - 1} | {4 * c + 3: c for c in range(NCH - 1)}
LOOKS_AT = {}
for _c in (NCH - 1, *range(NCH - 1)):
    for _k in range(4):
        _j = 2 + _k if _c == NCH - 1 else 33 + _k // 2 if _c == NCH - 2 else 4 * _c + 5 + _k
        LOOKS_AT.setdefault(_j, []).append((_c, _k))
LAG = 3
VG = [(_jt, min(_jt + 2, JT)) for _jt in range(0, JT, 2)]


def values_at(n):
    g, odd = divmod(n - JT - LAG - 2, 2)
    return g if not odd and 0 <= g < len(VG) else None


def rope_tables():
    half = AD // 2
    inv = (1.0 / np.power(np.float32(10000.0), np.arange(0, half, 2, dtype=np.float32) / np.float32(half))).astype(np.float32)
    freqs = (np.arange(T, dtype=np.float32)[:, None] * inv[None, :]).astype(np.float32)
    emb = np.concatenate((freqs, freqs), axis=-1)
    cos, sin = np.cos(emb).astype(np.float32), np.sin(emb).astype(np.float32)
    tab = np.zeros((P, 2, T), np.float32)
    for r in range(4):
        tab[32 * r:32 * r + half, 0] = 1.0
        tab[32 * r + half:32 * r + AD, 0] = cos.T
        tab[32 * r + half:32 * r + AD, 1] = sin.T * np.tile(np.float32([-1, 1]), half // 2)[:, None]
    return tab


def perceiver(nc, x, ctxT, promptT, w_prompt, w_img, w_q, w_k, w_v, w_out, b_out, wdT, ups, w_c,
              gate_w, base_wgu, base_wd, exp_wgu, exp_wd, rope, out):
    with ExitStack() as stack:
        sem_of = {}

        def sem(name):
            sem_of[name] = stack.enter_context(nc.semaphore(name))
            return sem_of[name]

        top = [0]

        def at(name, shape, dt, offset=None):
            size = int(np.prod(shape[1:])) * 4
            if offset is None:
                offset = base + top[0]
                top[0] += (size + 31) // 32 * 32
            return nc.alloc_sbuf_tensor_at(name, shape, dt, offset=offset)

        def psum(name):
            return stack.enter_context(nc.psum_tensor(name, [P, 512], F32))

        base = (nc.sbuf_base + 31) // 32 * 32
        ks_at = base + top[0]
        ks = at("ks", [P, 2, N_CTX], F32R)
        v_at = base + top[0]
        v = at("v", [P, JT, 4 * XD], F32)
        c_at = base + top[0]
        c1h = at("c1h", [P, KEYS], F32R)
        c1l = at("c1l", [P, KEYS], F32R)
        cr = at("cr", [P, KEYS], F32R)
        ks8 = at("ks8", [P, 2, 2, KEYS - N_CTX], F32R)
        qs_at = base + top[0]
        qh = at("qh", [P, XH, T], F32R)
        ql = at("ql", [P, XH, T], F32R)
        wk1h, wk1l, wkrh, wkrl = (at(n, [P, 512], F32R) for n in ("wk1h", "wk1l", "wkrh", "wkrl"))
        wv_at = base + top[0]
        wv1h, wv1l, wvrh, wvrl = (at(n, [P, 512], F32R) for n in ("wv1h", "wv1l", "wvrh", "wvrl"))
        weff = {n: at("weff_" + n, [P, CC, AH * 32], F32) for n in ("q", "qr", "k", "kr")}
        weff["v"] = at("weff_v", [P, CC, C], F32)
        ident = at("ident", [P, P], F32)
        mask = at("mask", [P, 2 * P], F32)
        ones = at("ones", [P, P], F32)
        onesr = at("onesr", [P, P], F32R)
        gsel = at("gsel", [P, XD], F32)
        RING = 5
        ering_at = base + top[0]
        ering = at("ering", [P, RING, 512], F32)
        mb_at = base + top[0]
        mb = at("mb", [P, 2, 512], F32)
        xn = at("xn", [P, TT, C], F32, mb_at)
        xnT = at("xnT", [P, CC, T], F32, mb_at + TT * C * 4)
        diag = at("diag", [P, 512], F32R)
        den = at("den", [P, 512], F32)
        pvs = at("pvs", [P, T], F32)
        rden = at("rden", [P, T], F32)
        ot_at = base + top[0]
        ot = at("ot", [P, PAIRS, T], F32)
        xs = at("xs", [P, TT, C], F32)
        bb = at("bb", [P, C], F32)
        mx = at("mx", [P, 4, NCH], F32)
        m4 = at("m4", [P, 2, 4], F32)
        st = at("st", [P, TT, 6], F32)
        ag = at("ag", [P, TT, 2], F32)
        sd = at("sd", [P, TT], F32)
        rs = at("rs", [P, TT], F32)
        epst = at("epst", [P, 1], F32)
        iota8 = at("iota8", [P, E], F32)
        gatew = at("gatew", [P, CC, E], F32)
        bdq = at("bdq", [P, 2, 2, AD], F32)
        bdk = at("bdk", [P, 2, 2, AD], F32)
        bdv = at("bdv", [P, 2, AD], F32)
        assert base + top[0] <= nc.sbuf_usable_end, (base + top[0], nc.sbuf_usable_end)

        wdt_s = at("wdt_s", [P, 3, 8, C], F32, ering_at)
        assert ering_at + 3 * 8 * C * 4 <= ot_at + PAIRS * T * 4
        stage = [ks_at]

        def staged(name, shape):
            stage[0] += int(np.prod(shape[1:])) * 4
            assert stage[0] <= v_at
            return at(name, shape, F32, stage[0] - int(np.prod(shape[1:])) * 4)

        wqd = staged("wqd", [P, CC, XH, 2, XD])
        wraw = staged("wraw", [P, 4, 512])
        wimg = staged("wimg", [P, CC, D_CTX])
        wprm = staged("wprm", [P, CC, D_CTX])
        prm = staged("prm", [P, CC, N_PROMPT])
        xn0 = staged("xn0", [P, TT, C])
        xnT0 = staged("xnT0", [P, CC, T])
        wout = at("wout", [P, PAIRS, C], F32, wv_at)
        raw = at("raw", [P, 8, 2, CHUNK], F32, v_at)

        SLOT = (CC * 2 * I + ICH * C) * 4
        s2_at = ks_at + 4 * SLOT
        assert c_at <= s2_at and s2_at + (3 * 2048 + AH * 3 * P) * 4 <= qs_at
        s2 = at("s2", [P, 3, 2048], F32, s2_at)
        pt = at("pt", [P, AH, 3 * P], F32, s2_at + 3 * 2048 * 4)
        q2 = at("q2", [P, AG, T], F32, qs_at)
        k2 = at("k2", [P, AG, T], F32, qs_at + 4096)
        r2 = at("r2", [P, 4, 2, T], F32, qs_at + 8192)
        v2 = at("v2", [P, TT, WPAD], F32, qs_at + 16384)
        wc = at("wc", [P, AG, C], F32, qs_at + 18560)
        y2 = at("y2", [P, AG, T], F32, qs_at + 22656)
        tab = at("tab", [P, 2, T], F32, qs_at + 28672)
        mx2 = at("mx2", [P, 32], F32, qs_at + 26752)
        nb2 = at("nb2", [P, 32], F32, qs_at + 26880)
        dn2 = at("dn2", [P, 32], F32, qs_at + 27008)
        rd2 = at("rd2", [P, 32], F32, qs_at + 27136)
        NSLOT = (qs_at - ks_at) // SLOT
        slot_at = [ks_at + i * SLOT for i in range(NSLOT)]
        wgu = [at(f"wgu{i}", [P, CC, 2 * I], F32, a) for i, a in enumerate(slot_at)]
        wd = [at(f"wd{i}", [P, ICH, C], F32, a + CC * 2 * I * 4) for i, a in enumerate(slot_at)]
        hid = [at(f"hid{i}", [P, ICH, T], F32, qs_at + i * ICH * T * 4) for i in range(2)]
        sg = at("sg", [P, 2, T], F32, qs_at + 2 * ICH * T * 4)
        acc = at("acc", [P, TT, C], F32, qs_at + 2 * ICH * T * 4 + 2048)
        cw_at = qs_at + 27264
        lg = at("lg", [P, TT, 8], F32, cw_at)
        t8 = at("t8", [P, TT, 8], F32, cw_at + 64)
        ng = at("ng", [P, TT], F32, cw_at + 128)
        ex = at("ex", [P, TT, 8], F32, cw_at + 160)
        e8 = at("e8", [P, TT, 8], F32, cw_at + 224)
        i8 = at("i8", [P, TT, 8], mybir.dt.uint32, cw_at + 288)
        fi = at("fi", [P, TT, 8], F32, cw_at + 352)
        sl = at("sl", [P, TT, 8], F32, cw_at + 416)
        w2 = at("w2", [P, TT], F32, cw_at + 480)
        rw = at("rw", [P, TT], F32, cw_at + 512)
        cw = at("cw", [P, TT, 8], F32, cw_at + 544)

        bank = [psum(f"bank{i}") for i in range(8)]
        ST, PJ, PR, PV, DEN = bank[0:3], bank[3], bank[4:6], bank[6], bank[7]

        x_in, wdt_in, up_in, qw_in, cw_in, kvw_in, misc_in = (sem(n) for n in (
            "x_in", "wdt_in", "up_in", "qw_in", "cw_in", "kvw_in", "misc_in"))
        raw_in = [sem(f"raw_in{i}") for i in range(4)]
        ffn_in = [sem(f"ffn_in{i}") for i in range(NSLOT)]
        wc_in, wc_zero = sem("wc_in"), sem("wc_zero")
        wout_in = sem("wout_in")
        out_done, tab_in, gsel_ready = sem("out_done"), sem("tab_in"), sem("gsel_ready")
        const_ready, bd_zero, bd_ready, weff_zero = sem("const_ready"), sem("bd_zero"), sem("bd_ready"), sem("weff_zero")
        fold_done, fold_out = sem("fold_done"), sem("fold_out")
        ln_ready, sd_ready, xn_ready, xt_done, xt_ready = (
            sem("ln_ready"), sem("sd_ready"), sem("xn_ready"), sem("xt_done"), sem("xt_ready"))
        dchain = sem("dchain")
        qp_done, qh_ready, ql_ready = sem("qp_done"), sem("qh_ready"), sem("ql_ready")
        xc_done = sem("xc_done")
        whi, wlo = sem("whi"), sem("wlo")
        chi, c1lo, c1lo8, crlo = sem("chi"), sem("c1lo"), sem("c1lo8"), sem("crlo")
        vp_done, vp_out = sem("vp_done"), sem("vp_out")
        kp_done, khi, klo = sem("kp_done"), sem("khi"), sem("klo")
        pr_done, pr_max = sem("pr_done"), sem("pr_max")
        dg_ready, mb_done, mb_ready = sem("dg_ready"), sem("mb_done"), sem("mb_ready")
        st_done, mid_ready, e_ready, pv_done = sem("st_done"), sem("mid_ready"), sem("e_ready"), sem("pv_done")
        den_out, pv_out, db_done, ot_ready = sem("den_out"), sem("pv_out"), sem("db_done"), sem("ot_ready")
        xo_done, xb_ready = sem("xo_done"), sem("xb_ready")
        qk_done, qk_ready, v2_done, v2_ready = sem("qk_done"), sem("qk_ready"), sem("v2_done"), sem("v2_ready")
        s2_done, s2_ready, p2_ready, pn_ready = sem("s2_done"), sem("s2_ready"), sem("p2_ready"), sem("pn_ready")
        tp_done, tpa, tpd = sem("tp_done"), sem("tpa"), sem("tpd")
        y2_done, y2_ready, o2_done = sem("y2_done"), sem("y2_ready"), sem("o2_done")
        lg_done, ex_ready, ng_ready, cw_ready = sem("lg_done"), sem("ex_ready"), sem("ng_ready"), sem("cw_ready")
        gu_done, sg_ready, hid_ready, yd_done, acc_ready = (
            sem("gu_done"), sem("sg_ready"), sem("hid_ready"), sem("yd_done"), sem("acc_ready"))

        block = stack.enter_context(nc.Block())

        st_at, st_free = {}, []

        def takes(what, release, count):
            st_at[what] = len(st_free)
            st_free.append((release, count))

        for g in range(len(VG)):
            takes(("values", 0, g), vp_out, g + 1)
        for i in range(3):
            takes(("fold", i), fold_out, 2 * i + 2)
        for n in range(PAIRS * JT):
            takes(("scores", n), mid_ready, n + 1)
            if values_at(n) is not None:
                takes(("values", 1, values_at(n)), vp_out, len(VG) + values_at(n) + 1)
            if n % JT == LAG + 1 and n > JT:
                takes(("den", n // JT - 1), ot_ready, n // JT)
        takes(("den", PAIRS - 1), ot_ready, PAIRS)

        def st_bank(*what):
            return ST[st_at[what] % 3]

        def key_cols(p, h, rows, lo, hi):
            if lo >= N_CTX:
                return ks8[rows, p % 2, h, lo - N_CTX:hi - N_CTX]
            return ks[rows, h, lo:hi]

        ALL = slice(0, P)
        LOOK_ORDER = [(c, k) for j in sorted(LOOKS_AT) for c, k in LOOKS_AT[j]]

        def looked(p, c, k):
            return 4 * NCH * p + (4 * c + k if p == 0 else LOOK_ORDER.index((c, k)))


        def expert(e):
            return (base_wgu, base_wd) if e == 0 else (exp_wgu[e - 1], exp_wd[e - 1])

        def GU(n):
            return bank[n % 6]

        def pt_dst(i):
            return pt[:, :, :].rearrange("p h k -> p (h k)")[:, 512 * i:512 * i + 512]

        @block.sync
        def _(sp):
            sp.dma_start(xs[:, :, :], x.rearrange("(t p) c -> p t c", p=P)).then_inc(x_in, 16)
            sp.dma_start(wraw[:, 0, :], w_k[0:P, :]).then_inc(kvw_in, 16)
            sp.dma_start(wraw[:, 2, :], w_v[0:P, :]).then_inc(kvw_in, 16)
            for rep in range(2):
                for ct in range(CC):
                    sp.dma_start(wqd[:, ct, :, rep, :],
                                 w_q[ct * P:(ct + 1) * P, :].rearrange("p (h d) -> p h d", d=XD)).then_inc(qw_in, 16)
            for n in range(4):
                for part in range(2):
                    rows = P if part == 0 else REST
                    sp.dma_start(raw[0:rows, 2 * n:2 * n + 2, part, :],
                                 ctxT[part * P:part * P + rows, 2 * n * CHUNK:(2 * n + 2) * CHUNK].rearrange(
                                     "p (c k) -> p c k", c=2)).then_inc(raw_in[n], 16)
            for h in range(2):
                rows = slice(AL * h, AL * h + AL)
                if h == 0:
                    sp.wait_ge(bd_zero, 3)
                for n, bd in ((0, bdq), (1, bdk)):
                    sp.dma_start(bd[rows, 0, h, 0:8], ups[2 * n]).then_inc(up_in, 16)
                    sp.dma_start(bd[rows, 0, h, 8:16], ups[2 * n + 1]).then_inc(up_in, 16)
                sp.dma_start(bdv[rows, h, :], ups[4]).then_inc(up_in, 16)
            for n in range(3):
                sp.dma_start(wdt_s[:, n, :, :], wdT[n].rearrange("(k p) c -> p k c", p=P)).then_inc(wdt_in, 16)
            sp.dma_start(bb[:, :], b_out.rearrange("(a c) -> a c", a=1).broadcast_to([P, C])).then_inc(misc_in, 16)
            sp.dma_start(gatew[:, :, :], gate_w.rearrange("(a p) e -> p a e", p=P)).then_inc(misc_in, 16)
            sp.wait_ge(vp_out, 2 * len(VG))
            sp.dma_start(wout[:, :, :], w_out.rearrange("(a p) c -> p a c", p=P)).then_inc(wout_in, 16)
            for e in range(E + 1):
                s = e % NSLOT
                if e == 0:
                    sp.wait_ge(pv_done, PAIRS * JT)
                    sp.dma_start(tab[:, :, :], rope).then_inc(tab_in, 16)
                if e == 4:
                    sp.wait_ge(y2_done, 2)
                if e >= NSLOT:
                    sp.wait_ge(yd_done, e - NSLOT + 1)
                gu, dn = expert(e)
                sp.dma_start(wgu[s][:, :, :], gu.rearrange("(a p) n -> p a n", p=P)).then_inc(ffn_in[s], 16)
                sp.dma_start(wd[s][:, 0:IFULL, :], dn[0:IFULL * P, :].rearrange("(a p) c -> p a c", p=P)).then_inc(ffn_in[s], 16)
                sp.dma_start(wd[s][0:ITAIL, IFULL, :], dn[IFULL * P:I, :]).then_inc(ffn_in[s], 16)
            sp.wait_ge(acc_ready, (E + 1) * TT)
            sp.dma_start(out.rearrange("(t p) c -> p t c", p=P), acc[:, :, :]).then_inc(out_done, 16)
            sp.wait_ge(out_done, 16)

        @block.gpsimd
        def _(pool):
            pool.memset(ident[:], 0.0).then_inc(const_ready, 1)
            pool.memset(mask[:], 0.0).then_inc(const_ready, 1)
            pool.memset(ones[:], 1.0).then_inc(const_ready, 1)
            pool.memset(epst[:], EPS).then_inc(const_ready, 1)
            for e in range(E):
                pool.memset(iota8[:, e:e + 1], float(e)).then_inc(const_ready, 1)
            pool.wait_ge(const_ready, 4 + E)
            pool.affine_select(out=ident[:, :], in_=ident[:, :], compare_op=ALU.not_equal, fill=1.0, base=0,
                               pattern=[[-1, P]], channel_multiplier=1).then_inc(const_ready, 1)
            pool.affine_select(out=mask[:, P:2 * P], in_=mask[:, P:2 * P], compare_op=ALU.is_ge, fill=NEG, base=0,
                               pattern=[[-1, P]], channel_multiplier=1).then_inc(const_ready, 1)
            for c in range(NCH - 1):
                cols = slice(c * CHUNK, (c + 1) * CHUNK)
                pool.wait_ge(chi, 2 * c + 1)
                pool.tensor_tensor(c1l[:, cols], raw[:, c, 0, :], c1h[:, cols].bitcast(F32),
                                   ALU.subtract).then_inc(c1lo, 1)
            pool.wait_ge(pv_done, PAIRS * JT)
            pool.memset(v2[:, :, C:WPAD], 0.0).then_inc(wc_zero, 1)
            pool.memset(wc[:, :, :], 0.0).then_inc(wc_zero, 1)
            pool.wait_ge(wc_zero, 2)
            for r in range(4):
                pool.dma_start(wc[32 * r:32 * r + AD, :, :],
                               w_c.rearrange("(g r d) c -> r d g c", g=AG, r=4)[r]).then_inc(wc_in, 16)

        CONST = 6 + E

        @block.scalar
        def _(act):
            for half in range(2):
                act.dma_start(wraw[64 * half:64 * half + REST, 1, :], w_k[P:D_CTX, :]).then_inc(kvw_in, 16)
                act.dma_start(wraw[64 * half:64 * half + REST, 3, :], w_v[P:D_CTX, :]).then_inc(kvw_in, 16)
            act.dma_start(wimg[:, :, :], w_img.rearrange("(a p) n -> p a n", p=P)).then_inc(cw_in, 16)
            act.dma_start(wprm[:, :, :], w_prompt.rearrange("(a p) n -> p a n", p=P)).then_inc(cw_in, 16)
            act.dma_start(prm[:, :, :], promptT.rearrange("(a p) n -> p a n", p=P)).then_inc(cw_in, 16)

            def ln_root(n):
                act.wait_ge(ln_ready, n + 1)
                act.activation(sd[:, :], ag[:, :, 1], ACT.Sqrt, bias=epst[:, 0:1]).then_inc(sd_ready, 1)

            def xt_copy(n, ps, xnT):
                act.wait_ge(xt_done, n + 1)
                act.activation(xnT[:, :, :], ps[:, :].rearrange("p (a t) -> p a t", a=CC), ACT.Copy).then_inc(xt_ready, 1)

            act.wait_ge(const_ready, CONST)
            ln_root(0)
            act.wait_ge(kvw_in, 96)
            for i, w in enumerate((wk1h, wkrh, wv1h, wvrh)):
                act.activation(w[:, :], wraw[:, i, :], ACT.Copy).then_inc(whi, 1)
            xt_copy(0, PR[1], xnT0)

            def context_hi(c):
                cols = slice(c * CHUNK, c * CHUNK + keys_of(c))
                if c < NCH - 1:
                    act.wait_ge(raw_in[c // 2], 32)
                    first, rest = raw[:, c, 0, :], raw[0:REST, c, 1, :]
                else:
                    act.wait_ge(xc_done, 1)
                    first, rest = PV[:, 0:keys_of(c)], DEN[0:REST, 0:keys_of(c)]
                act.activation(c1h[:, cols], first, ACT.Copy).then_inc(chi, 1)
                act.activation(cr[0:REST, cols], rest, ACT.Copy).then_inc(chi, 1)

            context_hi(0)
            for i in range(4):
                act.wait_ge(qp_done, i + 1)
                act.activation(qh[:, 2 * i:2 * i + 2, :], bank[i][:, :].rearrange("p (h t) -> p h t", h=2),
                               ACT.Copy).then_inc(qh_ready, 1)

            def values_out(half, g):
                a, b = VG[g]
                act.wait_ge(vp_done, half * len(VG) + g + 1)
                if half == 0:
                    c = min(a // 4, NCH - 2)
                    act.wait_ge(crlo, c + 1)
                    act.wait_ge(c1lo, c + 1)
                ps = st_bank("values", half, g)
                r = rows_of(b - 1)
                act.activation(v[0:r, a:b, :], ps[0:r, 0:256 * (b - a)].rearrange("p (j d) -> p j d", d=4 * XD),
                               ACT.Copy).then_inc(vp_out, 1)

            def keys_hi(p, c, h):
                w = keys_of(c)
                rows = slice(64 * h, 64 * h + 64)
                act.wait_ge(kp_done, place(p, c) + 1)
                act.activation(key_cols(p, h, rows, c * CHUNK, c * CHUNK + w), PJ[rows, 0:w], ACT.Copy).then_inc(khi, 1)

            def mb_copy(p):
                act.wait_ge(mb_done, p + 1)
                if p >= 2:
                    act.wait_ge(mid_ready, JT * (p - 1))
                act.activation(mb[:, p % 2, :], PR[0][:, :], ACT.Copy).then_inc(mb_ready, 1)

            for c in range(NCH):
                if c + 1 < NCH:
                    context_hi(c + 1)
                keys_hi(0, c, 0)
                keys_hi(0, c, 1)
                for g in range(2 * c, min(2 * c + 2, len(VG))):
                    values_out(0, g)
            for i, (nm, ct) in enumerate((("q", 0), ("q", 1), ("k", 0), ("k", 1))):
                ps = st_bank("fold", i) if i < 3 else PV
                act.wait_ge(fold_done, i + 1)
                src = ps[:, :].rearrange("p (k two h d) -> p two k h d", k=8, two=2, h=2)
                for j, part in enumerate((nm, nm + "r")):
                    act.activation(weff[part][:, ct, :].rearrange("p (k h d) -> p k h d", k=8, h=2)[:, :, :, 0:AD],
                                   src[:, j, :, :, :], ACT.Copy).then_inc(fold_out, 1)
            act.wait_ge(fold_done, 5)
            act.activation(weff["v"][:, :, 0:C], DEN[:, :].rearrange("p (a m) -> p a m", a=CC), ACT.Copy).then_inc(fold_out, 1)
            mb_copy(0)

            def exp_tile(n):
                r = rows_of(n % JT)
                act.wait_ge(mid_ready, n + 1)
                e = ering[0:r, n % RING, :]
                act.activation(e, e, ACT.Exp, scale=XD ** -0.5).then_inc(e_ready, 1)

            def sums_out(p):
                act.wait_ge(pv_done, JT * (p + 1))
                if p:
                    act.wait_ge(ot_ready, p)
                act.activation(pvs[:, :], PV[:, 0:T], ACT.Copy).then_inc(pv_out, 1)

            for n in range(PAIRS * JT):
                p, j = divmod(n, JT)
                ahead = p + 1 < PAIRS
                if j == 0 and ahead:
                    keys_hi(p + 1, NCH - 1, 0)
                    keys_hi(p + 1, NCH - 1, 1)
                if j == 0 and p:
                    mb_copy(p)
                if ahead and j and j % 4 == 0:
                    keys_hi(p + 1, j // 4 - 1, 0)
                exp_tile(n)
                if ahead and j and j % 4 == 0:
                    keys_hi(p + 1, j // 4 - 1, 1)
                if values_at(n) is not None:
                    values_out(1, values_at(n))
                if j == LAG - 1 and p:
                    sums_out(p - 1)
            sums_out(PAIRS - 1)

            ln_root(1)
            xt_copy(1, PR[1], xnT)
            act.wait_ge(v2_done, 1)
            act.activation(v2[:, :, 0:C], bank[0][:, :].rearrange("p (t c) -> p t c", t=TT), ACT.Copy).then_inc(v2_ready, 1)
            for rd in range(3):
                nh, w = (16, P) if rd == 0 else (8, 2 * P)
                o = (0, 16, 24)[rd]
                act.wait_ge(s2_ready, rd + 1)
                for i in range(nh):
                    e = s2[:, rd, i * w:(i + 1) * w]
                    act.activation(e, e, ACT.Exp, bias=nb2[:, o + i:o + i + 1], scale=AD ** -0.5,
                                   accum_out=dn2[:, o + i:o + i + 1]).then_inc(p2_ready, 1)
            for i in range(0, 12, 2):
                act.wait_ge(tp_done, i + 1)
                act.activation(pt_dst(i), bank[i % 8][:, :], ACT.Copy).then_inc(tpa, 1)
            act.wait_ge(y2_done, 1)
            act.activation(y2[:, 0:2, :], bank[4][:, :].rearrange("p (g t) -> p g t", g=2), ACT.Copy).then_inc(y2_ready, 1)

            ln_root(2)
            xt_copy(2, PR[1], xnT)
            act.wait_ge(ng_ready, 1)
            for tt in range(TT):
                act.activation(ex[:, tt, :], lg[:, tt, :], ACT.Exp, bias=ng[:, tt:tt + 1]).then_inc(ex_ready, 1)
            for e in range(E + 1):
                for i in range(ICH):
                    n = e * ICH + i
                    r = P if i < IFULL else ITAIL
                    act.wait_ge(gu_done, n + 1)
                    if n >= 2:
                        act.wait_ge(hid_ready, n - 1)
                    act.activation(sg[0:r, n % 2, :], GU(n)[0:r, 0:T], ACT.Silu).then_inc(sg_ready, 1)

        @block.vector
        def _(dve):
            chain = [0]

            def link(ins):
                chain[0] += 1
                ins.then_inc(dchain, 1)
                dve.wait_ge(dchain, chain[0])

            def layernorm(n, src, xn):
                for tt in range(TT):
                    link(dve.bn_stats(st[:, tt, :], src[:, tt, :]))
                for tt in range(TT - 1):
                    link(dve.bn_aggr(ag[:, tt, :], st[:, tt, :]))
                dve.bn_aggr(ag[:, TT - 1, :], st[:, TT - 1, :]).then_inc(ln_ready, 1)
                dve.wait_ge(sd_ready, n + 1)
                link(dve.reciprocal(rs[:, :], sd[:, :]))
                for tt in range(TT):
                    dve.tensor_scalar(xn[:, tt, :], src[:, tt, :], ag[:, tt, 0:1], rs[:, tt:tt + 1],
                                      ALU.subtract, ALU.mult).then_inc(xn_ready, 1)

            for bd in (bdq, bdk, bdv):
                dve.memset(bd[:], 0.0).then_inc(bd_zero, 1)
            link(dve.memset(gsel[:, :], 0.0))
            for r in range(4):
                dve.memset(gsel[32 * r:32 * r + 1, :], 1.0).then_inc(gsel_ready, 1)
            dve.wait_ge(x_in, 16)
            layernorm(0, xs, xn0)
            for nm in ("q", "qr", "k", "kr"):
                dve.memset(weff[nm][:], 0.0).then_inc(weff_zero, 1)
            dve.wait_ge(kvw_in, 96)
            for i, (w, h) in enumerate(((wk1l, wk1h), (wkrl, wkrh), (wv1l, wv1h), (wvrl, wvrh))):
                dve.wait_ge(whi, i + 1)
                dve.tensor_tensor(w[:, :], wraw[:, i, :], h[:, :].bitcast(F32), ALU.subtract).then_inc(wlo, 1)

            def context_lo(c):
                w = keys_of(c)
                cols = slice(c * CHUNK, c * CHUNK + w)
                dve.wait_ge(chi, 2 * c + 2)
                rest = raw[0:REST, c, 1, :] if c < NCH - 1 else DEN[0:REST, 0:w]
                dve.tensor_tensor(cr[REST:P, cols], rest, cr[0:REST, cols].bitcast(F32), ALU.subtract).then_inc(crlo, 1)
                if c == NCH - 1:
                    dve.tensor_tensor(c1l[:, cols], PV[:, 0:w], c1h[:, cols].bitcast(F32), ALU.subtract).then_inc(c1lo8, 1)

            context_lo(0)
            for i in range(4):
                dve.wait_ge(qh_ready, i + 1)
                dve.tensor_tensor(ql[:, 2 * i:2 * i + 2, :], bank[i][:, :].rearrange("p (h t) -> p h t", h=2),
                                  qh[:, 2 * i:2 * i + 2, :].bitcast(F32), ALU.subtract).then_inc(ql_ready, 1)

            def keys_lo(p, c, h):
                w = keys_of(c)
                rows, other = slice(64 * h, 64 * h + 64), slice(64 - 64 * h, 128 - 64 * h)
                lo, hi = c * CHUNK, c * CHUNK + w
                dve.wait_ge(khi, 2 * place(p, c) + h + 1)
                dve.tensor_tensor(key_cols(p, h, other, lo, hi), PJ[rows, 0:w],
                                  key_cols(p, h, rows, lo, hi).bitcast(F32), ALU.subtract).then_inc(klo, 1)

            def look_max(p, c, k):
                dve.wait_ge(pr_done, looked(p, c, k) + 1)
                dve.tensor_reduce(mx[:, k, c:c + 1], PR[k % 2][:, 0:keys_of(c)], AX_X, ALU.max).then_inc(pr_max, 1)

            def pair_max(p):
                dve.wait_ge(pr_max, 4 * NCH * (p + 1))
                link(dve.tensor_reduce(m4[:, p % 2, :], mx[:, :, :], AX_X, ALU.max))
                if p:
                    dve.wait_ge(mb_done, p)
                else:
                    dve.wait_ge(fold_done, 5)
                for k in range(4):
                    dve.tensor_scalar(diag[:, k * P:(k + 1) * P], ident[:, :], m4[:, p % 2, k:k + 1], None,
                                      ALU.mult).then_inc(dg_ready, 1)

            dve.wait_ge(const_ready, CONST)
            dve.wait_ge(up_in, 16 * 10)
            for bd in (bdq, bdk):
                for k in range(2):
                    dst = bd[:, 1, :, 8:16].rearrange("p h (m two) -> p h m two", two=2)
                    src = bd[:, 0, :, 8:16].rearrange("p h (m two) -> p h m two", two=2)
                    dve.tensor_copy(dst[:, :, :, k], src[:, :, :, 1 - k]).then_inc(bd_ready, 1)
            dve.tensor_copy(onesr[:, :], ones[:, :]).then_inc(gsel_ready, 1)
            for c in range(NCH):
                if c + 1 < NCH:
                    context_lo(c + 1)
                keys_lo(0, c, 0)
                keys_lo(0, c, 1)
                if c >= 1:
                    for k in range(4):
                        look_max(0, c - 1, k)
            for k in range(4):
                look_max(0, NCH - 1, k)
            pair_max(0)
            dve.wait_ge(misc_in, 32)
            dve.wait_ge(xn_ready, TT)
            for tt in range(TT):
                link(dve.tensor_tensor(xs[:, tt, :], xs[:, tt, :], bb[:, :], ALU.add))

            def sub_tile(n):
                p, jt = divmod(n, JT)
                r = rows_of(jt)
                dve.wait_ge(st_done, n + 1)
                if jt == 0:
                    dve.wait_ge(mb_ready, p + 1)
                if n >= RING:
                    dve.wait_ge(pv_done, n - RING + 1)
                dve.tensor_tensor(ering[0:r, n % RING, :], st_bank("scores", n)[0:r, :], mb[0:r, p % 2, :],
                                  ALU.subtract).then_inc(mid_ready, 1)

            def den_copy(p):
                dve.wait_ge(pv_done, JT * (p + 1))
                if p:
                    dve.wait_ge(db_done, p)
                dve.tensor_copy(den[:, :], DEN[:, :]).then_inc(den_out, 1)

            def normalise(p):
                dve.wait_ge(db_done, p + 1)
                link(dve.reciprocal(rden[:, :], st_bank("den", p)[:, 0:T]))
                dve.wait_ge(pv_out, p + 1)
                dve.tensor_tensor(ot[:, p, :], pvs[:, :], rden[:, :], ALU.mult).then_inc(ot_ready, 1)

            for n in range(PAIRS * JT):
                p, j = divmod(n, JT)
                sub_tile(n)
                if p + 1 < PAIRS:
                    if j in (1, 2):
                        keys_lo(p + 1, NCH - 1, j - 1)
                    if j and j % 4 == 0:
                        keys_lo(p + 1, j // 4 - 1, 0)
                    if j == 32 or (j > 4 and j % 4 == 1 and j < 32):
                        keys_lo(p + 1, (j - 1) // 4 - 1 if j < 32 else NCH - 2, 1)
                    for c, k in LOOKS_AT.get(j, ()):
                        look_max(p + 1, c, k)
                if j == LAG - 1 and p:
                    den_copy(p - 1)
                if j == LAG + 2 and p:
                    normalise(p - 1)
                if j == JT - 1 and p + 1 < PAIRS:
                    pair_max(p + 1)
            den_copy(PAIRS - 1)
            normalise(PAIRS - 1)

            dve.wait_ge(xo_done, 1)
            link(dve.tensor_tensor(xs[:, :, :], PJ[:, :].rearrange("p (t c) -> p t c", t=TT), xs[:, :, :], ALU.add))
            layernorm(1, xs, xn)
            dve.wait_ge(tab_in, 16)
            for n, (dst, lo) in enumerate(((q2, 0), (k2, 4))):
                for g in range(AG):
                    dve.wait_ge(qk_done, 4 * n + g + 1)
                    link(dve.tensor_tensor(r2[:, g, :, :], bank[lo + g][:, :].rearrange("p (a t) -> p a t", a=2),
                                           tab[:, :, :], ALU.mult))
                    dve.tensor_tensor(dst[:, g, :], r2[:, g, 0, :], r2[:, g, 1, :], ALU.add).then_inc(qk_ready, 1)
            for rd in range(3):
                nh, w = (16, P) if rd == 0 else (8, 2 * P)
                o, b0 = ((0, 0), (16, 4), (24, 0))[rd]
                mk = mask[:, P:2 * P] if rd == 0 else mask[:, :]
                for r in range(4):
                    dve.wait_ge(s2_done, 4 * rd + r + 1)
                    n = 512 // w
                    link(dve.tensor_tensor(s2[:, rd, 512 * r:512 * r + 512].rearrange("p (a k) -> p a k", k=w),
                                           bank[b0 + r][:, :].rearrange("p (a k) -> p a k", k=w),
                                           mk.rearrange("p (a k) -> p a k", a=1).broadcast_to([P, n, w]), ALU.add))
                link(dve.tensor_reduce(mx2[:, o:o + nh], s2[:, rd, :].rearrange("p (h k) -> p h k", k=w), AX_X, ALU.max))
                dve.tensor_scalar(nb2[:, o:o + nh], mx2[:, o:o + nh], -AD ** -0.5, None, ALU.mult).then_inc(s2_ready, 1)
            for rd in range(3):
                nh, w = (16, P) if rd == 0 else (8, 2 * P)
                o = (0, 16, 24)[rd]
                dve.wait_ge(p2_ready, (16, 24, 32)[rd])
                link(dve.reciprocal(rd2[:, o:o + nh], dn2[:, o:o + nh]))
                pr = s2[:, rd, :].rearrange("p (h k) -> p h k", k=w)
                rb = rd2[:, o:o + nh].rearrange("p (h a) -> p h a", a=1).broadcast_to([P, nh, w])
                dve.tensor_tensor(pr, pr, rb, ALU.mult).then_inc(pn_ready, 1)
            for i in range(1, 12, 2):
                dve.wait_ge(tp_done, i + 1)
                dve.tensor_copy(pt_dst(i), bank[i % 8][:, :]).then_inc(tpd, 1)
            dve.wait_ge(y2_done, 2)
            dve.tensor_copy(y2[:, 2:4, :], bank[5][:, :].rearrange("p (g t) -> p g t", g=2)).then_inc(y2_ready, 1)

            dve.wait_ge(o2_done, 1)
            link(dve.tensor_tensor(xs[:, :, :], bank[6][:, :].rearrange("p (t c) -> p t c", t=TT), xs[:, :, :], ALU.add))
            layernorm(2, xs, xn)
            dve.wait_ge(lg_done, 1)
            link(dve.tensor_copy(lg[:, :, :], PR[0][:, 0:TT * E].rearrange("p (t e) -> p t e", t=TT)))
            for tt in range(TT):
                link(dve.max(t8[:, tt, :], lg[:, tt, :]))
            dve.tensor_scalar(ng[:, :], t8[:, :, 0], -1.0, None, ALU.mult).then_inc(ng_ready, 1)
            dve.wait_ge(ex_ready, TT)
            for tt in range(TT):
                link(dve.max(e8[:, tt, :], ex[:, tt, :]))
            for tt in range(TT):
                link(dve.max_index(i8[:, tt, :], e8[:, tt, :], ex[:, tt, :]))
            link(dve.tensor_copy(fi[:, :, :], i8[:, :, :]))
            for tt in range(TT):
                link(dve.tensor_scalar(sl[:, tt, :], iota8[:, :], fi[:, tt, 0:1], None, ALU.is_equal))
                link(dve.scalar_tensor_tensor(out=sl[:, tt, :], in0=iota8[:, :], scalar=fi[:, tt, 1:2],
                                              in1=sl[:, tt, :], op0=ALU.is_equal, op1=ALU.add))
            link(dve.tensor_tensor(w2[:, :], e8[:, :, 0], e8[:, :, 1], ALU.add))
            link(dve.reciprocal(rw[:, :], w2[:, :]))
            for tt in range(TT):
                link(dve.scalar_tensor_tensor(out=cw[:, tt, :], in0=ex[:, tt, :], scalar=rw[:, tt:tt + 1],
                                              in1=sl[:, tt, :], op0=ALU.mult, op1=ALU.mult))

            def hidden(e):
                for i in range(ICH):
                    n = e * ICH + i
                    r = P if i < IFULL else ITAIL
                    dve.wait_ge(sg_ready, n + 1)
                    if i == 0 and e >= 2:
                        dve.wait_ge(yd_done, e - 1)
                    dve.tensor_tensor(hid[e % 2][0:r, i, :], GU(n)[0:r, T:2 * T], sg[0:r, n % 2, :],
                                      ALU.mult).then_inc(hid_ready, 1)

            hidden(0)
            for e in range(E + 1):
                if e < E:
                    hidden(e + 1)
                dve.wait_ge(yd_done, e + 1)
                if e:
                    dve.wait_ge(acc_ready, TT * e)
                for tt in range(TT):
                    y = bank[6 + e % 2][:, tt * C:(tt + 1) * C]
                    if e == 0:
                        dve.tensor_tensor(acc[:, tt, :], y, xs[:, tt, :], ALU.add).then_inc(acc_ready, 1)
                    else:
                        dve.scalar_tensor_tensor(out=acc[:, tt, :], in0=y, scalar=cw[:, tt, e - 1:e],
                                                 in1=acc[:, tt, :], op0=ALU.mult, op1=ALU.add).then_inc(acc_ready, 1)

        @block.tensor
        def _(pe):
            mm = pe.matmul

            def transposed(n, ps, xn):
                pe.wait_ge(xn_ready, TT * (n + 1))
                for ct in range(CC):
                    for tt in range(TT):
                        ins = pe.transpose(ps[:, ct * T + tt * P:ct * T + (tt + 1) * P],
                                           xn[:, tt, ct * P:(ct + 1) * P], ident[:, :])
                ins.then_inc(xt_done, 1)

            pe.wait_ge(const_ready, CONST)
            transposed(0, PR[1], xn0)
            pe.wait_ge(qw_in, 64)
            pe.wait_ge(xt_ready, 1)
            for h in range(XH):
                for ct in range(CC):
                    ins = mm(bank[h // 2][:, (h % 2) * T:(h % 2 + 1) * T], wqd[:, ct, h, :, :].rearrange("p a d -> p (a d)"),
                             xnT0[:, ct, :], start=(ct == 0), stop=(ct == CC - 1))
                if h % 2:
                    ins.then_inc(qp_done, 1)
            pe.wait_ge(cw_in, 48)
            for ps, lo, n in ((PV, 0, P), (DEN, P, REST)):
                for o, w, rhs, width in ((0, wprm, prm, N_PROMPT), (N_PROMPT, wimg, xnT0, T)):
                    for ct in range(CC):
                        ins = mm(ps[0:n, o:o + width], w[:, ct, lo:lo + n], rhs[:, ct, :],
                                 start=(ct == 0), stop=(ct == CC - 1))
            ins.then_inc(xc_done, 1)

            def st_wait(*what):
                i = st_at[what]
                if i >= 3:
                    pe.wait_ge(*st_free[i - 3])
                elif i == 0:
                    pe.wait_ge(ql_ready, 3)

            def values(half, g):
                a, b = VG[g]
                st_wait("values", half, g)
                ps = st_bank("values", half, g)
                cols = slice(half * 4 * XD, (half + 1) * 4 * XD)
                for jt in range(a, b):
                    r = rows_of(jt)
                    keys = slice(jt * P, jt * P + r)
                    o = ps[0:r, (jt - a) * 256:(jt - a) * 256 + 256]
                    terms = ((c1h, wv1h), (c1h, wv1l), (c1l, wv1h), (cr, wvrh), (cr, wvrl))
                    for t, (s, w) in enumerate(terms):
                        ins = mm(o, s[:, keys], w[:, cols], start=(t == 0), stop=(t == len(terms) - 1))
                ins.then_inc(vp_done, 1)

            def keys(p, c):
                w = keys_of(c)
                chunk = slice(c * CHUNK, c * CHUNK + w)
                cols = slice(p * P, (p + 1) * P)
                if place(p, c) == 0:
                    pe.wait_ge(ql_ready, 4)
                else:
                    pe.wait_ge(khi, 2 * place(p, c))
                    pe.wait_ge(klo, 2 * place(p, c))
                terms = ((wk1h, c1h), (wk1h, c1l), (wk1l, c1h), (wkrh, cr), (wkrl, cr))
                for t, (s, m) in enumerate(terms):
                    ins = mm(PJ[:, 0:w], s[:, cols], m[:, chunk], start=(t == 0), stop=(t == len(terms) - 1))
                ins.then_inc(kp_done, 1)

            def look(p, c, k):
                h, qt = divmod(k, 2)
                i = looked(p, c, k)
                pe.wait_ge(khi, 2 * place(p, c) + h + 1)
                pe.wait_ge(klo, 2 * place(p, c) + h + 1)
                if i >= 2:
                    pe.wait_ge(pr_max, i - 1)
                if p and i == 4 * NCH * p:
                    pe.wait_ge(mb_ready, p)
                mm(PR[k % 2][:, 0:keys_of(c)], qh[:, 2 * p + h, qt * P:(qt + 1) * P],
                   key_cols(p, h, ALL, c * CHUNK, c * CHUNK + keys_of(c)), start=True, stop=True).then_inc(pr_done, 1)

            def spread_max(p):
                pe.wait_ge(dg_ready, 4 * (p + 1))
                mm(PR[0][:, :], onesr[:, :], diag[:, :], start=True, stop=True).then_inc(mb_done, 1)

            def fold():
                pe.wait_ge(bd_ready, 4)
                pe.wait_ge(wdt_in, 48)
                pe.wait_ge(weff_zero, 4)
                for w, bd in ((0, bdq), (1, bdk)):
                    for ct in range(CC):
                        i = 2 * w + ct
                        if i < 3:
                            st_wait("fold", i)
                        else:
                            pe.wait_ge(c1lo8, 1)
                        ps = st_bank("fold", i) if i < 3 else PV
                        for k in range(8):
                            ins = mm(ps[:, 64 * k:64 * k + 64], wdt_s[:, w, k, ct * P:(ct + 1) * P],
                                     bd[:, :, :, :].rearrange("p a h d -> p (a h d)"), start=True, stop=True)
                        ins.then_inc(fold_done, 1)
                for ct in range(CC):
                    for k in range(8):
                        ins = mm(DEN[:, ct * C + 32 * k:ct * C + 32 * k + 32], wdt_s[:, 2, k, ct * P:(ct + 1) * P],
                                 bdv[:, :, :].rearrange("p h d -> p (h d)"), start=True, stop=True)
                ins.then_inc(fold_done, 1)

            pe.wait_ge(qh_ready, 4)
            pe.wait_ge(wlo, 4)
            for c in range(NCH):
                pe.wait_ge(crlo, c + 1)
                if c < NCH - 1:
                    pe.wait_ge(c1lo, c + 1)
                else:
                    pe.wait_ge(c1lo8, 1)
                keys(0, c)
                values(0, 2 * c)
                if c >= 1:
                    look(0, c - 1, 0)
                    look(0, c - 1, 1)
                if 2 * c + 1 < len(VG):
                    values(0, 2 * c + 1)
                if c >= 1:
                    look(0, c - 1, 2)
                    look(0, c - 1, 3)
            pe.wait_ge(gsel_ready, 5)
            fold()
            for k in range(4):
                look(0, NCH - 1, k)
            spread_max(0)
            pe.wait_ge(vp_out, len(VG))
            pe.wait_ge(fold_out, 9)

            def scores(n):
                p, jt = divmod(n, JT)
                r = rows_of(jt)
                st_wait("scores", n)
                for h in range(2):
                    o = st_bank("scores", n)[0:r, h * T:(h + 1) * T]
                    kt = key_cols(p, h, ALL, jt * P, jt * P + r)
                    mm(o, kt, qh[:, 2 * p + h, :], start=True, stop=False)
                    ins = mm(o, kt, ql[:, 2 * p + h, :], start=False, stop=True)
                ins.then_inc(st_done, 1)

            def attend(n):
                p, jt = divmod(n, JT)
                r = rows_of(jt)
                pe.wait_ge(e_ready, n + 1)
                if jt == 0 and p:
                    pe.wait_ge(pv_out, p)
                    pe.wait_ge(den_out, p)
                if p == 2:
                    pe.wait_ge(vp_out, len(VG) + jt // 2 + 1)
                e = ering[0:r, n % RING, :]
                for h in range(2):
                    d0 = (p % 2) * P + h * XD
                    mm(PV[64 * h:64 * h + 64, 0:T], v[0:r, jt, d0:d0 + XD], e[:, h * T:(h + 1) * T],
                       start=(jt == 0), stop=(jt == JT - 1))
                g = jt % 4
                mm(DEN[32 * g:32 * g + 32, :], ones[0:r, 0:32], e, start=(jt < 4), stop=(jt + 4 >= JT)).then_inc(pv_done, 1)

            def spread_den(p):
                st_wait("den", p)
                pe.wait_ge(den_out, p + 1)
                for h in range(2):
                    ins = mm(st_bank("den", p)[64 * h:64 * h + 64, 0:T], gsel[:, :], den[:, h * T:(h + 1) * T],
                             start=True, stop=True)
                ins.then_inc(db_done, 1)

            for n in range(PAIRS * JT):
                p, j = divmod(n, JT)
                scores(n)
                if values_at(n) is not None:
                    values(1, values_at(n))
                if j == LAG + 1 and p:
                    spread_den(p - 1)
                if p + 1 < PAIRS:
                    if j in KEYS_AT:
                        keys(p + 1, KEYS_AT[j])
                    for c, k in LOOKS_AT.get(j, ()):
                        look(p + 1, c, k)
                if j == 1 and p:
                    spread_max(p)
                if n >= LAG:
                    attend(n - LAG)
            for n in range(PAIRS * JT - LAG, PAIRS * JT):
                attend(n)
            spread_den(PAIRS - 1)

            pe.wait_ge(wout_in, 16)
            for tt in range(TT):
                for p in range(PAIRS):
                    if tt == 0:
                        pe.wait_ge(ot_ready, p + 1)
                    ins = mm(PJ[:, tt * C:(tt + 1) * C], ot[:, p, tt * P:(tt + 1) * P], wout[:, p, :],
                             start=(p == 0), stop=(p == PAIRS - 1))
            ins.then_inc(xo_done, 1)

            transposed(1, PR[1], xn)
            pe.wait_ge(xt_ready, 2)

            for n, (w, wr) in enumerate((("q", "qr"), ("k", "kr"))):
                for g in range(AG):
                    ps = bank[4 * n + g]
                    for j, nm in enumerate((w, wr)):
                        for ct in range(CC):
                            ins = mm(ps[:, j * T:(j + 1) * T], weff[nm][:, ct, g * P:(g + 1) * P], xnT[:, ct, :],
                                     start=(ct == 0), stop=(ct == CC - 1))
                    ins.then_inc(qk_done, 1)
            pe.wait_ge(qk_ready, 1)
            for tt in range(TT):
                for ct in range(CC):
                    ins = mm(bank[0][:, tt * C:(tt + 1) * C], xnT[:, ct, tt * P:(tt + 1) * P], weff["v"][:, ct, 0:C],
                             start=(ct == 0), stop=(ct == CC - 1))
            ins.then_inc(v2_done, 1)
            pe.wait_ge(qk_ready, 8)
            pe.wait_ge(v2_ready, 1)
            for rd in range(3):
                qt = 0 if rd == 0 else 1
                gs = ((0, 1, 2, 3), (0, 1), (2, 3))[rd]
                b0, w = ((0, P), (4, 2 * P), (0, 2 * P))[rd]
                for r in range(4):
                    if rd == 2:
                        pe.wait_ge(s2_ready, 1)
                    for i, g in enumerate(gs):
                        rows = slice(32 * r, 32 * r + AD)
                        ins = mm(bank[b0 + r][:, i * w:(i + 1) * w], q2[rows, g, qt * P:(qt + 1) * P], k2[rows, g, 0:w],
                                 start=True, stop=True)
                    ins.then_inc(s2_done, 1)
            for i, (rd, off) in enumerate(BLOCKS):
                if i % 4 == 0:
                    b = i // 4
                    pe.wait_ge(pn_ready, rd + 1)
                    if b >= 8:
                        pe.wait_ge(tpa if b % 2 == 0 else tpd, (b - 8) // 2 + 1)
                    elif b < 4:
                        pe.wait_ge(s2_ready, 3)
                else:
                    pe.wait_ge(pn_ready, rd + 1)
                ins = pe.transpose(bank[(i // 4) % 8][:, (i % 4) * P:(i % 4 + 1) * P], s2[:, rd, off:off + P], ident[:, :])
                if i % 4 == 3:
                    ins.then_inc(tp_done, 1)
            pe.wait_ge(tpa, 6)
            pe.wait_ge(tpd, 6)
            pe.wait_ge(wc_zero, 2)
            ptf = pt[:, :, :].rearrange("p h k -> p (h k)")
            for half in range(2):
                for g in (2 * half, 2 * half + 1):
                    for r in range(4):
                        h = 4 * g + r
                        vc = slice(AD * h, AD * h + 32)
                        o = bank[4 + half][32 * r:32 * r + 32, :]
                        c0 = (g % 2) * T
                        b = {k: BLOCK_AT[(h, k)] for k in range(3)}
                        mm(o[:, c0:c0 + P], v2[:, 0, vc], ptf[:, b[0]:b[0] + P], start=True, stop=True)
                        mm(o[:, c0 + P:c0 + T], v2[:, 0, vc], ptf[:, b[1]:b[1] + P], start=True, stop=False)
                        ins = mm(o[:, c0 + P:c0 + T], v2[:, 1, vc], ptf[:, b[2]:b[2] + P], start=False, stop=True)
                ins.then_inc(y2_done, 1)
            pe.wait_ge(y2_ready, 2)
            pe.wait_ge(wc_in, 64)
            for tt in range(TT):
                for g in range(AG):
                    ins = mm(bank[6][:, tt * C:(tt + 1) * C], y2[:, g, tt * P:(tt + 1) * P], wc[:, g, :],
                             start=(g == 0), stop=(g == AG - 1))
            ins.then_inc(o2_done, 1)

            transposed(2, PR[1], xn)
            pe.wait_ge(xt_ready, 3)
            for tt in range(TT):
                for ct in range(CC):
                    ins = mm(PR[0][:, tt * E:(tt + 1) * E], xnT[:, ct, tt * P:(tt + 1) * P], gatew[:, ct, :],
                             start=(ct == 0), stop=(ct == CC - 1))
            ins.then_inc(lg_done, 1)
            pe.wait_ge(ng_ready, 1)

            def gate_up(e):
                s = e % NSLOT
                pe.wait_ge(ffn_in[s], 48 * (e // NSLOT + 1))
                for i in range(ICH):
                    n = e * ICH + i
                    r = P if i < IFULL else ITAIL
                    if n >= 6:
                        pe.wait_ge(hid_ready, n - 5)
                    for j in range(2):
                        for ct in range(CC):
                            ins = mm(GU(n)[0:r, j * T:(j + 1) * T], wgu[s][:, ct, j * I + i * P:j * I + i * P + r],
                                     xnT[:, ct, :], start=(ct == 0), stop=(ct == CC - 1))
                    ins.then_inc(gu_done, 1)

            def down(e):
                s = e % NSLOT
                if e >= 2:
                    pe.wait_ge(acc_ready, TT * (e - 1))
                pe.wait_ge(hid_ready, (e + 1) * ICH)
                for tt in range(TT):
                    for i in range(ICH):
                        r = P if i < IFULL else ITAIL
                        ins = mm(bank[6 + e % 2][:, tt * C:(tt + 1) * C], hid[e % 2][0:r, i, tt * P:(tt + 1) * P],
                                 wd[s][0:r, i, :], start=(i == 0), stop=(i == ICH - 1))
                ins.then_inc(yd_done, 1)

            gate_up(0)
            for e in range(E + 1):
                if e < E:
                    gate_up(e + 1)
                down(e)


BLOCKS, BLOCK_AT = [], {}
for _rd, _gs, _w in ((0, (0, 1, 2, 3), P), (1, (0, 1), 2 * P), (2, (2, 3), 2 * P)):
    for _r in range(4):
        for _i, _g in enumerate(_gs):
            for _kt in range(_w // P):
                BLOCK_AT[(4 * _g + _r, 0 if _rd == 0 else 1 + _kt)] = P * len(BLOCKS)
                BLOCKS.append((_rd, 512 * _r + _i * _w + _kt * P))


def kernel(**inputs):
    import concourse.bacc as bacc
    from concourse.bass_utils import run_bass_kernel_spmd

    g = {k: np.asarray(a) for k, a in inputs.items()}
    arrays = {
        "x": g["x"][0],
        "ctxT": g["ctx_768"][0].T,
        "promptT": g["L0_xattn_prompt"][0].T,
        "w_prompt": g["L0_xattn_w_prompt"], "w_img": g["L0_xattn_w_img"], "w_q": g["L0_xattn_w_q"],
        "w_k": g["L0_xattn_w_k"], "w_v": g["L0_xattn_w_v"], "w_out": g["L0_xattn_w_out"], "b_out": g["L0_xattn_b_out"],
        "wdT0": g["L0_attn_Wq_down"].T, "wdT1": g["L0_attn_Wk_down"].T, "wdT2": g["L0_attn_Wv_down"].T,
        "up0": g["L0_attn_Wq_up_c"], "up1": g["L0_attn_Wq_up_e"], "up2": g["L0_attn_Wk_up_c"],
        "up3": g["L0_attn_Wk_up_e"], "up4": g["L0_attn_Wv_up"], "w_c": g["L0_attn_Wc"],
        "gate_w": g["L0_ffn_gate_w"], "base_wgu": g["L0_ffn_base_wgu"], "base_wd": g["L0_ffn_base_wd"],
        "exp_wgu": g["L0_ffn_exp_wgu"], "exp_wd": g["L0_ffn_exp_wd"],
        "rope": rope_tables(),
    }
    arrays = {k: np.ascontiguousarray(a) for k, a in arrays.items()}
    nc = bacc.Bacc("TRN2", target_bir_lowering=False, num_devices=1)
    ap = {k: nc.dram_tensor(k, a.shape, F32, kind="ExternalInput").ap() for k, a in arrays.items()}
    out = nc.dram_tensor("out", (T, C), F32, kind="ExternalOutput").ap()
    perceiver(nc, ap["x"], ap["ctxT"], ap["promptT"], ap["w_prompt"], ap["w_img"], ap["w_q"], ap["w_k"], ap["w_v"],
              ap["w_out"], ap["b_out"], [ap[f"wdT{i}"] for i in range(3)], [ap[f"up{i}"] for i in range(5)],
              ap["w_c"], ap["gate_w"], ap["base_wgu"], ap["base_wd"], ap["exp_wgu"], ap["exp_wd"], ap["rope"], out)
    r = run_bass_kernel_spmd(nc, [arrays], core_ids=[0])
    return r.results[0]["out"].reshape(1, T, C)
```

```python
import math
from contextlib import ExitStack

import numpy as np

import concourse.bass as bass
from concourse import mybir

F32 = mybir.dt.float32
F32R = mybir.dt.float32r
ALU = mybir.AluOpType
ACT = mybir.ActivationFunctionType
AX_X = mybir.AxisListType.X

P = 128
T, C = 256, 256
TT, CC = T // P, C // P
D_CTX = 192
REST = D_CTX - P
N_CTX, N_PROMPT = 4096, 64
KEYS = N_CTX + N_PROMPT + T
JT = (KEYS + P - 1) // P
CHUNK = 512
NCH = (KEYS + CHUNK - 1) // CHUNK
XH, XD = 8, 64
PAIRS = XH // 2
AH, AL, AD = 16, 64, 16
AG = AH // 4
WPAD = C + 16
E, I = 8, 704
IFULL, ITAIL = I // P, I % P
ICH = IFULL + 1
EPS = 1e-5
NEG = -1e30


def keys_of(c):
    return min(CHUNK, KEYS - c * CHUNK)


def tiles_of(c):
    return range(4 * c, min(4 * c + 4, JT))


def rows_of(jt):
    return min(P, KEYS - jt * P)


def place(p, c):
    return p * NCH + (c if p == 0 else (c + 1) % NCH)


RAW = ((0, 1), (1, 2), (2, 4), (4, 6), (6, 8))
KEYS_AT = {0: NCH - 1} | {4 * c + 3: c for c in range(NCH - 1)}
LOOKS_AT = {}
for _c in (NCH - 1, *range(NCH - 1)):
    for _k in range(4):
        _j = 2 + _k if _c == NCH - 1 else 33 + _k // 2 if _c == NCH - 2 else 4 * _c + 5 + _k
        LOOKS_AT.setdefault(_j, []).append((_c, _k))
PE_QUADS = (1, 3, 5, 7, 8)
SUMMED = [p * JT + jt for p in range(PAIRS) for jt in range(JT) if p + 1 < PAIRS or jt // 4 not in PE_QUADS]
DIRECT = {p * JT + j for p in range(PAIRS - 1) for j in range(4, JT) if j >= 32 or (j % 4 == 0 and p != 1)}
LAG = 3
VG = [(_jt, min(_jt + 2, JT)) for _jt in range(0, JT, 2)]


def values_at(n):
    g, odd = divmod(n - JT - LAG - 2, 2)
    return g if not odd and 0 <= g < len(VG) else None


def rope_tables():
    half = AD // 2
    inv = (1.0 / np.power(np.float32(10000.0), np.arange(0, half, 2, dtype=np.float32) / np.float32(half))).astype(np.float32)
    freqs = (np.arange(T, dtype=np.float32)[:, None] * inv[None, :]).astype(np.float32)
    emb = np.concatenate((freqs, freqs), axis=-1)
    cos, sin = np.cos(emb).astype(np.float32), np.sin(emb).astype(np.float32)
    tab = np.zeros((P, T + P), np.float32)
    for r in range(4):
        plain, kept, swapped = (32 * r + half * k + np.arange(half) for k in range(3))
        tab[plain, :T] = 1.0
        tab[kept, :T] = cos.T
        tab[swapped, :T] = sin.T * np.tile(np.float32([-1, 1]), half // 2)[:, None]
        tab[plain, T + plain] = 1.0
        for a in (kept, swapped):
            tab[a, T + kept] = tab[a, T + swapped] = 1.0
    return tab


def perceiver(nc, x, ctxT, promptT, w_prompt, w_img, w_q, w_k, w_v, w_out, b_out, wdT, ups, w_c,
              gate_w, base_wgu, base_wd, exp_wgu, exp_wd, rope, out):
    with ExitStack() as stack:
        sem_of = {}

        def sem(name):
            sem_of[name] = stack.enter_context(nc.semaphore(name))
            return sem_of[name]

        top = [0]

        def at(name, shape, dt, offset=None):
            size = int(np.prod(shape[1:])) * 4
            if offset is None:
                offset = base + top[0]
                top[0] += (size + 31) // 32 * 32
            return nc.alloc_sbuf_tensor_at(name, shape, dt, offset=offset)

        def psum(name):
            return stack.enter_context(nc.psum_tensor(name, [P, 512], F32))

        base = (nc.sbuf_base + 31) // 32 * 32
        ks_at = base + top[0]
        ks = at("ks", [P, 2, N_CTX], F32R)
        v_at = base + top[0]
        v = at("v", [P, JT, 4 * XD], F32)
        c_at = base + top[0]
        c1h = at("c1h", [P, KEYS], F32R)
        c1l = at("c1l", [P, KEYS], F32R)
        cr = at("cr", [P, KEYS], F32R)
        ks8 = at("ks8", [P, 2, 2, KEYS - N_CTX], F32R)
        qs_at = base + top[0]
        qh = at("qh", [P, XH, T], F32R)
        ql = at("ql", [P, XH, T], F32R)
        wk1h, wk1l, wkrh, wkrl = (at(n, [P, 512], F32R) for n in ("wk1h", "wk1l", "wkrh", "wkrl"))
        wv_at = base + top[0]
        wv1h, wv1l, wvrh, wvrl = (at(n, [P, 512], F32R) for n in ("wv1h", "wv1l", "wvrh", "wvrl"))
        weff = {n: at("weff_" + n, [P, CC, AH * 32], F32) for n in ("q", "k")}
        weff["v"] = at("weff_v", [P, CC, C], F32)
        ident_at = base + top[0]
        ident = at("ident", [P, P], F32)
        mask = at("mask", [P, 2 * P], F32)
        ones = at("ones", [P, P], F32)
        onesr = at("onesr", [P, P], F32R)
        negr = at("negr", [P, P], F32R)
        gsel = at("gsel", [P, XD], F32)
        RING = 8
        ering_at = base + top[0]
        ering = at("ering", [P, RING, 512], F32)
        mb_at = base + top[0]
        mb = at("mb", [P, 2, 512], F32R)
        xn = at("xn", [P, TT, C], F32, mb_at)
        xnT = at("xnT", [P, CC, T], F32, mb_at + TT * C * 4)
        den = at("den", [P, 512], F32)
        pvs = at("pvs", [P, T], F32)
        rden = at("rden", [P, T], F32)
        diag_at = base + top[0]
        esum = at("esum", [P, 2, 512], F32)
        diag = at("diag", [P, 512], F32R)
        ot_at = base + top[0]
        ot = at("ot", [P, PAIRS, T], F32)
        xs = at("xs", [P, TT, C], F32)
        bb = at("bb", [P, C], F32)
        mx = at("mx", [P, 4, NCH], F32)
        m4 = at("m4", [P, 2, 4], F32)
        st = at("st", [P, TT, 6], F32)
        ag = at("ag", [P, TT, 2], F32)
        sd = at("sd", [P, TT], F32)
        rs = at("rs", [P, TT], F32)
        epst = at("epst", [P, 1], F32)
        spare = at("spare", [P, 1], F32)
        iota8 = at("iota8", [P, E], F32)
        gatew = at("gatew", [P, CC, E], F32)
        bdq = at("bdq", [P, 2, 32], F32)
        bdk = at("bdk", [P, 2, 32], F32)
        bdv = at("bdv", [P, 2, AD], F32)
        assert base + top[0] <= nc.sbuf_usable_end, (base + top[0], nc.sbuf_usable_end)

        wdt_s = at("wdt_s", [P, 3, 8, C], F32, ering_at)
        assert ering_at + 3 * 8 * C * 4 <= diag_at
        stage = [ks_at]

        def staged(name, shape):
            stage[0] += int(np.prod(shape[1:])) * 4
            assert stage[0] <= v_at
            return at(name, shape, F32, stage[0] - int(np.prod(shape[1:])) * 4)

        wq = staged("wq", [P, CC, XH * XD])
        xn0 = staged("xn0", [P, TT, C])
        wraw = staged("wraw", [P, 4, 512])
        wimg = at("wimg", [P, CC, D_CTX], F32, v_at + 8 * 2 * CHUNK * 4)
        wprm = at("wprm", [P, CC, D_CTX], F32, v_at + 8 * 2 * CHUNK * 4 + CC * D_CTX * 4)
        assert 8 * 2 * CHUNK * 4 + 2 * CC * D_CTX * 4 <= JT * 4 * XD * 4
        xnT0 = at("xnT0", [P, CC, T], F32, ot_at)
        prm = at("prm", [P, CC, N_PROMPT], F32, ot_at + CC * T * 4)
        assert CC * (T + N_PROMPT) <= PAIRS * T
        wout = at("wout", [P, PAIRS, C], F32, wv_at)
        raw = at("raw", [P, 8, 2, CHUNK], F32, v_at)

        SLOT = (CC * 2 * I + ICH * C) * 4
        s2_at = ks_at + 4 * SLOT
        assert c_at <= s2_at and s2_at + (3 * 2048 + AH * 3 * P) * 4 <= qs_at
        s2 = at("s2", [P, 3, 2048], F32, s2_at)
        pt = at("pt", [P, AH, 3 * P], F32, s2_at + 3 * 2048 * 4)
        q2 = at("q2", [P, AG, T], F32, qs_at)
        k2 = at("k2", [P, AG, T], F32, qs_at + 4096)
        kb = at("kb", [P, AG, T], F32, qs_at + 8192)
        mask4 = at("mask4", [P, 4, P], F32R, qs_at + 12288)
        mask2 = at("mask2", [P, 2, 2 * P], F32R, qs_at + 14336)
        identr = at("identr", [P, P], F32R, qs_at + 30208)
        q2m = at("q2m", [P, 4, AG, T], F32, ering_at)
        v2 = at("v2", [P, TT, WPAD], F32, qs_at + 16384)
        wc = at("wc", [P, AG, C], F32, qs_at + 18560)
        y2 = at("y2", [P, AG, T], F32, qs_at + 22656)
        tab = at("tab", [P, T + P], F32, qs_at + 28672)
        mx2 = at("mx2", [P, 32], F32, qs_at + 26752)
        nb2 = at("nb2", [P, 32], F32, qs_at + 26880)
        dn2 = at("dn2", [P, 32], F32, qs_at + 27008)
        rd2 = at("rd2", [P, 32], F32, qs_at + 27136)
        rdx = at("rdx", [P, TT, AG, 4, 32], F32, qs_at + 8192)
        rt2 = at("rt2", [P, AG, T], F32, qs_at + 12288)
        NSLOT = 4
        slot_at = [ks_at + i * SLOT for i in range(NSLOT)]
        wgu = [at(f"wgu{i}", [P, 2 * CC, I], F32, a) for i, a in enumerate(slot_at)]
        wd = [at(f"wd{i}", [P, ICH, C], F32, a + CC * 2 * I * 4) for i, a in enumerate(slot_at)]
        ffn = [s2_at]

        def expert_buffer(name, shape, dt=F32R):
            ffn[0] += int(np.prod(shape[1:])) * 4
            assert ffn[0] <= ident_at
            return at(name, shape, dt, ffn[0] - int(np.prod(shape[1:])) * 4)

        gu_h, gu_l, gt_h, gt_l, wd_h, wd_l = [], [], [], [], [], []
        for i in range(2):
            gu_h.append(expert_buffer(f"gu_h{i}", [P, 2 * CC, IFULL * P]))
            gu_l.append(expert_buffer(f"gu_l{i}", [P, 2 * CC, IFULL * P]))
            gt_h.append(expert_buffer(f"gt_h{i}", [P, 2 * CC, ITAIL]))
            gt_l.append(expert_buffer(f"gt_l{i}", [P, 2 * CC, ITAIL]))
            if i == 0:
                assert ffn[0] <= s2_at + 3 * 2048 * 4
            wd_h.append(expert_buffer(f"wd_h{i}", [P, ICH, C]))
            wd_l.append(expert_buffer(f"wd_l{i}", [P, ICH, C]))
        hid_h = [expert_buffer(f"hid_h{i}", [P, ICH, T]) for i in range(2)]
        hid_l = [expert_buffer(f"hid_l{i}", [P, IFULL, T]) for i in range(2)]
        xh, xl = at("xh", [P, CC, T], F32R, ering_at), at("xl", [P, CC, T], F32R, ering_at + 2048)
        hid, sg = at("hid", [P, 2, T], F32, ering_at + 4096), at("sg", [P, 2, T], F32, ering_at + 6144)
        acc = at("acc", [P, TT, C], F32, ering_at + 8192)
        cw_at = ering_at + 10240
        assert cw_at + 640 <= mb_at
        lg = at("lg", [P, TT, 8], F32, cw_at)
        t8 = at("t8", [P, TT, 8], F32, cw_at + 64)
        ng = at("ng", [P, TT], F32, cw_at + 128)
        ex = at("ex", [P, TT, 8], F32, cw_at + 160)
        e8 = at("e8", [P, TT, 8], F32, cw_at + 224)
        i8 = at("i8", [P, TT, 8], mybir.dt.uint32, cw_at + 288)
        fi = at("fi", [P, TT, 8], F32, cw_at + 352)
        sl = at("sl", [P, TT, 8], F32, cw_at + 416)
        w2 = at("w2", [P, TT], F32, cw_at + 480)
        rw = at("rw", [P, TT], F32, cw_at + 512)
        cw = at("cw", [P, TT, 8], F32, cw_at + 544)

        bank = [psum(f"bank{i}") for i in range(8)]
        ST, PJ, PR, PV, DEN = bank[0:3], bank[3], bank[4:6], bank[6], bank[7]
        XT = PR

        x_in, wdt_in, up_in, qw_in, cw_in, kw_in, vw_in, misc_in = (sem(n) for n in (
            "x_in", "wdt_in", "up_in", "qw_in", "cw_in", "kw_in", "vw_in", "misc_in"))
        raw_in = [sem(f"raw_in{i}") for i in range(len(RAW))]
        ffn_in = [sem(f"ffn_in{i}") for i in range(NSLOT)]
        wc_in, wc_zero = sem("wc_in"), sem("wc_zero")
        wout_in = sem("wout_in")
        out_done, tab_in, gsel_ready = sem("out_done"), sem("tab_in"), sem("gsel_ready")
        const_ready, bd_zero, bd_ready = sem("const_ready"), sem("bd_zero"), sem("bd_ready")
        fold_done, fold_out = sem("fold_done"), sem("fold_out")
        ln_ready, sd_ready, xn_ready, xt_done, xt_ready = (
            sem("ln_ready"), sem("sd_ready"), sem("xn_ready"), sem("xt_done"), sem("xt_ready"))
        dchain = sem("dchain")
        qp_done, qh_ready, ql_ready = sem("qp_done"), sem("qh_ready"), sem("ql_ready")
        xc_done = sem("xc_done")
        whi, wlo = sem("whi"), sem("wlo")
        chi, c1lo, c1lo8, crlo = sem("chi"), sem("c1lo"), sem("c1lo8"), sem("crlo")
        crlo_v = sem("crlo_v")
        vp_done, vp_out = sem("vp_done"), sem("vp_out")
        kp_done, khi, klo = sem("kp_done"), sem("khi"), sem("klo")
        pr_done, pr_max = sem("pr_done"), sem("pr_max")
        dg_ready, mb_done, mb_ready = sem("dg_ready"), sem("mb_done"), sem("mb_ready")
        st_done, mid_ready, e_ready, pv_done = sem("st_done"), sem("mid_ready"), sem("e_ready"), sem("pv_done")
        rden_ready = sem("rden_ready")
        summed = sem("summed")
        quad_done = sem("quad_done")
        den_out, pv_out, db_done, ot_ready = sem("den_out"), sem("pv_out"), sem("db_done"), sem("ot_ready")
        xo_done, xb_ready = sem("xo_done"), sem("xb_ready")
        kb_done, k2_ready = sem("kb_done"), sem("k2_ready")
        qk_done, qk_ready, v2_done, v2_ready = sem("qk_done"), sem("qk_ready"), sem("v2_done"), sem("v2_ready")
        s2_done, nb2_ready, p2_ready = sem("s2_done"), sem("nb2_ready"), sem("p2_ready")
        q2_ready, q2m_zero, q2m_ready, mask_ready = sem("q2_ready"), sem("q2m_zero"), sem("q2m_ready"), sem("mask_ready")
        rdx_ready, rt_done, rt_ready = sem("rdx_ready"), sem("rt_done"), sem("rt_ready")
        tp_done, tpa, tpd = sem("tp_done"), sem("tpa"), sem("tpd")
        y2_done, y2_ready, o2_done = sem("y2_done"), sem("y2_ready"), sem("o2_done")
        lg_done, ex_ready, ng_ready, cw_ready = sem("lg_done"), sem("ex_ready"), sem("ng_ready"), sem("cw_ready")
        gu_done, sg_ready, hid_ready, yd_done, acc_ready = (
            sem("gu_done"), sem("sg_ready"), sem("hid_ready"), sem("yd_done"), sem("acc_ready"))
        xh_ready, xl_ready, xt1_ready = sem("xh_ready"), sem("xl_ready"), sem("xt1_ready")
        guh, gul, wdh, wdl = sem("guh"), sem("gul"), sem("wdh"), sem("wdl")

        block = stack.enter_context(nc.Block())

        st_at, st_free = {}, []

        def takes(what, release, count):
            st_at[what] = len(st_free)
            st_free.append((release, count))

        def shifted_to(n):
            return n + 1 - sum(m <= n for m in DIRECT)

        for g in range(len(VG)):
            takes(("values", 0, g), vp_out, g + 1)
        for i in range(10):
            takes(("fold", i), fold_out, i + 1)
        for n in range(PAIRS * JT):
            takes(("scores", n), *((e_ready, n + 1) if n in DIRECT else (mid_ready, shifted_to(n))))
            if values_at(n) is not None:
                takes(("values", 1, values_at(n)), vp_out, len(VG) + values_at(n) + 1)

        def st_bank(*what):
            return ST[st_at[what] % 3]

        def key_cols(p, h, rows, lo, hi):
            if lo >= N_CTX:
                return ks8[rows, p % 2, h, lo - N_CTX:hi - N_CTX]
            return ks[rows, h, lo:hi]

        QP = (PV, DEN)

        def of_head(q, i, h):
            return q[:, 4 * i:4 * i + 4, :].rearrange("p (a two) t -> p a two t", two=2)[:, :, h, :]

        def place_free(engine, n):
            m = n - RING
            if m in SUMMED:
                engine.wait_ge(pv_done, m + 1)
                engine.wait_ge(summed, summed_to(m))
            elif m >= 0:
                engine.wait_ge(quad_done, PE_QUADS.index(m % JT // 4) + 1)

        def summed_to(n):
            return sum(m <= n for m in SUMMED)

        ALL = slice(0, P)
        LOOK_ORDER = [(c, k) for j in sorted(LOOKS_AT) for c, k in LOOKS_AT[j]]

        def looked(p, c, k):
            return 4 * NCH * p + (4 * c + k if p == 0 else LOOK_ORDER.index((c, k)))


        def expert(e):
            return (base_wgu, base_wd) if e == 0 else (exp_wgu[e - 1], exp_wd[e - 1])

        def GU(n):
            return bank[n % 6]

        def Y(e, tt):
            return bank[6 + (e + (tt if e == E else 0)) % 2][:, tt * C:(tt + 1) * C]

        def gate_up_pieces(e, main, tail):
            raw = wgu[e % NSLOT]
            return ((raw[:, :, 0:2 * P], main[e % 2][:, :, 0:2 * P]),
                    (raw[:, :, 2 * P:IFULL * P], main[e % 2][:, :, 2 * P:IFULL * P]),
                    (raw[:, :, IFULL * P:I], tail[e % 2][:, :, :]))

        def pt_dst(i):
            return pt[:, :, :].rearrange("p h k -> p (h k)")[:, 512 * i:512 * i + 512]

        @block.sync
        def _(sp):
            sp.dma_start(xs[:, :, :], x.rearrange("(t p) c -> p t c", p=P)).then_inc(x_in, 16)
            sp.dma_start(wq[:, :, :], w_q.rearrange("(a p) n -> p a n", p=P)).then_inc(qw_in, 16)

            def context_in(i):
                a, b = RAW[i]
                for part in range(2):
                    rows = P if part == 0 else REST
                    sp.dma_start(raw[0:rows, a:b, part, :],
                                 ctxT[part * P:part * P + rows, a * CHUNK:b * CHUNK].rearrange(
                                     "p (c k) -> p c k", k=CHUNK)).then_inc(raw_in[i], 16)

            def key_value_weights(i, w, arrived):
                sp.dma_start(wraw[:, 2 * i, :], w[0:P, :]).then_inc(arrived, 16)
                for half in range(2):
                    sp.dma_start(wraw[64 * half:64 * half + REST, 2 * i + 1, :], w[P:D_CTX, :]).then_inc(arrived, 16)

            key_value_weights(0, w_k, kw_in)
            context_in(0)
            key_value_weights(1, w_v, vw_in)
            context_in(1)
            context_in(2)
            sp.dma_start(wimg[:, :, :], w_img.rearrange("(a p) n -> p a n", p=P)).then_inc(cw_in, 16)
            sp.dma_start(wprm[:, :, :], w_prompt.rearrange("(a p) n -> p a n", p=P)).then_inc(cw_in, 16)
            sp.dma_start(prm[:, :, :], promptT.rearrange("(a p) n -> p a n", p=P)).then_inc(cw_in, 16)
            context_in(3)
            context_in(4)
            for h in range(2):
                rows = slice(AL * h, AL * h + AL)
                if h == 0:
                    sp.wait_ge(bd_zero, 3)
                for n, bd in ((0, bdq), (1, bdk)):
                    sp.dma_start(bd[rows, h, 0:8], ups[2 * n]).then_inc(up_in, 16)
                    sp.dma_start(bd[rows, h, 8:16], ups[2 * n + 1]).then_inc(up_in, 16)
                sp.dma_start(bdv[rows, h, :], ups[4]).then_inc(up_in, 16)
            for n in range(3):
                sp.dma_start(wdt_s[:, n, :, :], wdT[n].rearrange("(k p) c -> p k c", p=P)).then_inc(wdt_in, 16)
            sp.dma_start(bb[:, :], b_out.rearrange("(a c) -> a c", a=1).broadcast_to([P, C])).then_inc(misc_in, 16)
            sp.dma_start(gatew[:, :, :], gate_w.rearrange("(a p) e -> p a e", p=P)).then_inc(misc_in, 16)
            sp.wait_ge(vp_out, 2 * len(VG))
            sp.dma_start(wout[:, :, :], w_out.rearrange("(a p) c -> p a c", p=P)).then_inc(wout_in, 16)
            for e in range(E + 1):
                s = e % NSLOT
                if e == 0:
                    sp.wait_ge(pv_done, PAIRS * JT)
                    sp.dma_start(tab[:, :], rope).then_inc(tab_in, 16)
                if e >= NSLOT:
                    sp.wait_ge(gul, 3 * (e - NSLOT + 1))
                    sp.wait_ge(wdl, e - NSLOT + 1)
                gu, dn = expert(e)
                sp.dma_start(wgu[s][:, :, :].rearrange("p (a j) n -> p a (j n)", a=CC),
                             gu.rearrange("(a p) n -> p a n", p=P)).then_inc(ffn_in[s], 16)
                sp.dma_start(wd[s][:, 0:IFULL, :], dn[0:IFULL * P, :].rearrange("(a p) c -> p a c", p=P)).then_inc(ffn_in[s], 16)
                for h in range(2):
                    sp.dma_start(wd[s][h * ITAIL:(h + 1) * ITAIL, IFULL, :], dn[IFULL * P:I, :]).then_inc(ffn_in[s], 16)
            for tt in range(TT):
                sp.wait_ge(acc_ready, E * TT + tt + 1)
                sp.dma_start(out[tt * P:(tt + 1) * P, :], acc[:, tt, :]).then_inc(out_done, 16)
            sp.wait_ge(out_done, 16 * TT)

        @block.gpsimd
        def _(pool):
            pool.memset(ident[:], 0.0).then_inc(const_ready, 1)
            pool.memset(mask[:], 0.0).then_inc(const_ready, 1)
            pool.memset(ones[:], 1.0).then_inc(const_ready, 1)
            pool.memset(epst[:], EPS).then_inc(const_ready, 1)
            for e in range(E):
                pool.memset(iota8[:, e:e + 1], float(e)).then_inc(const_ready, 1)
            pool.wait_ge(const_ready, 4 + E)
            pool.affine_select(out=ident[:, :], in_=ident[:, :], compare_op=ALU.not_equal, fill=1.0, base=0,
                               pattern=[[-1, P]], channel_multiplier=1).then_inc(const_ready, 1)
            pool.affine_select(out=mask[:, P:2 * P], in_=mask[:, P:2 * P], compare_op=ALU.is_ge, fill=NEG, base=0,
                               pattern=[[-1, P]], channel_multiplier=1).then_inc(const_ready, 1)
            for c in range(NCH - 1):
                cols = slice(c * CHUNK, (c + 1) * CHUNK)
                pool.wait_ge(chi, 2 * c + 1)
                if c >= 2:
                    pool.wait_ge(crlo, c - 1)
                pool.tensor_tensor(c1l[:, cols], raw[:, c, 0, :], c1h[:, cols].bitcast(F32),
                                   ALU.subtract).then_inc(c1lo, 1)
                if c:
                    pool.wait_ge(chi, 2 * c + 2)
                    pool.wait_ge(c1lo, c + 1)
                    pool.tensor_tensor(cr[REST:P, cols], raw[0:REST, c, 1, :], cr[0:REST, cols].bitcast(F32),
                                       ALU.subtract).then_inc(crlo, 1)
            for n in SUMMED:
                p, jt = divmod(n, JT)
                acc_e = esum[0:rows_of(jt), p % 2, :]
                if jt == 0:
                    continue
                pool.wait_ge(e_ready, n + 1)
                if jt == 1:
                    if p:
                        pool.wait_ge(summed, summed_to(n) - 2)
                    if p >= 2:
                        pool.wait_ge(db_done, p - 1)
                    pool.tensor_tensor(acc_e, ering[:, (n - 1) % RING, :], ering[:, n % RING, :], ALU.add).then_inc(summed, 2)
                else:
                    pool.wait_ge(summed, summed_to(n) - 1)
                    pool.tensor_tensor(acc_e, acc_e, ering[0:rows_of(jt), n % RING, :], ALU.add).then_inc(summed, 1)
            pool.wait_ge(pv_done, PAIRS * JT)
            pool.memset(v2[:, :, C:WPAD], 0.0).then_inc(wc_zero, 1)
            pool.memset(wc[:, :, :], 0.0).then_inc(wc_zero, 1)
            pool.wait_ge(quad_done, len(PE_QUADS))
            pool.wait_ge(summed, len(SUMMED))
            for r in range(4):
                pool.memset(q2m[:, r, :, :], 0.0).then_inc(q2m_zero, 1)
            pool.wait_ge(wc_zero, 2)
            for r in range(4):
                pool.dma_start(wc[32 * r:32 * r + AD, :, :],
                               w_c.rearrange("(g r d) c -> r d g c", g=AG, r=4)[r]).then_inc(wc_in, 16)
            for e in range(E + 1):
                pool.wait_ge(wdh, e + 1)
                if e >= 2:
                    pool.wait_ge(yd_done, TT * (e - 1))
                pool.tensor_tensor(wd_l[e % 2][:, :, :], wd[e % NSLOT][:, :, :], wd_h[e % 2][:, :, :].bitcast(F32),
                                   ALU.subtract).then_inc(wdl, 1)

        CONST = 6 + E

        @block.scalar
        def _(act):
            def ln_root(n):
                for tt in range(TT):
                    act.wait_ge(ln_ready, TT * n + tt + 1)
                    act.activation(sd[:, tt:tt + 1], ag[:, tt, 1:2], ACT.Sqrt, bias=epst[:, 0:1]).then_inc(sd_ready, 1)

            def load_table(function):
                act.activation(spare[:, :], epst[:, :], function)

            def xt_copy(n, ct, xnT):
                act.wait_ge(xt_done, CC * n + ct + 1)
                act.activation(xnT[:, ct, :], XT[ct][:, 0:T], ACT.Copy).then_inc(xt_ready, 1)

            act.wait_ge(const_ready, CONST)
            ln_root(0)
            xt_copy(0, 0, xnT0)
            xt_copy(0, 1, xnT0)

            def weights_hi(i):
                act.wait_ge((kw_in, vw_in)[i], 48)
                for k, w in enumerate(((wk1h, wkrh), (wv1h, wvrh))[i]):
                    act.activation(w[:, :], wraw[:, 2 * i + k, :], ACT.Copy).then_inc(whi, 1)

            def queries_hi(i):
                act.wait_ge(qp_done, i + 1)
                for h in range(2):
                    for half in range(2):
                        rows, to = slice(64 * h, 64 * h + 64), slice(64 * half, 64 * half + 64)
                        act.activation(of_head(qh, i, h)[to], QP[i][rows, :].rearrange("p (a t) -> p a t", a=2),
                                       ACT.Copy).then_inc(qh_ready, 1)

            def context_hi(c):
                cols = slice(c * CHUNK, c * CHUNK + keys_of(c))
                if c < NCH - 1:
                    act.wait_ge(raw_in[[a <= c < b for a, b in RAW].index(True)], 32)
                    first, rest = raw[:, c, 0, :], raw[0:REST, c, 1, :]
                else:
                    act.wait_ge(xc_done, 1)
                    first, rest = PV[:, 0:keys_of(c)], DEN[0:REST, 0:keys_of(c)]
                act.activation(c1h[:, cols], first, ACT.Copy).then_inc(chi, 1)
                act.activation(cr[0:REST, cols], rest, ACT.Copy).then_inc(chi, 1)

            weights_hi(0)
            context_hi(0)
            weights_hi(1)

            def values_out(half, g):
                a, b = VG[g]
                act.wait_ge(vp_done, half * len(VG) + g + 1)
                if half == 0:
                    c = min(a // 4, NCH - 2)
                    act.wait_ge(*((crlo, c) if c else (crlo_v, 1)))
                    act.wait_ge(c1lo, c + 1)
                ps = st_bank("values", half, g)
                r = rows_of(b - 1)
                act.activation(v[0:r, a:b, :], ps[0:r, 0:256 * (b - a)].rearrange("p (j d) -> p j d", d=4 * XD),
                               ACT.Copy).then_inc(vp_out, 1)

            def keys_hi(p, c, h):
                w = keys_of(c)
                rows = slice(64 * h, 64 * h + 64)
                act.wait_ge(kp_done, place(p, c) + 1)
                act.activation(key_cols(p, h, rows, c * CHUNK, c * CHUNK + w), PJ[rows, 0:w], ACT.Copy).then_inc(khi, 1)

            def mb_copy(p):
                act.wait_ge(mb_done, p + 1)
                if p >= 2:
                    act.wait_ge(mid_ready, shifted_to(JT * (p - 1) - 1))
                    act.wait_ge(st_done, JT * (p - 1))
                act.activation(mb[:, p % 2, :], PR[0][:, :], ACT.Copy).then_inc(mb_ready, 1)

            for c in range(NCH):
                if c + 1 < NCH:
                    context_hi(c + 1)
                if c == 2:
                    queries_hi(1)
                keys_hi(0, c, 0)
                keys_hi(0, c, 1)
                if c == 0:
                    queries_hi(0)
                for g in range(2 * c, min(2 * c + 2, len(VG))):
                    values_out(0, g)
            for i in range(5):
                w, half = divmod(i, 2)
                act.wait_ge(fold_done, i + 1)
                act.activation(wdt_s[:, w, 2 * half:2 * half + 2, :], st_bank("fold", i)[:, :].rearrange("p (g c) -> p g c", g=2),
                               ACT.Copy).then_inc(fold_out, 1)
            for i, dst in enumerate((weff["q"][:, 0, :], weff["q"][:, 1, :], weff["k"][:, 0, :], weff["k"][:, 1, :],
                                     weff["v"][:, :, :].rearrange("p a c -> p (a c)"))):
                act.wait_ge(fold_done, 5 + i + 1)
                act.activation(dst, st_bank("fold", 5 + i)[:, :], ACT.Copy).then_inc(fold_out, 1)
            mb_copy(0)

            def exp_tile(n):
                r = rows_of(n % JT)
                e = ering[0:r, n % RING, :]
                if n in DIRECT:
                    act.wait_ge(st_done, n + 1)
                    place_free(act, n)
                    act.activation(e, st_bank("scores", n)[0:r, :], ACT.Exp, scale=XD ** -0.5).then_inc(e_ready, 1)
                else:
                    act.wait_ge(mid_ready, shifted_to(n))
                    act.activation(e, e, ACT.Exp, scale=XD ** -0.5).then_inc(e_ready, 1)

            def sums_out(p):
                act.wait_ge(pv_done, JT * (p + 1))
                if p:
                    act.wait_ge(ot_ready, p)
                act.activation(pvs[:, :], PV[:, 0:T], ACT.Copy).then_inc(pv_out, 1)

            for n in range(PAIRS * JT):
                p, j = divmod(n, JT)
                ahead = p + 1 < PAIRS
                if j == 0 and p:
                    mb_copy(p)
                if j == 0 and ahead:
                    keys_hi(p + 1, NCH - 1, 0)
                    keys_hi(p + 1, NCH - 1, 1)
                if ahead and j and j % 4 == 0:
                    keys_hi(p + 1, j // 4 - 1, 0)
                exp_tile(n)
                if ahead and j and j % 4 == 0:
                    keys_hi(p + 1, j // 4 - 1, 1)
                if values_at(n) is not None:
                    values_out(1, values_at(n))
                if j == LAG - 1 and p:
                    sums_out(p - 1)
            sums_out(PAIRS - 1)

            def gate_up_hi(e, k):
                if k == 0:
                    act.wait_ge(ffn_in[e % NSLOT], 64 * (e // NSLOT + 1))
                    if e >= 2:
                        act.wait_ge(gu_done, ICH * (e - 1))
                raw, part = gate_up_pieces(e, gu_h, gt_h)[k]
                act.activation(part, raw, ACT.Copy).then_inc(guh, 1)

            load_table(ACT.Sqrt)
            act.wait_ge(pv_done, PAIRS * JT)
            for m, src in ((mask4[:, :, :], mask[:, P:2 * P].rearrange("p (a k) -> p a k", a=1).broadcast_to([P, 4, P])),
                           (mask2[:, :, :], mask[:, :].rearrange("p (a k) -> p a k", a=1).broadcast_to([P, 2, 2 * P])),
                           (identr[:, :], ident[:, :])):
                act.activation(m, src, ACT.Copy).then_inc(mask_ready, 1)
            ln_root(1)
            xt_copy(1, 0, xnT)
            load_table(ACT.Exp)
            for i in range(2):
                act.wait_ge(kb_done, i + 1)
                act.activation(k2[:, 2 * i:2 * i + 2, :], bank[5 + i][:, :].rearrange("p (g t) -> p g t", g=2),
                               ACT.Copy).then_inc(k2_ready, 1)
            act.wait_ge(qk_ready, 4)
            act.wait_ge(q2m_zero, 4)
            for r in (1, 3):
                act.activation(q2m[32 * r:32 * r + 32, r, :, :], q2[32 * r:32 * r + 32, :, :], ACT.Copy).then_inc(q2m_ready, 1)
            act.wait_ge(v2_done, 1)
            act.activation(v2[:, :, 0:C], bank[4][:, :].rearrange("p (t c) -> p t c", t=TT), ACT.Copy).then_inc(v2_ready, 1)
            for b in range(12):
                heads, w = heads_of(b)
                act.wait_ge(nb2_ready, b + 1)
                for i in range(len(heads)):
                    ins = act.activation(s2[:, b // 4, (b % 4) * 512 + i * w:(b % 4) * 512 + (i + 1) * w],
                                         bank[S2_BANK[b]][:, i * w:(i + 1) * w], ACT.Exp,
                                         bias=nb2[:, first_of(b) + i:first_of(b) + i + 1], scale=AD ** -0.5,
                                         accum_out=dn2[:, first_of(b) + i:first_of(b) + i + 1])
                ins.then_inc(p2_ready, 1)
            for i in TP_BY_ACT:
                act.wait_ge(tp_done, i + 1)
                act.activation(pt_dst(i), bank[TP_BANK[i]][:, :], ACT.Copy).then_inc(tpa, 1)
            gate_up_hi(0, 0)
            gate_up_hi(0, 1)
            for half in range(2):
                act.wait_ge(rt_done, half + 1)
                act.activation(rt2[:, 2 * half:2 * half + 2, :], bank[2 + half][:, :].rearrange("p (g t) -> p g t", g=2),
                               ACT.Copy).then_inc(rt_ready, 1)

            load_table(ACT.Sqrt)
            gate_up_hi(0, 2)

            ln_root(2)
            for ct in range(CC):
                act.wait_ge(xt_done, 2 * CC + ct + 1)
                act.activation(xh[:, ct, :], XT[ct][:, 0:T], ACT.Copy).then_inc(xh_ready, 1)
            load_table(ACT.Silu)
            for ct in range(CC):
                act.wait_ge(xl_ready, ct + 1)
                xt_copy(2, ct, xnT)

            for e in range(E + 1):
                for i in range(ICH):
                    n = e * ICH + i
                    act.wait_ge(gu_done, n + 1)
                    if n >= 2:
                        act.wait_ge(hid_ready, n - 1)
                    rows, to = (slice(0, P), slice(0, P)) if i < IFULL else (slice(0, ITAIL), slice(ITAIL, P))
                    act.activation(sg[to, n % 2, :], GU(n)[rows, 0:T], ACT.Silu).then_inc(sg_ready, 1)
                    if i < 3 and e < E:
                        gate_up_hi(e + 1, i)
                    if i == (3 if e < E else 0):
                        if e >= 2:
                            act.wait_ge(yd_done, TT * (e - 1))
                        act.activation(wd_h[e % 2][:, :, :], wd[e % NSLOT][:, :, :], ACT.Copy).then_inc(wdh, 1)
                    if e == 1 and i == 4:
                        act.wait_ge(ng_ready, 1)
                        for tt in range(TT):
                            act.activation(ex[:, tt, :], lg[:, tt, :], ACT.Exp, bias=ng[:, tt:tt + 1]).then_inc(ex_ready, 1)

        @block.vector
        def _(dve):
            chain = [0]

            def link(ins):
                chain[0] += 1
                ins.then_inc(dchain, 1)
                dve.wait_ge(dchain, chain[0])

            def layernorm(n, src, xn, added=None, added_done=None):
                for tt in range(TT):
                    if added:
                        dve.wait_ge(added_done, tt + 1)
                        link(dve.tensor_tensor(src[:, tt, :], added[tt][:, 0:C], src[:, tt, :], ALU.add))
                    link(dve.bn_stats(st[:, tt, :], src[:, tt, :]))
                    dve.bn_aggr(ag[:, tt, :], st[:, tt, :]).then_inc(ln_ready, 1)
                for tt in range(TT):
                    dve.wait_ge(sd_ready, TT * n + tt + 1)
                    link(dve.reciprocal(rs[:, tt:tt + 1], sd[:, tt:tt + 1]))
                    dve.tensor_scalar(xn[:, tt, :], src[:, tt, :], ag[:, tt, 0:1], rs[:, tt:tt + 1],
                                      ALU.subtract, ALU.mult).then_inc(xn_ready, 1)

            for bd in (bdq, bdk, bdv):
                dve.memset(bd[:], 0.0).then_inc(bd_zero, 1)
            link(dve.memset(gsel[:, :], 0.0))
            for r in range(4):
                dve.memset(gsel[32 * r:32 * r + 1, :], 1.0).then_inc(gsel_ready, 1)
            dve.wait_ge(x_in, 16)
            layernorm(0, xs, xn0)
            def weights_lo(i):
                for k, (w, h) in enumerate((((wk1l, wk1h), (wkrl, wkrh)), ((wv1l, wv1h), (wvrl, wvrh)))[i]):
                    dve.wait_ge(whi, 2 * i + k + 1)
                    dve.tensor_tensor(w[:, :], wraw[:, 2 * i + k, :], h[:, :].bitcast(F32), ALU.subtract).then_inc(wlo, 1)

            def queries_lo(i, k):
                h, half = divmod(k, 2)
                rows, to = slice(64 * h, 64 * h + 64), slice(64 * half, 64 * half + 64)
                dve.wait_ge(qh_ready, 4 * i + 4)
                dve.tensor_tensor(of_head(ql, i, h)[to], QP[i][rows, :].rearrange("p (a t) -> p a t", a=2),
                                  of_head(qh, i, h)[rows].bitcast(F32), ALU.subtract).then_inc(ql_ready, 1)

            def context_lo(c):
                w = keys_of(c)
                cols = slice(c * CHUNK, c * CHUNK + w)
                dve.wait_ge(chi, 2 * c + 2)
                rest = raw[0:REST, c, 1, :] if c < NCH - 1 else DEN[0:REST, 0:w]
                dve.tensor_tensor(cr[REST:P, cols], rest, cr[0:REST, cols].bitcast(F32), ALU.subtract).then_inc(crlo_v, 1)
                if c == NCH - 1:
                    dve.tensor_tensor(c1l[:, cols], PV[:, 0:w], c1h[:, cols].bitcast(F32), ALU.subtract).then_inc(c1lo8, 1)

            weights_lo(0)
            context_lo(0)
            weights_lo(1)

            def keys_lo(p, c, h):
                w = keys_of(c)
                rows, other = slice(64 * h, 64 * h + 64), slice(64 - 64 * h, 128 - 64 * h)
                lo, hi = c * CHUNK, c * CHUNK + w
                dve.wait_ge(khi, 2 * place(p, c) + h + 1)
                dve.tensor_tensor(key_cols(p, h, other, lo, hi), PJ[rows, 0:w],
                                  key_cols(p, h, rows, lo, hi).bitcast(F32), ALU.subtract).then_inc(klo, 1)

            def look_max(p, c, k):
                dve.wait_ge(pr_done, looked(p, c, k) + 1)
                dve.tensor_reduce(mx[:, k, c:c + 1], PR[k % 2][:, 0:keys_of(c)], AX_X, ALU.max).then_inc(pr_max, 1)

            def pair_max(p):
                dve.wait_ge(pr_max, 4 * NCH * (p + 1))
                link(dve.tensor_reduce(m4[:, p % 2, :], mx[:, :, :], AX_X, ALU.max))
                if p:
                    dve.wait_ge(mb_done, p)
                for k in range(4):
                    dve.tensor_scalar(diag[:, k * P:(k + 1) * P], ident[:, :], m4[:, p % 2, k:k + 1], None,
                                      ALU.mult).then_inc(dg_ready, 1)

            def up_projections():
                dve.wait_ge(const_ready, CONST)
                dve.wait_ge(up_in, 16 * 10)
                for bd in (bdq, bdk):
                    for k in range(2):
                        dst = bd[:, :, 16:24].rearrange("p h (m two) -> p h m two", two=2)
                        src = bd[:, :, 8:16].rearrange("p h (m two) -> p h m two", two=2)
                        dve.tensor_copy(dst[:, :, :, k], src[:, :, :, 1 - k]).then_inc(bd_ready, 1)
                dve.tensor_copy(onesr[:, :], ones[:, :]).then_inc(gsel_ready, 1)
                dve.tensor_scalar(negr[:, :], ones[:, :], -1.0 / P, None, ALU.mult).then_inc(gsel_ready, 1)

            for c in range(NCH):
                if c + 1 == NCH - 1:
                    context_lo(c + 1)
                if 1 <= c < 3:
                    for k in range(2 * c - 2, 2 * c):
                        queries_lo(0, k)
                elif 3 <= c < 7:
                    queries_lo(1, c - 3)
                    if c == 6:
                        up_projections()
                if c >= 1:
                    look_max(0, c - 1, 0)
                keys_lo(0, c, 0)
                keys_lo(0, c, 1)
                if c >= 1:
                    for k in range(1, 4):
                        look_max(0, c - 1, k)
            for k in range(4):
                look_max(0, NCH - 1, k)
            pair_max(0)
            dve.wait_ge(misc_in, 32)
            dve.wait_ge(xn_ready, TT)
            for tt in range(TT):
                link(dve.tensor_tensor(xs[:, tt, :], xs[:, tt, :], bb[:, :], ALU.add))

            def sub_tile(n):
                p, jt = divmod(n, JT)
                r = rows_of(jt)
                dve.wait_ge(st_done, n + 1)
                if jt == 0:
                    dve.wait_ge(mb_ready, p + 1)
                if n == 0:
                    dve.wait_ge(fold_done, 10)
                place_free(dve, n)
                dve.tensor_tensor(ering[0:r, n % RING, :], st_bank("scores", n)[0:r, :], mb[0:r, p % 2, :].bitcast(F32),
                                  ALU.subtract).then_inc(mid_ready, 1)

            def den_copy():
                dve.wait_ge(quad_done, len(PE_QUADS))
                dve.tensor_copy(den[:, :], DEN[:, :]).then_inc(den_out, 1)

            def invert(p, part):
                if part == 0:
                    dve.wait_ge(db_done, p + 1)
                q = slice(part * T // 4, (part + 1) * T // 4)
                ins = dve.reciprocal(rden[:, q], DEN[:, q])
                if part < 3:
                    ins.then_inc(rden_ready, 1)
                else:
                    link(ins)
                    dve.wait_ge(rden_ready, 3 * (p + 1))
                    dve.wait_ge(pv_out, p + 1)
                    dve.tensor_tensor(ot[:, p, :], pvs[:, :], rden[:, :], ALU.mult).then_inc(ot_ready, 1)

            def normalise_last():
                p = PAIRS - 1
                dve.wait_ge(db_done, p + 1)
                for tt in range(TT):
                    q = slice(tt * P, (tt + 1) * P)
                    link(dve.reciprocal(rden[:, q], DEN[:, q]))
                    if tt == 0:
                        dve.wait_ge(pv_out, p + 1)
                    dve.tensor_tensor(ot[:, p, q], pvs[:, q], rden[:, q], ALU.mult).then_inc(ot_ready, 1)

            for n in range(PAIRS * JT):
                p, j = divmod(n, JT)
                if n not in DIRECT:
                    sub_tile(n)
                if p + 1 < PAIRS:
                    if j in (1, 2):
                        keys_lo(p + 1, NCH - 1, j - 1)
                    if j and j % 4 == 0:
                        keys_lo(p + 1, j // 4 - 1, 0)
                    if j == 32 or (j > 4 and j % 4 == 1 and j < 32):
                        keys_lo(p + 1, (j - 1) // 4 - 1 if j < 32 else NCH - 2, 1)
                    for c, k in LOOKS_AT.get(j, ()):
                        look_max(p + 1, c, k)
                if p and LAG + 2 <= j < LAG + 6:
                    invert(p - 1, j - LAG - 2)
                if j == JT - 1 and p + 1 < PAIRS:
                    pair_max(p + 1)
            den_copy()
            normalise_last()

            layernorm(1, xs, xn, added=(PJ, PV), added_done=xo_done)
            dve.wait_ge(xt_done, 2 * CC)
            dve.tensor_copy(xnT[:, 1, :], XT[1][:, 0:T]).then_inc(xt1_ready, 1)
            dve.wait_ge(tab_in, 16)
            for i in range(4):
                dve.wait_ge(qk_done, i + 1)
                table = tab[:, 0:T].rearrange("p (g t) -> p g t", g=1).broadcast_to([P, 2, T])
                dve.tensor_tensor((kb if i < 2 else q2)[:, 2 * (i % 2):2 * (i % 2) + 2, :],
                                  bank[i][:, :].rearrange("p (g t) -> p g t", g=2), table, ALU.mult).then_inc(qk_ready, 1)
            dve.wait_ge(qk_ready, 4)
            dve.wait_ge(q2m_zero, 4)
            for r in (0, 2):
                dve.tensor_copy(q2m[32 * r:32 * r + 32, r, :, :], q2[32 * r:32 * r + 32, :, :]).then_inc(q2_ready, 1)

            def gate_up_lo(e, k):
                dve.wait_ge(guh, 3 * e + k + 1)
                if k == 0 and e >= 2:
                    dve.wait_ge(gu_done, ICH * (e - 1))
                raw, part = gate_up_pieces(e, gu_l, gt_l)[k]
                dve.tensor_tensor(part, raw, gate_up_pieces(e, gu_h, gt_h)[k][1].bitcast(F32),
                                  ALU.subtract).then_inc(gul, 1)

            def bank_maxima(b):
                heads, w = heads_of(b)
                o, n = first_of(b), len(heads)
                dve.wait_ge(s2_done, b + 1)
                link(dve.tensor_reduce(mx2[:, o:o + n], bank[S2_BANK[b]][:, :].rearrange("p (h k) -> p h k", k=w), AX_X, ALU.max))
                dve.tensor_scalar(nb2[:, o:o + n], mx2[:, o:o + n], -AD ** -0.5, None, ALU.mult).then_inc(nb2_ready, 1)

            def transposed_out(i):
                dve.wait_ge(tp_done, i + 1)
                dve.tensor_copy(pt_dst(i), bank[TP_BANK[i]][:, :]).then_inc(tpd, 1)

            def reciprocals(rd):
                dve.wait_ge(p2_ready, 4 * rd + 4)
                o, n, qt, g0 = ((0, 4, 0, 0), (16, 2, 1, 0), (24, 2, 1, 2))[rd]
                link(dve.reciprocal(rd2[:, o:o + 4 * n], dn2[:, o:o + 4 * n]))
                for g in range(n):
                    src = rd2[:, o:o + 4 * n].rearrange("p (r g a) -> p g r a", r=4, a=1)[:, g, :, :].broadcast_to([P, 4, 32])
                    dve.tensor_copy(rdx[:, qt, g0 + g, :, :], src).then_inc(rdx_ready, 1)

            for b in range(12):
                bank_maxima(b)
            for i in range(12):
                if i not in TP_BY_ACT:
                    transposed_out(i)
            for rd in range(3):
                reciprocals(rd)
            gate_up_lo(0, 0)
            for half in range(2):
                dve.wait_ge(y2_done, half + 1)
                dve.wait_ge(rt_ready, half + 1)
                dve.tensor_tensor(y2[:, 2 * half:2 * half + 2, :], bank[half][:, :].rearrange("p (g t) -> p g t", g=2),
                                  rt2[:, 2 * half:2 * half + 2, :], ALU.mult).then_inc(y2_ready, 1)
                if half == 0:
                    gate_up_lo(0, 1)
            layernorm(2, xs, xn, added=(bank[6], bank[7]), added_done=o2_done)
            gate_up_lo(0, 2)
            dve.wait_ge(xh_ready, 1)
            dve.tensor_tensor(xl[:, 0, :], XT[0][:, 0:T], xh[:, 0, :].bitcast(F32), ALU.subtract).then_inc(xl_ready, 1)
            dve.wait_ge(xh_ready, 2)
            dve.tensor_tensor(xl[:, 1, :], XT[1][:, 0:T], xh[:, 1, :].bitcast(F32), ALU.subtract).then_inc(xl_ready, 1)

            def router_logits():
                dve.wait_ge(lg_done, 1)
                link(dve.tensor_copy(lg[:, :, :], bank[7][:, 0:TT * E].rearrange("p (t e) -> p t e", t=TT)))
                for tt in range(TT):
                    link(dve.max(t8[:, tt, :], lg[:, tt, :]))
                dve.tensor_scalar(ng[:, :], t8[:, :, 0], -1.0, None, ALU.mult).then_inc(ng_ready, 1)

            def router_weights():
                dve.wait_ge(ex_ready, TT)
                for tt in range(TT):
                    link(dve.max(e8[:, tt, :], ex[:, tt, :]))
                for tt in range(TT):
                    link(dve.max_index(i8[:, tt, :], e8[:, tt, :], ex[:, tt, :]))
                link(dve.tensor_copy(fi[:, :, :], i8[:, :, :]))
                for tt in range(TT):
                    link(dve.tensor_scalar(sl[:, tt, :], iota8[:, :], fi[:, tt, 0:1], None, ALU.is_equal))
                    link(dve.scalar_tensor_tensor(out=sl[:, tt, :], in0=iota8[:, :], scalar=fi[:, tt, 1:2],
                                                  in1=sl[:, tt, :], op0=ALU.is_equal, op1=ALU.add))
                link(dve.tensor_tensor(w2[:, :], e8[:, :, 0], e8[:, :, 1], ALU.add))
                link(dve.reciprocal(rw[:, :], w2[:, :]))
                for tt in range(TT):
                    link(dve.scalar_tensor_tensor(out=cw[:, tt, :], in0=ex[:, tt, :], scalar=rw[:, tt:tt + 1],
                                                  in1=sl[:, tt, :], op0=ALU.mult, op1=ALU.mult))

            def hidden(e, i):
                n = e * ICH + i
                dve.wait_ge(sg_ready, n + 1)
                if i == 0 and e >= 2:
                    dve.wait_ge(yd_done, TT * (e - 1))
                h = hid[:, n % 2, :]
                if i < IFULL:
                    link(dve.tensor_tensor(h, GU(n)[:, T:2 * T], sg[:, n % 2, :], ALU.mult))
                    link(dve.tensor_copy(hid_h[e % 2][:, i, :], h))
                    dve.tensor_tensor(hid_l[e % 2][:, i, :], h, hid_h[e % 2][:, i, :].bitcast(F32),
                                      ALU.subtract).then_inc(hid_ready, 1)
                else:
                    h, hi = h[0:ITAIL], hid_h[e % 2][0:ITAIL, i, :]
                    link(dve.tensor_tensor(h, GU(n)[ITAIL:P, 0:T], sg[ITAIL:P, n % 2, :], ALU.mult))
                    link(dve.tensor_copy(hi, h))
                    dve.tensor_tensor(hid_h[e % 2][ITAIL:P, i, :], h, hi.bitcast(F32), ALU.subtract).then_inc(hid_ready, 1)

            def add_expert(e):
                if e:
                    dve.wait_ge(acc_ready, TT * e)
                for tt in range(TT):
                    dve.wait_ge(yd_done, TT * e + (tt + 1 if e == E else TT))
                    y = Y(e, tt)
                    if e == 0:
                        dve.tensor_tensor(acc[:, tt, :], y, xs[:, tt, :], ALU.add).then_inc(acc_ready, 1)
                    else:
                        dve.scalar_tensor_tensor(out=acc[:, tt, :], in0=y, scalar=cw[:, tt, e - 1:e],
                                                 in1=acc[:, tt, :], op0=ALU.mult, op1=ALU.add).then_inc(acc_ready, 1)

            for e in range(E + 1):
                for i in range(ICH):
                    hidden(e, i)
                    if i < 3 and e < E:
                        gate_up_lo(e + 1, i)
                    if i == (3 if e < E else 0) and e >= 2:
                        add_expert(e - 2)
                    if e == 1 and i == 3:
                        router_logits()
                    if e == 2 and i == 2:
                        router_weights()
            add_expert(E - 1)
            add_expert(E)

        @block.tensor
        def _(pe):
            mm = pe.matmul

            def transposed(n, xn):
                for tt in range(TT):
                    pe.wait_ge(xn_ready, TT * n + tt + 1)
                    for ct in range(CC):
                        ins = pe.transpose(XT[ct][:, tt * P:(tt + 1) * P], xn[:, tt, ct * P:(ct + 1) * P], ident[:, :])
                        if tt == TT - 1:
                            ins.then_inc(xt_done, 1)

            pe.wait_ge(const_ready, CONST)
            transposed(0, xn0)
            pe.wait_ge(qw_in, 16)
            pe.wait_ge(xt_ready, CC)
            for p in range(PAIRS):
                for ct in range(CC):
                    ins = mm(QP[p // 2][:, (p % 2) * T:(p % 2 + 1) * T], wq[:, ct, p * P:(p + 1) * P], xnT0[:, ct, :],
                             start=(ct == 0), stop=(ct == CC - 1))
                if p % 2:
                    ins.then_inc(qp_done, 1)

            def last_context():
                pe.wait_ge(ql_ready, 8)
                pe.wait_ge(cw_in, 48)
                for ps, lo, n in ((PV, 0, P), (DEN, P, REST)):
                    for o, w, rhs, width in ((0, wprm, prm, N_PROMPT), (N_PROMPT, wimg, xnT0, T)):
                        for ct in range(CC):
                            ins = mm(ps[0:n, o:o + width], w[:, ct, lo:lo + n], rhs[:, ct, :],
                                     start=(ct == 0), stop=(ct == CC - 1))
                ins.then_inc(xc_done, 1)

            def st_wait(*what):
                i = st_at[what]
                if i >= 3:
                    pe.wait_ge(*st_free[i - 3])

            def values(half, g):
                a, b = VG[g]
                st_wait("values", half, g)
                ps = st_bank("values", half, g)
                cols = slice(half * 4 * XD, (half + 1) * 4 * XD)
                for jt in range(a, b):
                    r = rows_of(jt)
                    keys = slice(jt * P, jt * P + r)
                    o = ps[0:r, (jt - a) * 256:(jt - a) * 256 + 256]
                    terms = ((c1h, wv1h), (c1h, wv1l), (c1l, wv1h), (cr, wvrh), (cr, wvrl))
                    for t, (s, w) in enumerate(terms):
                        ins = mm(o, s[:, keys], w[:, cols], start=(t == 0), stop=(t == len(terms) - 1))
                ins.then_inc(vp_done, 1)

            def keys(p, c):
                w = keys_of(c)
                chunk = slice(c * CHUNK, c * CHUNK + w)
                cols = slice(p * P, (p + 1) * P)
                if place(p, c):
                    pe.wait_ge(khi, 2 * place(p, c))
                    pe.wait_ge(klo, 2 * place(p, c))
                terms = ((wk1h, c1h), (wk1h, c1l), (wk1l, c1h), (wkrh, cr), (wkrl, cr))
                for t, (s, m) in enumerate(terms):
                    ins = mm(PJ[:, 0:w], s[:, cols], m[:, chunk], start=(t == 0), stop=(t == len(terms) - 1))
                ins.then_inc(kp_done, 1)

            def look(p, c, k):
                h, qt = divmod(k, 2)
                i = looked(p, c, k)
                pe.wait_ge(khi, 2 * place(p, c) + h + 1)
                pe.wait_ge(klo, 2 * place(p, c) + h + 1)
                if i >= 2:
                    pe.wait_ge(pr_max, i - 1)
                if p and i == 4 * NCH * p:
                    pe.wait_ge(mb_ready, p)
                mm(PR[k % 2][:, 0:keys_of(c)], qh[:, 2 * p + h, qt * P:(qt + 1) * P],
                   key_cols(p, h, ALL, c * CHUNK, c * CHUNK + keys_of(c)), start=True, stop=True).then_inc(pr_done, 1)

            def spread_max(p):
                pe.wait_ge(dg_ready, 4 * (p + 1))
                mm(PR[0][:, :], onesr[:, :], diag[:, :], start=True, stop=True).then_inc(mb_done, 1)

            def fold(i):
                if i == 0:
                    pe.wait_ge(bd_ready, 4)
                    pe.wait_ge(wdt_in, 48)
                st_wait("fold", i)
                ps = st_bank("fold", i)
                if i < 4:
                    w, half = divmod(i, 2)
                    for k in range(4 * half, 4 * half + 4):
                        o = ps[64 * (k % 2):64 * (k % 2) + 64, (k // 2 % 2) * C:(k // 2 % 2 + 1) * C]
                        ins = mm(o, (bdq, bdk)[w][:, :, :].rearrange("p h d -> p (h d)"), wdt_s[:, w, k, :], start=True, stop=True)
                elif i == 4:
                    for k in range(8):
                        o = ps[32 * (k % 4):32 * (k % 4) + 32, (k // 4) * C:(k // 4 + 1) * C]
                        ins = mm(o, bdv[:, :, :].rearrange("p h d -> p (h d)"), wdt_s[:, 2, k, :], start=True, stop=True)
                else:
                    w, ct = divmod(i - 5, 2)
                    pe.wait_ge(fold_out, (2, 2, 4, 4, 5)[i - 5])
                    for b in range(4):
                        g, c = (b, ct) if i < 9 else (b % 2, b // 2)
                        ins = pe.transpose(ps[:, b * P:(b + 1) * P], wdt_s[:, w, g, c * P:(c + 1) * P], ident[:, :])
                ins.then_inc(fold_done, 1)

            pe.wait_ge(wlo, 2)
            for c in range(NCH):
                if c == NCH - 2:
                    last_context()
                pe.wait_ge(*((crlo_v, 1 + c // (NCH - 1)) if c in (0, NCH - 1) else (crlo, c)))
                if c < NCH - 1:
                    pe.wait_ge(c1lo, c + 1)
                else:
                    pe.wait_ge(c1lo8, 1)
                keys(0, c)
                if c == 0:
                    pe.wait_ge(wlo, 4)
                else:
                    if c == 1:
                        pe.wait_ge(qh_ready, 4)
                    look(0, c - 1, 0)
                values(0, 2 * c)
                if c >= 1:
                    look(0, c - 1, 1)
                if 2 * c + 1 < len(VG):
                    values(0, 2 * c + 1)
                if c >= 1:
                    look(0, c - 1, 2)
                    look(0, c - 1, 3)
            pe.wait_ge(gsel_ready, 6)
            for k in range(4):
                look(0, NCH - 1, k)
                fold(k)
            fold(4)
            spread_max(0)
            for i in range(5, 10):
                fold(i)
            pe.wait_ge(vp_out, len(VG))
            pe.wait_ge(fold_out, 10)

            def scores(n):
                p, jt = divmod(n, JT)
                r = rows_of(jt)
                st_wait("scores", n)
                if n in DIRECT:
                    pe.wait_ge(mb_ready, p + 1)
                    mm(st_bank("scores", n)[0:r, :], negr[:, 0:r], mb[:, p % 2, :], start=True, stop=False)
                for h in range(2):
                    o = st_bank("scores", n)[0:r, h * T:(h + 1) * T]
                    kt = key_cols(p, h, ALL, jt * P, jt * P + r)
                    mm(o, kt, qh[:, 2 * p + h, :], start=n not in DIRECT, stop=False)
                    ins = mm(o, kt, ql[:, 2 * p + h, :], start=False, stop=(n not in DIRECT or h == 1))
                ins.then_inc(st_done, 1)

            def attend(n):
                p, jt = divmod(n, JT)
                r = rows_of(jt)
                pe.wait_ge(e_ready, n + 1)
                if jt == 0 and p:
                    pe.wait_ge(pv_out, p)
                if p == 2:
                    pe.wait_ge(vp_out, len(VG) + jt // 2 + 1)
                e = ering[0:r, n % RING, :]
                for h in range(2):
                    d0 = (p % 2) * P + h * XD
                    ins = mm(PV[64 * h:64 * h + 64, 0:T], v[0:r, jt, d0:d0 + XD], e[:, h * T:(h + 1) * T],
                             start=(jt == 0), stop=(jt == JT - 1))
                ins.then_inc(pv_done, 1)
                if p == PAIRS - 1 and jt // 4 in PE_QUADS and (jt % 4 == 3 or jt == JT - 1):
                    if jt // 4 == PE_QUADS[0]:
                        pe.wait_ge(ot_ready, p)
                    for t in range(jt - jt % 4, jt + 1):
                        r, g = rows_of(t), t % 4
                        ins = mm(DEN[32 * g:32 * g + 32, :], ones[0:r, 0:32], ering[0:r, (p * JT + t) % RING, :],
                                 start=(t // 4 == PE_QUADS[0]), stop=(t + 4 >= JT))
                    ins.then_inc(quad_done, 1)

            def spread_den(p):
                pe.wait_ge(summed, summed_to(JT * (p + 1) - 1))
                if p:
                    pe.wait_ge(ot_ready, p)
                last = p == PAIRS - 1
                if last:
                    pe.wait_ge(den_out, 1)
                for h in range(2):
                    o, cols = DEN[64 * h:64 * h + 64, 0:T], slice(h * T, (h + 1) * T)
                    ins = mm(o, ones[:, 0:64], esum[:, p % 2, cols], start=True, stop=not last)
                    if last:
                        ins = mm(o, gsel[:, :], den[:, cols], start=False, stop=True)
                ins.then_inc(db_done, 1)

            for n in range(PAIRS * JT):
                p, j = divmod(n, JT)
                scores(n)
                if values_at(n) is not None:
                    values(1, values_at(n))
                if j == LAG + 1 and p:
                    spread_den(p - 1)
                if p + 1 < PAIRS:
                    if j in KEYS_AT:
                        keys(p + 1, KEYS_AT[j])
                if n >= LAG:
                    attend(n - LAG)
                if j == 0 and p:
                    spread_max(p)
                if p + 1 < PAIRS:
                    for c, k in LOOKS_AT.get(j, ()):
                        look(p + 1, c, k)
            for n in range(PAIRS * JT - LAG, PAIRS * JT):
                attend(n)
            spread_den(PAIRS - 1)

            pe.wait_ge(wout_in, 16)
            for tt in range(TT):
                for p in range(PAIRS):
                    pe.wait_ge(ot_ready, p + 1 if p + 1 < PAIRS else PAIRS + tt)
                    ins = mm((PJ, PV)[tt][:, 0:C], ot[:, p, tt * P:(tt + 1) * P], wout[:, p, :],
                             start=(p == 0), stop=(p == PAIRS - 1))
                ins.then_inc(xo_done, 1)

            transposed(1, xn)
            pe.wait_ge(xt_ready, CC + 1)
            pe.wait_ge(xt1_ready, 1)

            for i, (nm, g0) in enumerate((("k", 0), ("k", 2), ("q", 0), ("q", 2))):
                for g in (g0, g0 + 1):
                    for ct in range(CC):
                        ins = mm(bank[i][:, (g - g0) * T:(g - g0 + 1) * T], weff[nm][:, ct, g * P:(g + 1) * P], xnT[:, ct, :],
                                 start=(ct == 0), stop=(ct == CC - 1))
                ins.then_inc(qk_done, 1)
            for i in range(2):
                pe.wait_ge(qk_ready, i + 1)
                mm(bank[5 + i][:, :], tab[:, T:T + P], kb[:, 2 * i:2 * i + 2, :].rearrange("p g t -> p (g t)"),
                   start=True, stop=True).then_inc(kb_done, 1)
            for tt in range(TT):
                for ct in range(CC):
                    ins = mm(bank[4][:, tt * C:(tt + 1) * C], xnT[:, ct, tt * P:(tt + 1) * P], weff["v"][:, ct, 0:C],
                             start=(ct == 0), stop=(ct == CC - 1))
            ins.then_inc(v2_done, 1)
            pe.wait_ge(k2_ready, 2)
            pe.wait_ge(qk_ready, 4)
            pe.wait_ge(mask_ready, 3)
            for b in range(12):
                heads, w = heads_of(b)
                r, qt = b % 4, 0 if b < 4 else 1
                if b < 4:
                    pe.wait_ge(*((q2_ready, r // 2 + 1) if r % 2 == 0 else (q2m_ready, r // 2 + 1)))
                elif b < 8:
                    pe.wait_ge(v2_ready, 1)
                else:
                    pe.wait_ge(p2_ready, b - 8 + 1)
                o = bank[S2_BANK[b]]
                m = mask4[:, :, :] if b < 4 else mask2[:, :, :]
                mm(o[:, :], identr[:, :], m.rearrange("p a k -> p (a k)"), start=True, stop=False)
                for i, h in enumerate(heads):
                    ins = mm(o[:, i * w:(i + 1) * w], q2m[:, r, h // 4, qt * P:(qt + 1) * P], k2[:, h // 4, 0:w],
                             start=False, stop=(h == heads[-1]))
                ins.then_inc(s2_done, 1)

            def copied_out(b):
                by_act = sum(i <= b for i in TP_BY_ACT)
                if by_act:
                    pe.wait_ge(tpa, by_act)
                pe.wait_ge(tpd, b + 1 - by_act)

            def transpose_bank(b):
                pe.wait_ge(p2_ready, (b if b >= 4 else b + 4) + 1)
                if 4 <= b < 8:
                    pe.wait_ge(p2_ready, b + 4 + 1)
                if b >= 8:
                    copied_out(b - 8)
                for i in range(4):
                    ins = pe.transpose(bank[TP_BANK[b]][:, i * P:(i + 1) * P],
                                       s2[:, b // 4, (b % 4) * 512 + i * P:(b % 4) * 512 + (i + 1) * P], ident[:, :])
                ins.then_inc(tp_done, 1)

            def spread_reciprocals(half):
                pe.wait_ge(rdx_ready, (6, 8)[half])
                for g in (2 * half, 2 * half + 1):
                    for qt in range(TT):
                        ins = mm(bank[2 + half][:, (g % 2) * T + qt * P:(g % 2) * T + (qt + 1) * P],
                                 rdx[:, qt, g, :, :].rearrange("p r a -> p (r a)"), ident[:, :], start=True, stop=True)
                ins.then_inc(rt_done, 1)

            def outputs(half):
                ptf = pt[:, :, :].rearrange("p h k -> p (h k)")
                for g in (2 * half, 2 * half + 1):
                    for r in range(4):
                        h = 4 * g + r
                        vc = slice(AD * h, AD * h + 32)
                        o = bank[half][32 * r:32 * r + 32, :]
                        c0 = (g % 2) * T
                        b = {k: BLOCK_AT[(h, k)] for k in range(3)}
                        mm(o[:, c0:c0 + P], v2[:, 0, vc], ptf[:, b[0]:b[0] + P], start=True, stop=True)
                        mm(o[:, c0 + P:c0 + T], v2[:, 0, vc], ptf[:, b[1]:b[1] + P], start=True, stop=False)
                        ins = mm(o[:, c0 + P:c0 + T], v2[:, 1, vc], ptf[:, b[2]:b[2] + P], start=False, stop=True)
                ins.then_inc(y2_done, 1)

            for b in range(12):
                transpose_bank(b)
            pe.wait_ge(wc_zero, 2)
            copied_out(7)
            outputs(0)
            spread_reciprocals(0)
            spread_reciprocals(1)
            copied_out(11)
            outputs(1)
            pe.wait_ge(wc_in, 64)
            for tt in range(TT):
                for g in range(AG):
                    if g % 2 == 0:
                        pe.wait_ge(y2_ready, g // 2 + 1)
                    ins = mm(bank[6 + tt][:, 0:C], y2[:, g, tt * P:(tt + 1) * P], wc[:, g, :],
                             start=(g == 0), stop=(g == AG - 1))
                ins.then_inc(o2_done, 1)

            transposed(2, xn)

            def gate_up(e):
                for i in range(ICH):
                    n = e * ICH + i
                    if i in (0, 2, IFULL):
                        k = (0, 2, IFULL).index(i)
                        pe.wait_ge(guh, 3 * e + k + 1)
                        pe.wait_ge(gul, 3 * e + k + 1)
                    if n in (4, 5):
                        pe.wait_ge(xt_ready, CC + 1 + n - 3)
                    if n >= 6:
                        pe.wait_ge(hid_ready, n - 5)
                    for j in range(2 if i < IFULL else 1):
                        o = GU(n)[:, j * T:(j + 1) * T]
                        if i < IFULL:
                            parts = [[part[e % 2][:, 2 * ct + j, i * P:(i + 1) * P] for part in (gu_h, gu_l)]
                                     for ct in range(CC)]
                        else:
                            parts = [[part[e % 2][:, 2 * ct:2 * ct + 2, :].rearrange("p j n -> p (j n)")
                                      for part in (gt_h, gt_l)] for ct in range(CC)]
                        for ct in range(CC):
                            if n == 0 and j == 0:
                                pe.wait_ge(xh_ready, ct + 1)
                            mm(o, parts[ct][1], xh[:, ct, :], start=(ct == 0), stop=False)
                            mm(o, parts[ct][0], xh[:, ct, :], start=False, stop=False)
                        for ct in range(CC):
                            if n == 0 and j == 0:
                                pe.wait_ge(xl_ready, ct + 1)
                            ins = mm(o, parts[ct][0], xl[:, ct, :], start=False, stop=(ct == CC - 1))
                    ins.then_inc(gu_done, 1)

            def down(e):
                if e >= 2:
                    pe.wait_ge(acc_ready, TT * (e - 1))
                pe.wait_ge(wdh, e + 1)
                pe.wait_ge(wdl, e + 1)
                for tt in range(TT):
                    if e == E and tt:
                        pe.wait_ge(acc_ready, TT * E)
                    o = Y(e, tt)
                    q = slice(tt * P, (tt + 1) * P)
                    for i in range(ICH):
                        if tt == 0:
                            pe.wait_ge(hid_ready, e * ICH + i + 1)
                        hh, wh, wl = hid_h[e % 2][:, i, q], wd_h[e % 2][:, i, :], wd_l[e % 2][:, i, :]
                        mm(o, hh, wh, start=(i == 0), stop=False)
                        ins = mm(o, hh, wl, start=False, stop=(i == ICH - 1))
                        if i < IFULL:
                            mm(o, hid_l[e % 2][:, i, q], wh, start=False, stop=False)
                    ins.then_inc(yd_done, 1)

            gate_up(0)
            for tt in range(TT):
                for ct in range(CC):
                    ins = mm(bank[7][:, tt * E:(tt + 1) * E], xnT[:, ct, tt * P:(tt + 1) * P], gatew[:, ct, :],
                             start=(ct == 0), stop=(ct == CC - 1))
            ins.then_inc(lg_done, 1)
            for e in range(E + 1):
                if e < E:
                    gate_up(e + 1)
                if e == 1:
                    pe.wait_ge(ng_ready, 1)
                down(e)


S2_BANK = [b % 8 for b in range(12)]
TP_BY_ACT = (3, 5, 7, 9, 11)
TP_BANK = [4 + b for b in range(4)] + [b for b in range(4)] + [4 + b for b in range(4)]


def heads_of(b):
    gs, w = (((0, 1, 2, 3), P), ((0, 1), 2 * P), ((2, 3), 2 * P))[b // 4]
    return [4 * g + b % 4 for g in gs], w


def first_of(b):
    return (0, 16, 24)[b // 4] + (b % 4) * len(heads_of(b)[0])


BLOCK_AT = {}
for _b in range(12):
    for _i, _h in enumerate(heads_of(_b)[0]):
        for _kt in range(heads_of(_b)[1] // P):
            BLOCK_AT[(_h, 0 if _b < 4 else 1 + _kt)] = 512 * _b + _i * heads_of(_b)[1] + _kt * P


def kernel(**inputs):
    import concourse.bacc as bacc
    from concourse.bass_utils import run_bass_kernel_spmd

    g = {k: np.asarray(a) for k, a in inputs.items()}
    arrays = {
        "x": g["x"][0],
        "ctxT": g["ctx_768"][0].T,
        "promptT": g["L0_xattn_prompt"][0].T,
        "w_prompt": g["L0_xattn_w_prompt"], "w_img": g["L0_xattn_w_img"], "w_q": g["L0_xattn_w_q"],
        "w_k": g["L0_xattn_w_k"], "w_v": g["L0_xattn_w_v"], "w_out": g["L0_xattn_w_out"], "b_out": g["L0_xattn_b_out"],
        "wdT0": g["L0_attn_Wq_down"].T, "wdT1": g["L0_attn_Wk_down"].T, "wdT2": g["L0_attn_Wv_down"].T,
        "up0": g["L0_attn_Wq_up_c"], "up1": g["L0_attn_Wq_up_e"], "up2": g["L0_attn_Wk_up_c"],
        "up3": g["L0_attn_Wk_up_e"], "up4": g["L0_attn_Wv_up"], "w_c": g["L0_attn_Wc"],
        "gate_w": g["L0_ffn_gate_w"], "base_wgu": g["L0_ffn_base_wgu"], "base_wd": g["L0_ffn_base_wd"],
        "exp_wgu": g["L0_ffn_exp_wgu"], "exp_wd": g["L0_ffn_exp_wd"],
        "rope": rope_tables(),
    }
    arrays = {k: np.ascontiguousarray(a) for k, a in arrays.items()}
    nc = bacc.Bacc("TRN2", target_bir_lowering=False, num_devices=1)
    ap = {k: nc.dram_tensor(k, a.shape, F32, kind="ExternalInput").ap() for k, a in arrays.items()}
    out = nc.dram_tensor("out", (T, C), F32, kind="ExternalOutput").ap()
    perceiver(nc, ap["x"], ap["ctxT"], ap["promptT"], ap["w_prompt"], ap["w_img"], ap["w_q"], ap["w_k"], ap["w_v"],
              ap["w_out"], ap["b_out"], [ap[f"wdT{i}"] for i in range(3)], [ap[f"up{i}"] for i in range(5)],
              ap["w_c"], ap["gate_w"], ap["base_wgu"], ap["base_wd"], ap["exp_wgu"], ap["exp_wd"], ap["rope"], out)
    r = run_bass_kernel_spmd(nc, [arrays], core_ids=[0])
    return r.results[0]["out"].reshape(1, T, C)
```
